# Optimizing a Trainium2 kernel written in Bass

```python
import numpy as np
import jax
import jax.numpy as jnp

def _softmax(x, axis=-1):
    return jax.nn.softmax(x, axis=axis)

def _gelu(x):
    return jax.nn.gelu(x, approximate=True)

def _silu(x):
    return jax.nn.silu(x)

def _sigmoid(x):
    return jax.nn.sigmoid(x)

def _layernorm(x, axis=-1, eps=1e-05):
    m = jnp.mean(x, axis=axis, keepdims=True)
    v = jnp.var(x, axis=axis, keepdims=True)
    return (x - m) / jnp.sqrt(v + eps)

def _scatter_add(tgt, idx, src, axis=0):
    return tgt.at[idx].add(src)

def _segment_sum(src, seg, n):
    return jax.ops.segment_sum(src, seg, n)
kernel_name = 'mk_macaron_d4_jaxref_r8_561155'

def setup_inputs(seed: int=0):
    np.random.seed(seed)
    _w = jnp.asarray

    def _L0_attn_setup():
        import jax, jax.numpy as jnp
        import numpy as np
        B, T, D = (8, 96, 128)
        H = 16
        DH = D // H
        ROPE_BASE = 10000.0

        def _rope_tables(length, dim, dtype):
            inv_freq = 1.0 / ROPE_BASE ** (jnp.arange(0, dim, 2, dtype=jnp.float32) / dim)
            ang = jnp.arange(length, dtype=jnp.float32)[:, None] * inv_freq[None, :]
            cos = jnp.concatenate([jnp.cos(ang), jnp.cos(ang)], axis=-1).astype(dtype)
            sin = jnp.concatenate([jnp.sin(ang), jnp.sin(ang)], axis=-1).astype(dtype)
            return (cos, sin)

        def _rotate_half(x):
            half = x.shape[-1] // 2
            return jnp.concatenate([-x[..., half:], x[..., :half]], axis=-1)

        def _apply_rope(x, cos, sin):
            return x * cos[None, None] + _rotate_half(x) * sin[None, None]
        key = jax.random.key(seed)
        kx, kw, kb = jax.random.split(key, 3)
        x = jax.random.normal(kx, (B, T, D), dtype=jnp.float32)
        bound = 1.0 / np.sqrt(D)
        W_qkv = jax.random.uniform(kw, (3 * D, D), dtype=jnp.float32, minval=-bound, maxval=bound)
        b_qkv = jax.random.uniform(kb, (3 * D,), dtype=jnp.float32, minval=-bound, maxval=bound)
        return {'x': x, 'W_qkv': W_qkv, 'b_qkv': b_qkv}
    _L0_attn_in = _L0_attn_setup()

    def _L0_ffn_setup():
        import jax, jax.numpy as jnp
        import numpy as np
        HIDDEN_SIZE = 128
        NUM_EXPERTS = 8
        MOE_INTERMEDIATE_SIZE = 176
        NUM_EXPERTS_PER_TOK = 2
        SHARED_EXPERT_INTERMEDIATE_SIZE = 352
        B, T = (2, 128)
        W_SCALE = 0.02
        key = jax.random.key(seed)
        ks = jax.random.split(key, 8)
        H, E, I, SI = (HIDDEN_SIZE, NUM_EXPERTS, MOE_INTERMEDIATE_SIZE, SHARED_EXPERT_INTERMEDIATE_SIZE)
        return {'x': jax.random.normal(ks[0], (B, T, H), jnp.float32), 'gate_w': jax.random.normal(ks[1], (E, H), jnp.float32) * W_SCALE, 'experts_gate_up': jax.random.normal(ks[2], (E, 2 * I, H), jnp.float32) * W_SCALE, 'experts_down': jax.random.normal(ks[3], (E, H, I), jnp.float32) * W_SCALE, 'shared_gate_w': jax.random.normal(ks[4], (SI, H), jnp.float32) * W_SCALE, 'shared_up_w': jax.random.normal(ks[5], (SI, H), jnp.float32) * W_SCALE, 'shared_down_w': jax.random.normal(ks[6], (H, SI), jnp.float32) * W_SCALE, 'shared_expert_gate_w': jax.random.normal(ks[7], (1, H), jnp.float32) * W_SCALE}
    _L0_ffn_in = _L0_ffn_setup()

    def _L1_attn_setup():
        import jax, jax.numpy as jnp
        import numpy as np
        D_MODEL = 128
        NUM_HEADS = 16
        D_K = 128
        D_V = 128
        D_IN = 128
        THETA = 10000.0
        B, S = (2, 256)

        def _rope(t, theta):
            hd = t.shape[-1]
            inv_freq = 1.0 / theta ** (jnp.arange(0, hd, 2, dtype=jnp.float32) / hd)
            pos = jnp.arange(t.shape[-2], dtype=jnp.float32)
            ang = pos[:, None] * inv_freq[None, :]
            cos, sin = (jnp.cos(ang), jnp.sin(ang))
            tp = t.reshape(t.shape[:-1] + (hd // 2, 2))
            t0, t1 = (tp[..., 0], tp[..., 1])
            out = jnp.stack([t0 * cos - t1 * sin, t0 * sin + t1 * cos], axis=-1)
            return out.reshape(t.shape)
        key = jax.random.key(seed)
        k1, k2, k3, k4, k5 = jax.random.split(key, 5)
        std_qkv = (2.0 / (D_IN + D_K)) ** 0.5
        std_o = (2.0 / (D_V + D_MODEL)) ** 0.5
        x = jax.random.normal(k1, (B, S, D_IN), jnp.float32)
        wq = jax.random.normal(k2, (D_IN, D_K), jnp.float32) * std_qkv
        wk = jax.random.normal(k3, (D_IN, D_K), jnp.float32) * std_qkv
        wv = jax.random.normal(k4, (D_IN, D_V), jnp.float32) * std_qkv
        wo = jax.random.normal(k5, (D_V, D_MODEL), jnp.float32) * std_o
        return {'x': x, 'wq': wq, 'wk': wk, 'wv': wv, 'wo': wo}
    _L1_attn_in = _L1_attn_setup()

    def _L1_ffn_setup():
        import jax, jax.numpy as jnp
        import numpy as np
        H = 32
        MB = 2
        TOP_K = 2
        key = jax.random.key(seed)
        ks = jax.random.split(key, 8)
        B, S, D, E = (8, 128, 128, 8)
        Fd = 4 * D

        def w(k, shape, fan):
            return jax.random.normal(k, shape, jnp.float32) / np.float32(np.sqrt(fan))
        return dict(x=jax.random.normal(ks[0], (B, S, D), jnp.float32), ln_g=jnp.ones((D,), jnp.float32), ln_b=jnp.zeros((D,), jnp.float32), wq=w(ks[1], (D, D), D), wk=w(ks[2], (D, D), D), wv=w(ks[3], (D, D), D), wo=w(ks[4], (D, D), D), gate_w=w(ks[5], (E, D), D), w1=w(ks[6], (E, D, Fd), D), b1=jnp.zeros((E, Fd), jnp.float32), w2=w(ks[7], (E, Fd, D), Fd), b2=jnp.zeros((E, D), jnp.float32))
    _L1_ffn_in = _L1_ffn_setup()

    def _L2_attn_setup():
        import math
        import jax, jax.numpy as jnp
        import numpy as np
        DIM = 128
        N_HEADS = 16
        HEAD_DIM = DIM // N_HEADS
        MAX_SEQ_LEN = 512
        ROPE_BASE = 10000.0

        def _rope_tables(seq_len):
            inv_freq = 1.0 / ROPE_BASE ** (jnp.arange(0, HEAD_DIM, 2, dtype=jnp.float32) / HEAD_DIM)
            t = jnp.arange(seq_len, dtype=jnp.float32)
            freqs = jnp.outer(t, inv_freq)
            return (jnp.cos(freqs), jnp.sin(freqs))

        def _rotate_half(x):
            x1 = x[..., 0::2]
            x2 = x[..., 1::2]
            return jnp.stack([-x2, x1], axis=-1).reshape(x.shape)

        def _apply_rope(xq, xk, cos, sin):
            cos = jnp.repeat(cos, 2, axis=-1)[None, None]
            sin = jnp.repeat(sin, 2, axis=-1)[None, None]
            xq_out = xq * cos + _rotate_half(xq) * sin
            xk_out = xk * cos + _rotate_half(xk) * sin
            return (xq_out, xk_out)
        key = jax.random.key(seed)
        kx, kq, kk, kv, ko = jax.random.split(key, 5)
        B, S = (1, 512)
        x = jax.random.normal(kx, (B, S, DIM), dtype=jnp.float32)
        scale = 0.02
        Wq = jax.random.normal(kq, (DIM, DIM), dtype=jnp.float32) * scale
        Wk = jax.random.normal(kk, (DIM, DIM), dtype=jnp.float32) * scale
        Wv = jax.random.normal(kv, (DIM, DIM), dtype=jnp.float32) * scale
        Wo = jax.random.normal(ko, (DIM, DIM), dtype=jnp.float32) * scale
        return {'x': x, 'Wq': Wq, 'Wk': Wk, 'Wv': Wv, 'Wo': Wo}
    _L2_attn_in = _L2_attn_setup()

    def _L2_ffn_setup():
        import jax, jax.numpy as jnp
        import numpy as np
        EPS = 1e-06
        LN_EPS = 1e-05

        def _absmean_core(W):
            gamma = jnp.mean(jnp.abs(W)) + EPS
            Ws = W / gamma
            Wq = jnp.sign(Ws) * jnp.minimum(jnp.round(jnp.abs(Ws)), 1.0)
            return (Wq, gamma)

        @jax.custom_vjp
        def absmean(W):
            return _absmean_core(W)[0]

        def _absmean_fwd(W):
            Wq, gamma = _absmean_core(W)
            return (Wq, gamma)

        def _absmean_bwd(gamma, g):
            return (g / gamma,)
        absmean.defvjp(_absmean_fwd, _absmean_bwd)

        def layernorm(x, w, b, eps=LN_EPS):
            mu = jnp.mean(x, axis=-1, keepdims=True)
            var = jnp.mean((x - mu) ** 2, axis=-1, keepdims=True)
            return (x - mu) * jax.lax.rsqrt(var + eps) * w + b
        key = jax.random.key(seed)
        k1, k2, k3 = jax.random.split(key, 3)
        d, h = (128, 512)
        B, T = (8, 256)
        return {'x': jax.random.normal(k1, (B, T, d), jnp.float32), 'W_fc': jax.random.normal(k2, (h, d), jnp.float32), 'ln_w': jnp.ones((h,), jnp.float32), 'ln_b': jnp.zeros((h,), jnp.float32), 'W_proj': jax.random.normal(k3, (d, h), jnp.float32)}
    _L2_ffn_in = _L2_ffn_setup()

    def _L3_attn_setup():
        import jax, jax.numpy as jnp
        import numpy as np
        B, T, D, H, FFN = (2, 256, 128, 16, 512)
        K = D // H
        EPS = 1e-06
        LN_EPS = 1e-05
        LAM_MIN = 1e-08

        def _ln(x, w, b):
            m = x.mean(-1, keepdims=True)
            v = ((x - m) ** 2).mean(-1, keepdims=True)
            return (x - m) * jax.lax.rsqrt(v + LN_EPS) * w + b

        def _lion(phi_q, phi_k, v, lam):
            b, h, t, kk = phi_q.shape
            kv = v.shape[-1]
            to_t = lambda a: a.transpose(2, 0, 1, 3)
            qt, kt, vt, lt = (to_t(phi_q), to_t(phi_k), to_t(v), to_t(lam))
            S0 = jnp.zeros((b, h, kk, kv), phi_q.dtype)

            def fwd(S, inp):
                q_t, k_t, v_t, l_t = inp
                S = S * l_t[..., None] + k_t[..., None] * v_t[..., None, :]
                return (S, jnp.einsum('bhk,bhkv->bhv', q_t, S))
            _, out_f = jax.lax.scan(fwd, S0, (qt, kt, vt, lt))
            q_shift = jnp.concatenate([qt[:1], qt[:-1]], axis=0)

            def bwd(R, inp):
                qs_t, k_t, v_t, l_t = inp
                R = l_t[..., None] * (k_t[..., None] * v_t[..., None, :] + R)
                return (R, jnp.einsum('bhk,bhkv->bhv', qs_t, R))
            _, out_b = jax.lax.scan(bwd, S0, (q_shift, kt, vt, lt), reverse=True)
            out_b = jnp.concatenate([out_b[1:], jnp.zeros_like(out_b[:1])], axis=0)
            return (out_f + out_b).transpose(1, 2, 0, 3)
        key = jax.random.key(seed)
        ks = jax.random.split(key, 12)
        s = 0.02
        w = lambda k, shp: jax.random.normal(k, shp, jnp.float32) * s
        return {'x': jax.random.normal(ks[0], (B, T, D), jnp.float32), 'q_w': w(ks[1], (D, D)), 'q_b': jnp.zeros((D,), jnp.float32), 'k_w': w(ks[2], (D, D)), 'k_b': jnp.zeros((D,), jnp.float32), 'v_w': w(ks[3], (D, D)), 'v_b': jnp.zeros((D,), jnp.float32), 'o_w': w(ks[4], (D, D)), 'o_b': jnp.zeros((D,), jnp.float32), 'ln1_w': jnp.ones((D,), jnp.float32), 'ln1_b': jnp.zeros((D,), jnp.float32), 'ln2_w': jnp.ones((D,), jnp.float32), 'ln2_b': jnp.zeros((D,), jnp.float32), 'dec_w': w(ks[5], (D, H)), 'dec_b': jnp.full((H,), 5.0, jnp.float32), 'f1_w': w(ks[6], (D, FFN)), 'f1_b': jnp.zeros((FFN,), jnp.float32), 'f2_w': w(ks[7], (FFN, D)), 'f2_b': jnp.zeros((D,), jnp.float32)}
    _L3_attn_in = _L3_attn_setup()

    def _L3_ffn_setup():
        import jax, jax.numpy as jnp
        import numpy as np

        def _binarize(w):
            alpha = jax.lax.stop_gradient(jnp.mean(jnp.abs(w), axis=1, keepdims=True))
            bw = alpha * jnp.sign(w)
            return w + jax.lax.stop_gradient(bw - w)
        key = jax.random.key(seed)
        k1, k2, k3, k4, k5 = jax.random.split(key, 5)
        D, H = (128, 512)
        x = jax.random.normal(k1, (64, 196, D), dtype=jnp.float32)
        w1 = jax.random.normal(k2, (H, D), dtype=jnp.float32) * 0.02
        b1 = jax.random.normal(k3, (H,), dtype=jnp.float32) * 0.02
        w2 = jax.random.normal(k4, (D, H), dtype=jnp.float32) * 0.02
        b2 = jax.random.normal(k5, (D,), dtype=jnp.float32) * 0.02
        return {'x': x, 'w1': w1, 'b1': b1, 'w2': w2, 'b2': b2}
    _L3_ffn_in = _L3_ffn_setup()
    _d = {'L0_attn_x': _L0_attn_in['x'], 'L0_attn_W_qkv': _L0_attn_in['W_qkv'], 'L0_attn_b_qkv': _L0_attn_in['b_qkv'], 'L0_ffn_gate_w': _L0_ffn_in['gate_w'], 'L0_ffn_experts_gate_up': _L0_ffn_in['experts_gate_up'], 'L0_ffn_experts_down': _L0_ffn_in['experts_down'], 'L0_ffn_shared_gate_w': _L0_ffn_in['shared_gate_w'], 'L0_ffn_shared_up_w': _L0_ffn_in['shared_up_w'], 'L0_ffn_shared_down_w': _L0_ffn_in['shared_down_w'], 'L0_ffn_shared_expert_gate_w': _L0_ffn_in['shared_expert_gate_w'], 'L1_attn_wq': _L1_attn_in['wq'], 'L1_attn_wk': _L1_attn_in['wk'], 'L1_attn_wv': _L1_attn_in['wv'], 'L1_attn_wo': _L1_attn_in['wo'], 'L1_ffn_ln_g': _L1_ffn_in['ln_g'], 'L1_ffn_ln_b': _L1_ffn_in['ln_b'], 'L1_ffn_wq': _L1_ffn_in['wq'], 'L1_ffn_wk': _L1_ffn_in['wk'], 'L1_ffn_wv': _L1_ffn_in['wv'], 'L1_ffn_wo': _L1_ffn_in['wo'], 'L1_ffn_gate_w': _L1_ffn_in['gate_w'], 'L1_ffn_w1': _L1_ffn_in['w1'], 'L1_ffn_b1': _L1_ffn_in['b1'], 'L1_ffn_w2': _L1_ffn_in['w2'], 'L1_ffn_b2': _L1_ffn_in['b2'], 'L2_attn_Wq': _L2_attn_in['Wq'], 'L2_attn_Wk': _L2_attn_in['Wk'], 'L2_attn_Wv': _L2_attn_in['Wv'], 'L2_attn_Wo': _L2_attn_in['Wo'], 'L2_ffn_W_fc': _L2_ffn_in['W_fc'], 'L2_ffn_ln_w': _L2_ffn_in['ln_w'], 'L2_ffn_ln_b': _L2_ffn_in['ln_b'], 'L2_ffn_W_proj': _L2_ffn_in['W_proj'], 'L3_attn_q_w': _L3_attn_in['q_w'], 'L3_attn_q_b': _L3_attn_in['q_b'], 'L3_attn_k_w': _L3_attn_in['k_w'], 'L3_attn_k_b': _L3_attn_in['k_b'], 'L3_attn_v_w': _L3_attn_in['v_w'], 'L3_attn_v_b': _L3_attn_in['v_b'], 'L3_attn_o_w': _L3_attn_in['o_w'], 'L3_attn_o_b': _L3_attn_in['o_b'], 'L3_attn_ln1_w': _L3_attn_in['ln1_w'], 'L3_attn_ln1_b': _L3_attn_in['ln1_b'], 'L3_attn_ln2_w': _L3_attn_in['ln2_w'], 'L3_attn_ln2_b': _L3_attn_in['ln2_b'], 'L3_attn_dec_w': _L3_attn_in['dec_w'], 'L3_attn_dec_b': _L3_attn_in['dec_b'], 'L3_attn_f1_w': _L3_attn_in['f1_w'], 'L3_attn_f1_b': _L3_attn_in['f1_b'], 'L3_attn_f2_w': _L3_attn_in['f2_w'], 'L3_attn_f2_b': _L3_attn_in['f2_b'], 'L3_ffn_w1': _L3_ffn_in['w1'], 'L3_ffn_b1': _L3_ffn_in['b1'], 'L3_ffn_w2': _L3_ffn_in['w2'], 'L3_ffn_b2': _L3_ffn_in['b2']}
    _x0 = _d['L0_attn_x']
    _d['L0_attn_x'] = jax.random.normal(jax.random.fold_in(jax.random.key(seed), 1), (2, 1024, 128), dtype=_x0.dtype)
    del _x0
    return _d

def reference(L0_attn_x, L0_attn_W_qkv, L0_attn_b_qkv, L0_ffn_gate_w, L0_ffn_experts_gate_up, L0_ffn_experts_down, L0_ffn_shared_gate_w, L0_ffn_shared_up_w, L0_ffn_shared_down_w, L0_ffn_shared_expert_gate_w, L1_attn_wq, L1_attn_wk, L1_attn_wv, L1_attn_wo, L1_ffn_ln_g, L1_ffn_ln_b, L1_ffn_wq, L1_ffn_wk, L1_ffn_wv, L1_ffn_wo, L1_ffn_gate_w, L1_ffn_w1, L1_ffn_b1, L1_ffn_w2, L1_ffn_b2, L2_attn_Wq, L2_attn_Wk, L2_attn_Wv, L2_attn_Wo, L2_ffn_W_fc, L2_ffn_ln_w, L2_ffn_ln_b, L2_ffn_W_proj, L3_attn_q_w, L3_attn_q_b, L3_attn_k_w, L3_attn_k_b, L3_attn_v_w, L3_attn_v_b, L3_attn_o_w, L3_attn_o_b, L3_attn_ln1_w, L3_attn_ln1_b, L3_attn_ln2_w, L3_attn_ln2_b, L3_attn_dec_w, L3_attn_dec_b, L3_attn_f1_w, L3_attn_f1_b, L3_attn_f2_w, L3_attn_f2_b, L3_ffn_w1, L3_ffn_b1, L3_ffn_w2, L3_ffn_b2):

    def _L0_attn_ref(x, W_qkv, b_qkv):
        import jax, jax.numpy as jnp
        import numpy as np
        B, T, D = (8, 96, 128)
        H = 16
        DH = D // H
        ROPE_BASE = 10000.0

        def _rope_tables(length, dim, dtype):
            inv_freq = 1.0 / ROPE_BASE ** (jnp.arange(0, dim, 2, dtype=jnp.float32) / dim)
            ang = jnp.arange(length, dtype=jnp.float32)[:, None] * inv_freq[None, :]
            cos = jnp.concatenate([jnp.cos(ang), jnp.cos(ang)], axis=-1).astype(dtype)
            sin = jnp.concatenate([jnp.sin(ang), jnp.sin(ang)], axis=-1).astype(dtype)
            return (cos, sin)

        def _rotate_half(x):
            half = x.shape[-1] // 2
            return jnp.concatenate([-x[..., half:], x[..., :half]], axis=-1)

        def _apply_rope(x, cos, sin):
            return x * cos[None, None] + _rotate_half(x) * sin[None, None]
        batch, length, dim = x.shape
        qkv = x @ W_qkv.T + b_qkv
        q, k, v = jnp.split(qkv, 3, axis=-1)

        def to_heads(t):
            return t.reshape(batch, length, H, DH).transpose(0, 2, 1, 3)
        q, k, v = (to_heads(q), to_heads(k), to_heads(v))
        cos, sin = _rope_tables(length, DH, x.dtype)
        q = _apply_rope(q, cos, sin)
        k = _apply_rope(k, cos, sin)
        scores = jnp.einsum('bhtd,bhsd->bhts', q, k)
        mask = jnp.tril(jnp.ones((length, length), dtype=x.dtype))
        retention = scores * mask[None, None]
        out = jnp.einsum('bhts,bhsd->bhtd', retention, v)
        return out.transpose(0, 2, 1, 3).reshape(batch, length, dim)

    def _L0_ffn_ref(x, gate_w, experts_gate_up, experts_down, shared_gate_w, shared_up_w, shared_down_w, shared_expert_gate_w):
        import jax, jax.numpy as jnp
        import numpy as np
        HIDDEN_SIZE = 128
        NUM_EXPERTS = 8
        MOE_INTERMEDIATE_SIZE = 176
        NUM_EXPERTS_PER_TOK = 2
        SHARED_EXPERT_INTERMEDIATE_SIZE = 352
        B, T = (2, 128)
        W_SCALE = 0.02
        Bx, Tx, H = x.shape
        E = gate_w.shape[0]
        I = experts_down.shape[2]
        x_flat = x.reshape(Bx * Tx, H)
        logits = x_flat @ gate_w.T
        scores = jax.nn.softmax(logits, axis=-1)
        _, topk_ids = jax.lax.top_k(scores, NUM_EXPERTS_PER_TOK)
        in_topk = jax.nn.one_hot(topk_ids, E, dtype=x.dtype).sum(axis=1)
        w = scores * in_topk
        gu = jnp.einsum('nh,eih->nei', x_flat, experts_gate_up)
        g, u = (gu[..., :I], gu[..., I:])
        h = jax.nn.silu(g) * u
        expert_out = jnp.einsum('nei,ehi->neh', h, experts_down)
        out = jnp.einsum('neh,ne->nh', expert_out, w)
        shared = jax.nn.silu(x_flat @ shared_gate_w.T) * (x_flat @ shared_up_w.T) @ shared_down_w.T
        shared_weight = jax.nn.sigmoid(x_flat @ shared_expert_gate_w.T)
        out = out + shared_weight * shared
        return out.reshape(Bx, Tx, H)

    def _L1_attn_ref(x, wq, wk, wv, wo):
        import jax, jax.numpy as jnp
        import numpy as np
        D_MODEL = 128
        NUM_HEADS = 16
        D_K = 128
        D_V = 128
        D_IN = 128
        THETA = 10000.0
        B, S = (2, 256)

        def _rope(t, theta):
            hd = t.shape[-1]
            inv_freq = 1.0 / theta ** (jnp.arange(0, hd, 2, dtype=jnp.float32) / hd)
            pos = jnp.arange(t.shape[-2], dtype=jnp.float32)
            ang = pos[:, None] * inv_freq[None, :]
            cos, sin = (jnp.cos(ang), jnp.sin(ang))
            tp = t.reshape(t.shape[:-1] + (hd // 2, 2))
            t0, t1 = (tp[..., 0], tp[..., 1])
            out = jnp.stack([t0 * cos - t1 * sin, t0 * sin + t1 * cos], axis=-1)
            return out.reshape(t.shape)
        b, s, _ = x.shape
        hd = D_K // NUM_HEADS
        hdv = D_V // NUM_HEADS
        q = jnp.einsum('bsd,de->bse', x, wq).reshape(b, s, NUM_HEADS, hd).transpose(2, 0, 1, 3)
        k = jnp.einsum('bsd,de->bse', x, wk).reshape(b, s, NUM_HEADS, hd).transpose(2, 0, 1, 3)
        v = jnp.einsum('bsd,de->bse', x, wv).reshape(b, s, NUM_HEADS, hdv).transpose(2, 0, 1, 3)
        q = _rope(q, THETA)
        k = _rope(k, THETA)
        scale = 1.0 / jnp.sqrt(jnp.asarray(hd, jnp.float32))
        scores = jnp.einsum('hbqd,hbkd->hbqk', q, k) * scale
        causal = jnp.tril(jnp.ones((s, s), dtype=bool))
        scores = jnp.where(causal, scores, -jnp.inf)
        attn = jax.nn.softmax(scores, axis=-1)
        o = jnp.einsum('hbqk,hbkd->hbqd', attn, v)
        o = o.transpose(1, 2, 0, 3).reshape(b, s, D_V)
        return jnp.einsum('bsd,de->bse', o, wo)

    def _L1_ffn_ref(x, ln_g, ln_b, wq, wk, wv, wo, gate_w, w1, b1, w2, b2):
        import jax, jax.numpy as jnp
        import numpy as np
        H = 32
        MB = 2
        TOP_K = 2
        B, S, D = x.shape
        E = w1.shape[0]
        hd = D // H
        mu = jnp.mean(x, axis=-1, keepdims=True)
        var = jnp.var(x, axis=-1, keepdims=True)
        xn = (x - mu) / jnp.sqrt(var + 1e-05) * ln_g + ln_b
        q = (xn @ wq).reshape(B, S, H, hd)
        k = (xn @ wk).reshape(B, S, H, hd)
        v = (xn @ wv).reshape(B, S, H, hd)
        att = jnp.einsum('bqhd,bkhd->bhqk', q, k) / np.float32(np.sqrt(hd))
        p = jax.nn.softmax(att, axis=-1)
        o = jnp.einsum('bhqk,bkhd->bqhd', p, v).reshape(B, S, D) @ wo + x
        xf = o.reshape(-1, D)
        logits = xf @ gate_w.T
        _ = jax.lax.top_k(logits, TOP_K)
        tpe = xf.shape[0] // (MB * E)
        xe = xf.reshape(MB, E, tpe, D)
        h = jax.nn.gelu(jnp.einsum('metd,edf->metf', xe, w1) + b1[None, :, None, :], approximate=False)
        y = jnp.einsum('metf,efd->metd', h, w2) + b2[None, :, None, :]
        return y.reshape(B, S, D)

    def _L2_attn_ref(x, Wq, Wk, Wv, Wo):
        import math
        import jax, jax.numpy as jnp
        import numpy as np
        DIM = 128
        N_HEADS = 16
        HEAD_DIM = DIM // N_HEADS
        MAX_SEQ_LEN = 512
        ROPE_BASE = 10000.0

        def _rope_tables(seq_len):
            inv_freq = 1.0 / ROPE_BASE ** (jnp.arange(0, HEAD_DIM, 2, dtype=jnp.float32) / HEAD_DIM)
            t = jnp.arange(seq_len, dtype=jnp.float32)
            freqs = jnp.outer(t, inv_freq)
            return (jnp.cos(freqs), jnp.sin(freqs))

        def _rotate_half(x):
            x1 = x[..., 0::2]
            x2 = x[..., 1::2]
            return jnp.stack([-x2, x1], axis=-1).reshape(x.shape)

        def _apply_rope(xq, xk, cos, sin):
            cos = jnp.repeat(cos, 2, axis=-1)[None, None]
            sin = jnp.repeat(sin, 2, axis=-1)[None, None]
            xq_out = xq * cos + _rotate_half(xq) * sin
            xk_out = xk * cos + _rotate_half(xk) * sin
            return (xq_out, xk_out)
        B, S, _ = x.shape
        q = (x @ Wq.T).reshape(B, S, N_HEADS, HEAD_DIM).transpose(0, 2, 1, 3)
        k = (x @ Wk.T).reshape(B, S, N_HEADS, HEAD_DIM).transpose(0, 2, 1, 3)
        v = (x @ Wv.T).reshape(B, S, N_HEADS, HEAD_DIM).transpose(0, 2, 1, 3)
        cos, sin = _rope_tables(S)
        q, k = _apply_rope(q, k, cos, sin)
        scores = jnp.einsum('bhqd,bhkd->bhqk', q, k) / math.sqrt(HEAD_DIM)
        mask = jnp.triu(jnp.full((S, S), -jnp.inf, dtype=scores.dtype), k=1)
        scores = scores + mask[None, None]
        probs = jax.nn.softmax(scores, axis=-1)
        out = jnp.einsum('bhqk,bhkd->bhqd', probs, v)
        out = out.transpose(0, 2, 1, 3).reshape(B, S, DIM)
        return out @ Wo.T

    def _L2_ffn_ref(x, W_fc, ln_w, ln_b, W_proj):
        import jax, jax.numpy as jnp
        import numpy as np
        EPS = 1e-06
        LN_EPS = 1e-05

        def _absmean_core(W):
            gamma = jnp.mean(jnp.abs(W)) + EPS
            Ws = W / gamma
            Wq = jnp.sign(Ws) * jnp.minimum(jnp.round(jnp.abs(Ws)), 1.0)
            return (Wq, gamma)

        @jax.custom_vjp
        def absmean(W):
            return _absmean_core(W)[0]

        def _absmean_fwd(W):
            Wq, gamma = _absmean_core(W)
            return (Wq, gamma)

        def _absmean_bwd(gamma, g):
            return (g / gamma,)
        absmean.defvjp(_absmean_fwd, _absmean_bwd)

        def layernorm(x, w, b, eps=LN_EPS):
            mu = jnp.mean(x, axis=-1, keepdims=True)
            var = jnp.mean((x - mu) ** 2, axis=-1, keepdims=True)
            return (x - mu) * jax.lax.rsqrt(var + eps) * w + b
        h = jnp.einsum('btd,hd->bth', x, absmean(W_fc))
        h = jax.nn.gelu(h, approximate=False)
        h = layernorm(h, ln_w, ln_b)
        return jnp.einsum('bth,dh->btd', h, absmean(W_proj))

    def _L3_attn_ref(x, q_w, q_b, k_w, k_b, v_w, v_b, o_w, o_b, ln1_w, ln1_b, ln2_w, ln2_b, dec_w, dec_b, f1_w, f1_b, f2_w, f2_b):
        import jax, jax.numpy as jnp
        import numpy as np
        B, T, D, H, FFN = (2, 256, 128, 16, 512)
        K = D // H
        EPS = 1e-06
        LN_EPS = 1e-05
        LAM_MIN = 1e-08

        def _ln(x, w, b):
            m = x.mean(-1, keepdims=True)
            v = ((x - m) ** 2).mean(-1, keepdims=True)
            return (x - m) * jax.lax.rsqrt(v + LN_EPS) * w + b

        def _lion(phi_q, phi_k, v, lam):
            b, h, t, kk = phi_q.shape
            kv = v.shape[-1]
            to_t = lambda a: a.transpose(2, 0, 1, 3)
            qt, kt, vt, lt = (to_t(phi_q), to_t(phi_k), to_t(v), to_t(lam))
            S0 = jnp.zeros((b, h, kk, kv), phi_q.dtype)

            def fwd(S, inp):
                q_t, k_t, v_t, l_t = inp
                S = S * l_t[..., None] + k_t[..., None] * v_t[..., None, :]
                return (S, jnp.einsum('bhk,bhkv->bhv', q_t, S))
            _, out_f = jax.lax.scan(fwd, S0, (qt, kt, vt, lt))
            q_shift = jnp.concatenate([qt[:1], qt[:-1]], axis=0)

            def bwd(R, inp):
                qs_t, k_t, v_t, l_t = inp
                R = l_t[..., None] * (k_t[..., None] * v_t[..., None, :] + R)
                return (R, jnp.einsum('bhk,bhkv->bhv', qs_t, R))
            _, out_b = jax.lax.scan(bwd, S0, (q_shift, kt, vt, lt), reverse=True)
            out_b = jnp.concatenate([out_b[1:], jnp.zeros_like(out_b[:1])], axis=0)
            return (out_f + out_b).transpose(1, 2, 0, 3)
        bb, tt, dd = x.shape
        residual = x
        x_n = _ln(x, ln1_w, ln1_b)
        split = lambda y: y.reshape(bb, tt, H, K).transpose(0, 2, 1, 3)
        q = split(x_n @ q_w + q_b)
        k = split(x_n @ k_w + k_b)
        v = split(x_n @ v_w + v_b)
        phi_q = jax.nn.elu(q) + 1.0
        phi_k = jax.nn.elu(k) + 1.0
        lam = jax.nn.sigmoid(x_n @ dec_w + dec_b)
        lam = jnp.maximum(lam, LAM_MIN).transpose(0, 2, 1)
        lam = jnp.broadcast_to(lam[..., None], (bb, H, tt, K))
        v_ext = jnp.concatenate([v, jnp.ones((bb, H, tt, 1), v.dtype)], axis=-1)
        out = _lion(phi_q, phi_k, v_ext, lam)
        num, den = (out[..., :K], jnp.maximum(out[..., K:], EPS))
        attn = (num / den).transpose(0, 2, 1, 3).reshape(bb, tt, dd)
        x = residual + (attn @ o_w + o_b)
        x2 = _ln(x, ln2_w, ln2_b)
        h = jax.nn.gelu(x2 @ f1_w + f1_b, approximate=False)
        return x + (h @ f2_w + f2_b)

    def _L3_ffn_ref(x, w1, b1, w2, b2):
        import jax, jax.numpy as jnp
        import numpy as np

        def _binarize(w):
            alpha = jax.lax.stop_gradient(jnp.mean(jnp.abs(w), axis=1, keepdims=True))
            bw = alpha * jnp.sign(w)
            return w + jax.lax.stop_gradient(bw - w)
        bw1 = _binarize(w1)
        h = jnp.einsum('bsd,hd->bsh', x, bw1) + b1
        h = jax.nn.gelu(h, approximate=False)
        bw2 = _binarize(w2)
        out = jnp.einsum('bsh,dh->bsd', h, bw2) + b2
        return out
    x = L0_attn_x
    x = x + 0.5 * _L0_ffn_ref(_layernorm(x, axis=-1), L0_ffn_gate_w, L0_ffn_experts_gate_up, L0_ffn_experts_down, L0_ffn_shared_gate_w, L0_ffn_shared_up_w, L0_ffn_shared_down_w, L0_ffn_shared_expert_gate_w)
    x = x + _L0_attn_ref(_layernorm(x, axis=-1), L0_attn_W_qkv, L0_attn_b_qkv)
    x = x + 0.5 * _L0_ffn_ref(_layernorm(x, axis=-1), L0_ffn_gate_w, L0_ffn_experts_gate_up, L0_ffn_experts_down, L0_ffn_shared_gate_w, L0_ffn_shared_up_w, L0_ffn_shared_down_w, L0_ffn_shared_expert_gate_w)
    x = x + 0.5 * _L1_ffn_ref(_layernorm(x, axis=-1), L1_ffn_ln_g, L1_ffn_ln_b, L1_ffn_wq, L1_ffn_wk, L1_ffn_wv, L1_ffn_wo, L1_ffn_gate_w, L1_ffn_w1, L1_ffn_b1, L1_ffn_w2, L1_ffn_b2)
    x = x + _L1_attn_ref(_layernorm(x, axis=-1), L1_attn_wq, L1_attn_wk, L1_attn_wv, L1_attn_wo)
    x = x + 0.5 * _L1_ffn_ref(_layernorm(x, axis=-1), L1_ffn_ln_g, L1_ffn_ln_b, L1_ffn_wq, L1_ffn_wk, L1_ffn_wv, L1_ffn_wo, L1_ffn_gate_w, L1_ffn_w1, L1_ffn_b1, L1_ffn_w2, L1_ffn_b2)
    x = x + 0.5 * _L2_ffn_ref(_layernorm(x, axis=-1), L2_ffn_W_fc, L2_ffn_ln_w, L2_ffn_ln_b, L2_ffn_W_proj)
    x = x + _L2_attn_ref(_layernorm(x, axis=-1), L2_attn_Wq, L2_attn_Wk, L2_attn_Wv, L2_attn_Wo)
    x = x + 0.5 * _L2_ffn_ref(_layernorm(x, axis=-1), L2_ffn_W_fc, L2_ffn_ln_w, L2_ffn_ln_b, L2_ffn_W_proj)
    x = x + 0.5 * _L3_ffn_ref(_layernorm(x, axis=-1), L3_ffn_w1, L3_ffn_b1, L3_ffn_w2, L3_ffn_b2)
    x = x + _L3_attn_ref(_layernorm(x, axis=-1), L3_attn_q_w, L3_attn_q_b, L3_attn_k_w, L3_attn_k_b, L3_attn_v_w, L3_attn_v_b, L3_attn_o_w, L3_attn_o_b, L3_attn_ln1_w, L3_attn_ln1_b, L3_attn_ln2_w, L3_attn_ln2_b, L3_attn_dec_w, L3_attn_dec_b, L3_attn_f1_w, L3_attn_f1_b, L3_attn_f2_w, L3_attn_f2_b)
    x = x + 0.5 * _L3_ffn_ref(_layernorm(x, axis=-1), L3_ffn_w1, L3_ffn_b1, L3_ffn_w2, L3_ffn_b2)
    return x

_drawn_inputs = setup_inputs


def setup_inputs(seed=0):
    import zlib

    import numpy as np

    out = dict(_drawn_inputs(seed))
    spreads = {'L1_ffn_ln_g': (1.0, 0.6),
     'L1_ffn_ln_b': (0.0, 0.8),
     'L1_ffn_b1': (0.0, 0.8),
     'L1_ffn_b2': (0.0, 0.8),
     'L2_ffn_ln_w': (1.0, 0.2),
     'L2_ffn_ln_b': (0.0, 0.1),
     'L3_attn_q_b': (0.0, 2.0),
     'L3_attn_k_b': (0.0, 2.0),
     'L3_attn_v_b': (0.0, 0.8),
     'L3_attn_o_b': (0.0, 2.0),
     'L3_attn_ln1_w': (1.0, 0.6),
     'L3_attn_ln1_b': (0.0, 0.8),
     'L3_attn_ln2_w': (1.0, 0.6),
     'L3_attn_ln2_b': (0.0, 0.8),
     'L3_attn_dec_b': (5.0, 0.6),
     'L3_attn_f1_b': (0.0, 0.8),
     'L3_attn_f2_b': (0.0, 2.0)}
    factors = {'L0_ffn_gate_w': 8.0,
     'L0_ffn_experts_gate_up': 8.0,
     'L0_ffn_experts_down': 8.0,
     'L0_ffn_shared_gate_w': 8.0,
     'L0_ffn_shared_up_w': 8.0,
     'L0_ffn_shared_down_w': 8.0,
     'L0_ffn_shared_expert_gate_w': 8.0,
     'L1_attn_wq': 3.782,
     'L1_attn_wk': 3.569,
     'L1_ffn_wq': 6.58,
     'L1_ffn_wk': 6.007,
     'L1_ffn_wv': 5.173,
     'L1_ffn_wo': 5.057,
     'L2_attn_Wq': 8.0,
     'L2_attn_Wk': 8.0,
     'L2_attn_Wv': 8.0,
     'L2_attn_Wo': 8.0,
     'L3_attn_q_w': 31.537,
     'L3_attn_k_w': 24.411,
     'L3_attn_v_w': 8.0,
     'L3_attn_o_w': 8.0,
     'L3_attn_dec_w': 8.0,
     'L3_attn_f1_w': 8.0,
     'L3_attn_f2_w': 8.0,
     'L3_ffn_w1': 8.0,
     'L3_ffn_b1': 64.0,
     'L3_ffn_w2': 8.0,
     'L3_ffn_b2': 64.0}
    for name, (base, spread) in spreads.items():
        noise = np.random.default_rng([zlib.crc32(name.encode()), seed]).standard_normal(out[name].shape)
        drawn = base * np.exp(spread * noise) if base else spread * noise
        out[name] = jnp.asarray(drawn.astype(out[name].dtype))
    for name, factor in factors.items():
        out[name] = (out[name] * factor).astype(out[name].dtype)
    return out
```

```python
from collections import namedtuple
from contextlib import ExitStack

import concourse.bass as bass
from concourse import mybir

F32 = mybir.dt.float32
BF16 = mybir.dt.bfloat16
ACT = mybir.ActivationFunctionType
ALU = mybir.AluOpType
AXX = mybir.AxisListType.X

P = 128
D = 128
BATCH, SEQ = 2, 1024
TOKENS = BATCH * SEQ
TILES = TOKENS // P
CHUNK = 512
CHUNKS = TOKENS // CHUNK
TPC = CHUNK // P
KB = SEQ // P
EPS = 1e-5
GROUP = 4

EXPERTS, INTER = 8, 176
WAYS = EXPERTS + 2
PAIRS = WAYS // 2
TAIL = INTER - P
FF = 512
FT = FF // P

TP = 0


class Tally:

    def __init__(self, sem, base=0):
        self.sem, self.base, self.n = sem, base, 0

    def done(self, ins):
        ins.then_inc(self.sem, 1)
        self.n += 1

    def settle(self, eng, ins):
        self.done(ins)
        eng.wait_ge(self.sem, self.base + self.n)


def Sems(nc, tag, names):
    names = names.split()
    return namedtuple("Sems", names)(*[nc.alloc_semaphore(name=f"{tag}_{n}") for n in names])


def macaron(nc, a, out):
    with ExitStack() as ctx:
        def sb(name, shape, dt=F32):
            return ctx.enter_context(nc.sbuf_tensor(name, shape, dt))[tuple([slice(None)] * len(shape))]

        def dram(name, shape, dt=F32):
            return nc.dram_tensor(name, shape, dt, kind="Internal").ap()

        def sems(tag, names):
            return Sems(nc, tag, names)

        ps = ctx.enter_context(nc.psum_tensor("ps", [P, 8, 512], F32))[:, :, :]

        x = sb("x", [P, TILES * D])
        xnT = sb("xnT", [P, TOKENS])
        res = sb("res", [P, TILES * D])
        xn = sb("xn", [P, TPC, D])
        stat = sb("stat", [P, TPC, 6])
        mv = sb("mv", [P, TPC, 2])
        var = sb("var", [P, TPC])
        rstd = sb("rstd", [P, TPC])
        neghalf = sb("neghalf", [P, TPC])

        ident = sb("ident", [P, P])
        identb = sb("identb", [P, P], BF16)
        masks = sb("masks", [P, 3, P])
        maskb = sb("maskb", [P, 2, P], BF16)
        ones = sb("ones", [P, P])
        lower = sb("lower", [P, EXPERTS * EXPERTS])
        cols = sb("cols", [P, 96])
        rows = sb("rows", [1, 10 * D])

        w2fc = sb("w2fc", [P, FF])
        w2pj = sb("w2pj", [P, FT, D])
        w3a = sb("w3a", [P, FF])
        w3b = sb("w3b", [P, FT, D])
        wproj = sb("wproj", [P, 4, D])

        ARENA = 31 * 1024
        arena = sb("arena", [P, ARENA])

        class Carve:
            def __init__(self):
                self.at = 0

            def __call__(self, n, dt=F32):
                words = n if dt == F32 else n // 2
                view = arena[:, self.at:self.at + words]
                self.at += words
                assert self.at <= ARENA, self.at
                return view if dt == F32 else view.bitcast(dt)

        names = ["b_q", "b_qs", "b_k", "b_ks", "ln_g", "ln_b"]
        col_at = {n: i for i, n in enumerate(names)}
        n_cols = len(names)
        for n, k in (("b_v", 0), ("b1_l1", EXPERTS * FT), ("l3w_b1", FT), ("l2_w", FT), ("l2_b", FT),
                     ("l3_f1b", FT), ("l3_qb", 1), ("l3_kb", 1), ("l3_db", 1), ("l3_vb", 8),
                     ("l3_g1", 1), ("l3_o1", 1), ("l3_g2", 1), ("l3_o2", 1), ("scr", 4)):
            col_at[n] = n_cols
            n_cols += k
        assert n_cols <= 96, n_cols

        def col(name, k=0):
            return cols[:, col_at[name] + k:col_at[name] + k + 1]

        def row(k):
            return rows[0:1, k * D:(k + 1) * D]

        ROW_B2, ROW_L3B2 = 0, 8

        boot = sems("boot", "const cols zero ones gsum gabs gcol quant bsign bsum bw vec pool")
        COLS_SHARED = ["ln_g", "ln_b", "b1_l1", "l3w_b1", "l2_w", "l2_b", "l3_f1b", "l3_qb", "l3_kb",
                       "l3_db", "l3_vb", "l3_g1", "l3_o1", "l3_g2", "l3_o2"]

        def norm_vector(dve, s, t, src, dst, chunk):
            for n in range(TPC):
                last = nc.vector.bn_stats(stat[:, n, :], src(n))
            t.settle(dve, last)
            for n in range(TPC):
                last = nc.vector.bn_aggr(mv[:, n, :], stat[:, n, :])
            last.then_inc(s.stats, 1)
            dve.wait_ge(s.rstd, chunk + 1)
            for n in range(TPC):
                last = nc.vector.tensor_scalar(dst(n), src(n), mv[:, n, 0:1], rstd[:, n:n + 1],
                                               ALU.subtract, ALU.mult)
            return last

        def norm_gpsimd(pool, s, t, chunk):
            pool.wait_ge(s.stats, chunk + 1)
            t.settle(pool, nc.gpsimd.tensor_scalar(var[:, :], mv[:, :, 1], EPS, None, ALU.add))
            nc.gpsimd.tensor_tensor(rstd[:, :], var[:, :], neghalf[:, :], ALU.pow).then_inc(s.rstd, 1)

        def norm_tensor(pe, s, chunk):
            pe.wait_ge(s.xn, chunk + 1)
            pe.wait_ge(s.xT, chunk)
            for n in range(TPC):
                last = nc.tensor.transpose(ps[:, TP, n * P:(n + 1) * P], xn[:, n, :], ident[:, :])
            last.then_inc(s.tp, 1)

        UPS, HS = 6 * PAIRS, 3 * PAIRS
        RING, FIRST_UP, FIRST_Y = 5, 1, 6
        up_w = dn_w = None

        def moe(tag):
            c = Carve()
            up_w = c(UPS * P)
            dn_w = c(PAIRS * 3 * D)
            gate_w = c(EXPERTS + 1)
            hid = c(HS * CHUNK).rearrange("p (n t) -> p n t", n=HS)
            sg = c(3 * CHUNK).rearrange("p (n t) -> p n t", n=3)
            gT = c(CHUNK)
            lg = c(TPC * 9).rearrange("p (n e) -> p n e", e=9)
            ex = c(TPC * 9).rearrange("p (n e) -> p n e", e=9)
            mx = c(TPC)
            den = c(TPC)
            cmp = c(TPC * 64).rearrange("p (n e f) -> p n e f", e=8, f=8)
            eq = c(TPC * 64).rearrange("p (n e f) -> p n e f", e=8, f=8)
            rank = c(TPC * 8).rearrange("p (n e) -> p n e", e=8)
            wts = c(TPC * WAYS).rearrange("p (n e) -> p n e", e=WAYS)
            s = sems(tag, "w stats rstd xn tp xT vec pool gmm gcopy gtp shift gexp up silu h y yused")
            VEC = 13

            def sync(sp):
                sp.dma_start(gate_w, a["gate0"]).then_inc(s.w, 16)
                sp.dma_start(up_w, a["up0"]).then_inc(s.w, 16)
                sp.dma_start(dn_w, a["down0"]).then_inc(s.w, 16)

            def tensor(pe):
                def up(ch, first, end):
                    for k in range(first, end):
                        if k % 2:
                            pe.wait_ge(s.silu, ch * HS + (k - 5) // 2 + 1 + 3)
                        else:
                            pe.wait_ge(s.h, ch * HS + (k - 6) // 2 + 1 + 3)
                        nc.tensor.matmul(ps[:, FIRST_UP + k % RING, :], up_w[:, k * P:(k + 1) * P],
                                         xnT[:, ch * CHUNK:(ch + 1) * CHUNK], start=True, stop=True)\
                            .then_inc(s.up, 1)

                def down(ch, p):
                    pe.wait_ge(s.h, ch * HS + 3 * p + 3 + 3)
                    for half in range(2):
                        way = 2 * p + half
                        pe.wait_ge(s.yused, ch * WAYS + way - 2 + 1 + 2)
                        bank = FIRST_Y + half
                        r = slice(64 * half, 64 * half + 64)
                        for n in range(TPC):
                            t = slice(n * P, (n + 1) * P)
                            nc.tensor.matmul(ps[:, bank, t], hid[:, 3 * p + half, t],
                                             dn_w[:, (3 * p + half) * D:(3 * p + half + 1) * D],
                                             start=True, stop=False)
                            last = nc.tensor.matmul(ps[:, bank, t], hid[r, 3 * p + 2, t],
                                                    dn_w[r, (3 * p + 2) * D:(3 * p + 3) * D],
                                                    start=False, stop=True)
                        last.then_inc(s.y, 1)

                pe.wait_ge(s.w, 48)
                for ch in range(CHUNKS):
                    norm_tensor(pe, s, ch)
                    pe.wait_ge(s.xT, ch + 1)
                    nc.tensor.matmul(ps[0:9, TP, :], gate_w, xnT[:, ch * CHUNK:(ch + 1) * CHUNK],
                                     start=True, stop=True).then_inc(s.gmm, 1)
                    up(ch, 0, 3)
                    pe.wait_ge(s.gcopy, ch + 1)
                    for n in range(TPC):
                        last = nc.tensor.transpose(ps[:, TP, n * 16:n * 16 + 9],
                                                   gT[0:9, n * P:(n + 1) * P], ident[0:9, 0:9])
                    last.then_inc(s.gtp, 1)
                    up(ch, 3, 6)
                    for p in range(PAIRS):
                        if p + 1 < PAIRS:
                            up(ch, 6 * p + 6, 6 * p + 12)
                        down(ch, p)

            def scalar(act):
                act.sem_inc(s.silu, 3)
                for ch in range(CHUNKS):
                    act.wait_ge(s.tp, ch + 1)
                    nc.scalar.activation(xnT[:, ch * CHUNK:(ch + 1) * CHUNK], ps[:, TP, :], ACT.Copy)\
                        .then_inc(s.xT, 1)
                    act.wait_ge(s.gmm, ch + 1)
                    nc.scalar.activation(gT[0:9, :], ps[0:9, TP, :], ACT.Copy).then_inc(s.gcopy, 1)
                    act.wait_ge(s.shift, ch + 1)
                    nc.scalar.activation(ex, lg, ACT.Exp).then_inc(s.gexp, 1)
                    for n in range(HS):
                        act.wait_ge(s.up, ch * UPS + 2 * n + 1)
                        act.wait_ge(s.h, ch * HS + n - 3 + 1 + 3)
                        nc.scalar.activation(sg[:, n % 3, :], ps[:, FIRST_UP + (2 * n) % RING, :],
                                             ACT.Silu).then_inc(s.silu, 1)

            def gpsimd(pool):
                for ch in range(CHUNKS):
                    norm_gpsimd(pool, s, Tally(s.pool, ch), ch)

            def vector(dve):
                dve.sem_inc(s.h, 3)
                dve.sem_inc(s.yused, 2)
                for ch in range(CHUNKS):
                    t = Tally(s.vec, ch * VEC)

                    def tile(n):
                        return x[:, ch * CHUNK + n * D:ch * CHUNK + (n + 1) * D]

                    last = norm_vector(dve, s, t, tile, lambda n: xn[:, n, :], ch)
                    last.then_inc(s.xn, 1)
                    dve.wait_ge(s.gtp, ch + 1)
                    zp = ps[:, TP, 0:TPC * 16].rearrange("p (n e) -> p n e", e=16)
                    nc.vector.tensor_reduce(mx, zp[:, :, 0:8], AXX, ALU.max)
                    t.settle(dve, nc.vector.tensor_scalar(lg[:, :, 8:9], zp[:, :, 8:9], -1.0, None,
                                                          ALU.mult))
                    nc.vector.tensor_tensor(lg[:, :, 0:8], zp[:, :, 0:8],
                                            mx.unsqueeze(2).to_broadcast([P, TPC, 8]),
                                            ALU.subtract).then_inc(s.shift, 1)
                    dve.wait_ge(s.gexp, ch + 1)
                    t.settle(dve, nc.vector.tensor_reduce(den, ex[:, :, 0:8], AXX, ALU.add))
                    t.settle(dve, nc.vector.reciprocal(den, den))
                    t.settle(dve, nc.vector.tensor_tensor(
                        ex[:, :, 0:8], ex[:, :, 0:8], den.unsqueeze(2).to_broadcast([P, TPC, 8]),
                        ALU.mult))
                    mine = ex[:, :, 0:8].unsqueeze(3).to_broadcast([P, TPC, 8, 8])
                    for n in range(TPC):
                        e_of = ex[:, n, 0:8].unsqueeze(2).to_broadcast([P, 8, 8])
                        f_of = ex[:, n, 0:8].unsqueeze(1).to_broadcast([P, 8, 8])
                        nc.vector.tensor_tensor(cmp[:, n], f_of, e_of, ALU.is_gt)
                        last = nc.vector.tensor_tensor(eq[:, n], f_of, e_of, ALU.is_equal)
                    t.settle(dve, last)
                    for n in range(TPC):
                        last = nc.vector.tensor_tensor(eq[:, n], eq[:, n],
                                                       lower.rearrange("p (e f) -> p e f", e=8),
                                                       ALU.mult)
                    t.settle(dve, last)
                    t.settle(dve, nc.vector.tensor_tensor(
                        cmp.rearrange("p n e f -> p (n e f)"), cmp.rearrange("p n e f -> p (n e f)"),
                        eq.rearrange("p n e f -> p (n e f)"), ALU.add))
                    t.settle(dve, nc.vector.tensor_reduce(rank, cmp, AXX, ALU.add))
                    t.settle(dve, nc.vector.tensor_scalar(rank, rank, 1.5, 0.5, ALU.is_lt, ALU.mult))
                    nc.vector.tensor_tensor(wts[:, :, 0:8], rank, ex[:, :, 0:8], ALU.mult)
                    t.settle(dve, nc.vector.tensor_scalar(wts[:, :, 8:9], ex[:, :, 8:9], 1.0, 2.0,
                                                          ALU.add, ALU.mult))
                    t.settle(dve, nc.vector.reciprocal(wts[:, :, 8:9], wts[:, :, 8:9]))
                    t.settle(dve, nc.vector.tensor_copy(wts[:, :, 9:10], wts[:, :, 8:9]))

                    def gated(n):
                        dve.wait_ge(s.silu, ch * HS + n + 1 + 3)
                        dve.wait_ge(s.up, ch * UPS + 2 * n + 2)
                        if n % 3 == 0:
                            dve.wait_ge(s.y, (ch + 1) * WAYS - 10 + 0)
                        nc.vector.tensor_tensor(hid[:, n, :], sg[:, n % 3, :],
                                                ps[:, FIRST_UP + (2 * n + 1) % RING, :], ALU.mult)\
                            .then_inc(s.h, 1)

                    def add(way):
                        dve.wait_ge(s.y, ch * WAYS + way + 1)
                        if way:
                            dve.wait_ge(s.yused, ch * WAYS + way + 2)
                        for n in range(TPC):
                            last = nc.vector.scalar_tensor_tensor(
                                tile(n), ps[:, FIRST_Y + way % 2, n * P:(n + 1) * P],
                                wts[:, n, way:way + 1], tile(n), ALU.mult, ALU.add)
                        last.then_inc(s.yused, 1)

                    for n in range(3):
                        gated(n)
                    for p in range(PAIRS):
                        if p + 1 < PAIRS:
                            for n in range(3 * p + 3, 3 * p + 6):
                                gated(n)
                        add(2 * p)
                        add(2 * p + 1)
                    assert t.n == VEC, t.n

            return dict(sync=sync, tensor=tensor, scalar=scalar, gpsimd=gpsimd, vector=vector, sems=s)

        S_SLOT = 0
        ST_RING = 4
        O_BANK = 7

        def attention(tag, hd, kind, rope, scale, weights, has_wo, double):
            heads = D // hd
            HG = heads // GROUP
            UNITS = BATCH * HG
            R = 9 * hd
            KR = R + 3 if kind != "linear" else R
            rows4 = GROUP * hd
            soft = kind != "linear"
            full = kind == "full"
            halves = []
            for qc in range(2):
                kbs = range(KB) if full else range(4 * qc + 4)
                halves.append([(qc, kb, 0 if full or kb < 4 * qc else (kb - 4 * qc) * P)
                               for kb in kbs])
            steps = halves[0] + halves[1]
            NS = len(steps)
            ends = [len(halves[0]) - 1, NS - 1]

            qs = dram(f"{tag}_q", [3, UNITS * rows4, SEQ], BF16)
            ks = dram(f"{tag}_k", [3, UNITS * rows4, SEQ], BF16)
            ot = dram(f"{tag}_o", [UNITS * GROUP * (hd + 1), SEQ])

            c = Carve()
            if double:
                w1 = c(EXPERTS * FF)
                w2 = c(EXPERTS * FF)
            v_sb = c(UNITS * KB * rows4)
            v_un = v_sb.rearrange("p (u k r) -> p u k r", u=UNITS, k=KB)
            base = c.at
            Qop = [c(GROUP * SEQ, BF16).rearrange("p (j t) -> p j t", j=GROUP) for _ in range(3)]
            Kop = [c(GROUP * SEQ, BF16).rearrange("p (j t) -> p j t", j=GROUP) for _ in range(3)]
            pr = c(8 * CHUNK).rearrange("p (n t) -> p n t", n=8)
            vx = [c(KB * GROUP * 32).rearrange("p (k j c) -> p k j c", k=KB, j=GROUP) for _ in range(3)]
            osb = c(2 * CHUNK).rearrange("p (n t) -> p n t", n=2)
            mq = c(2 * 16).rearrange("p (n m) -> p n m", n=2)
            mT = c(P)
            mr = c(P)
            ms = c(2 * 3 * P, BF16).rearrange("p (n a t) -> p n a t", n=2, a=3)
            c.at = base
            tab = c(2 * SEQ).rearrange("p (n t) -> p n t", n=2)
            rot = c(2 * CHUNK).rearrange("p (n t) -> p n t", n=2)
            rem = c(2 * CHUNK).rearrange("p (n t) -> p n t", n=2)
            cut = [c(3 * CHUNK, BF16).rearrange("p (a t) -> p a t", a=3) for _ in range(2)]
            c.at = base
            num = c(SEQ * 2)
            den = c(SEQ * 2)
            hT = c(FT * 2 * P).rearrange("p (f t) -> p f t", f=FT)

            s = sems(tag, "w tab stats rstd xn tp xT vec pool proj rope cut0 rem1 cut1 cut2 qst kst "
                          "vps vcp ops0 ops1 ops2 kneg vset vx s sread mtp mcp mps ml0 ml1 st ex msk "
                          "av ocp ost0 ost1 nl0 nl1 oT y x up gel")
            cut_stored = (s.qst, s.kst)
            operands = (s.ops0, s.ops1, s.ops2)
            max_placed = (s.ml0, s.ml1)
            sums_stored = (s.ost0, s.ost1)
            sums_loaded = (s.nl0, s.nl1)
            N_OPS = 18

            def sync(sp):
                for n, w in enumerate(weights):
                    sp.dma_start(wproj[:, n, :], a[w]).then_inc(s.w, 16)
                if rope:
                    sp.dma_start(wprs[:, 0, :], a[rope + "_wqs"]).then_inc(s.w, 16)
                    sp.dma_start(wprs[:, 1, :], a[rope + "_wks"]).then_inc(s.w, 16)
                    sp.dma_start(tab, a[rope + "_tab"]).then_inc(s.tab, 16)
                if double:
                    sp.dma_start(w1, a["w1_1"]).then_inc(s.w, 16)
                    sp.dma_start(w2, a["w2_1"]).then_inc(s.w, 16)
                for ch in range(CHUNKS):
                    b, t0 = ch // 2, (ch % 2) * CHUNK
                    for side, to in ((0, qs), (1, ks)):
                        sp.wait_ge(s.cut2, 2 * ch + side + 1)
                        for part in range(3):
                            sp.dma_start(to[part, b * P:(b + 1) * P, t0:t0 + CHUNK],
                                         cut[side][:, part, :]).then_inc(cut_stored[side], 16)
                sp.wait_ge(s.qst, 16 * 3 * CHUNKS)
                sp.wait_ge(s.kst, 16 * 3 * CHUNKS)
                sp.wait_ge(s.kneg, 3)

                def load(u, par):
                    r0 = bass.ds(u * rows4, rows4)
                    for i in range(3):
                        for n in range(3):
                            r = slice((3 * i + n) * hd, (3 * i + n + 1) * hd)
                            sp.dma_start(Qop[par][r], qs[i, r0, :].rearrange(
                                "(j d) t -> d j t", d=hd)).then_inc(operands[par], 16)
                            sp.dma_start(Kop[par][r], ks[n, r0, :].rearrange(
                                "(j d) t -> d j t", d=hd)).then_inc(operands[par], 16)

                def put_max(u, par, qc):
                    sp.wait_ge(s.mps, 2 * u + qc + 1)
                    for i in range(3):
                        for j in range(GROUP):
                            sp.dma_start(Qop[par][R + i:R + i + 1, j, qc * CHUNK:(qc + 1) * CHUNK],
                                         ms[4 * j:4 * j + 4, qc, i, :]).then_inc(max_placed[qc], 16)

                def store(u, qc):
                    sp.wait_ge(s.ocp, 2 * u + qc + 1 + 1)
                    for j in range(GROUP):
                        sp.dma_start(ot[bass.ds((u * GROUP + j) * (hd + 1), hd + 1),
                                        qc * CHUNK:(qc + 1) * CHUNK],
                                     osb[32 * j:32 * j + hd + 1, qc, :]).then_inc(sums_stored[qc], 16)

                def unit(u, third, par, ahead2, ahead1):
                    if soft:
                        put_max(u, par, 1)
                    if ahead2:
                        sp.wait_ge(s.st, u * 4 * NS + 1)
                        load(u + 2, (par + 2) % 3)
                    store(u, 0)
                    if soft and ahead1:
                        put_max(u + 1, (par + 1) % 3, 0)
                    store(u, 1)

                load(0, 0)
                load(1, 1)
                if soft:
                    put_max(0, 0, 0)
                loops(sp, unit)
                sp.wait_ge(s.ost0, 64 * UNITS + 1)
                sp.wait_ge(s.ost1, 64 * UNITS + 1)
                for b in range(BATCH):
                    src = ot.rearrange("(b h d) t -> b h d t", b=BATCH, d=hd + 1)[b]
                    sp.dma_start(num[:, b * SEQ:(b + 1) * SEQ], src[:, 0:hd, :]).then_inc(sums_loaded[b], 16)
                    if soft:
                        sp.dma_start(den[:, b * SEQ:(b + 1) * SEQ],
                                     src[:, hd:hd + 1, :].to_broadcast([heads, hd, SEQ]))\
                            .then_inc(sums_loaded[b], 16)

            def loops(eng, unit):
                whole = (UNITS - 2) // 3
                with eng.Fori(0, whole) as i:
                    for par in range(3):
                        unit(i * 3 + par, i, par, True, True)
                for u in range(3 * whole, UNITS):
                    unit(u, u // 3, u % 3, u + 2 < UNITS, u + 1 < UNITS)

            def s_tasks(half):
                return [(j, qb) for qb in range(4) for j in range(GROUP)]

            def tensor(pe):
                pe.wait_ge(s.w, 16 * (len(weights) + (2 if rope else 0) + (2 if double else 0)))
                for ch in range(CHUNKS):
                    norm_tensor(pe, s, ch)
                    pe.wait_ge(s.xT, ch + 1)
                    t = slice(ch * CHUNK, (ch + 1) * CHUNK)
                    for side in range(2):
                        if ch:
                            pe.wait_ge(s.rem1, 2 * (ch - 1) + side + 1)
                        last = nc.tensor.matmul(ps[:, 1 + 2 * side, :], wproj[:, side, :], xnT[:, t],
                                                start=True, stop=True)
                        if rope:
                            last = nc.tensor.matmul(ps[:, 2 + 2 * side, :], wprs[:, side, :],
                                                    xnT[:, t], start=True, stop=True)
                        last.then_inc(s.proj, 1)
                    if ch:
                        pe.wait_ge(s.vcp, ch)
                    for n in range(TPC):
                        last = nc.tensor.matmul(ps[:, 5, n * P:(n + 1) * P],
                                                xnT[:, ch * CHUNK + n * P:ch * CHUNK + (n + 1) * P],
                                                wproj[:, 2, :], start=True, stop=not bias_v)
                        if bias_v:
                            last = nc.tensor.matmul(ps[:, 5, n * P:(n + 1) * P], ones[0:1, :],
                                                    row(9), start=False, stop=True)
                    last.then_inc(s.vps, 1)

                def slot(pos):
                    b = S_SLOT + 2 * (pos % 2)
                    return ps[:, b:b + 2, :]

                def wait_slot(u, pos):
                    q = pos - 2
                    uu = u if q >= 0 else u - 1
                    q %= 34
                    if q in (0, 17):
                        pe.wait_ge(s.mcp, 2 * uu + (3 if q == 17 else 2))
                    else:
                        pe.wait_ge(s.sread, (uu + 1) * 32 + (q - 1 if q < 17 else q - 2) + 1)

                def scores(u, par, half, k, fresh=False):
                    j, qb = s_tasks(half)[k]
                    pos = 1 + k + 17 * half
                    if not (fresh and pos < 3):
                        wait_slot(u, pos)
                    q0 = half * CHUNK + qb * P
                    width = SEQ if full else q0 + P
                    at = slot(pos)
                    last = None
                    for k0 in range(0, width, CHUNK):
                        n = min(CHUNK, width - k0)
                        last = nc.tensor.matmul(at[:, k0 // CHUNK, 0:n], Qop[par][0:R, j, q0:q0 + P],
                                                Kop[par][0:R, j, k0:k0 + n], start=True,
                                                stop=full or k0 + n < width)
                    if not full:
                        off = (width - P) % CHUNK
                        last = nc.tensor.matmul(at[:, (width - 1) // CHUNK, off:off + P], identb[:, :],
                                                maskb[:, 0, :], start=False, stop=True)
                    last.then_inc(s.s, 1)

                def turn_max(u, pos, hn, fresh=False):
                    if not fresh:
                        wait_slot(u, pos)
                    pe.wait_ge(s.sread, 16 * (hn + 1))
                    nc.tensor.transpose(slot(pos)[0:16, 0, 0:P], mq[:, 0 if pos else 1, :],
                                        ident[:, :]).then_inc(s.mtp, 1)

                def attend(u, vpar, at):
                    qc, kb, off = steps[at]
                    pe.wait_ge(s.ex, u * 4 * NS + 4 * at + 4 + 3)
                    if not soft and (kb >= 4 * qc):
                        pe.wait_ge(s.msk, (u * 8 + kb + 1))
                    if kb == 0:
                        pe.wait_ge(s.vx, u + 1)
                        pe.wait_ge(s.ocp, 2 * u + qc + 1)
                    for j in range(GROUP):
                        last = nc.tensor.matmul(ps[32 * j:32 * j + 32, O_BANK, off:CHUNK],
                                                vx[vpar][:, kb, j, :],
                                                pr[:, (at % 2) * 4 + j, off:CHUNK],
                                                start=kb == 0, stop=at in ends,
                                                tile_position=(0, 32 * j), skip_group_check=True)
                    last.then_inc(s.av, 1)

                def unit(u, third, par, ahead2, ahead1):
                    for at, (qc, kb, off) in enumerate(steps):
                        if soft and kb == 0:
                            pe.wait_ge(max_placed[qc], 16 * 12 * (u + 1) + 1)
                        if at == 0:
                            if soft:
                                if ahead1:
                                    pe.wait_ge(operands[(par + 1) % 3],
                                               16 * N_OPS * (third + 1 + par // 2))
                            else:
                                pe.wait_ge(operands[par], 16 * N_OPS * (third + 1))
                        todo = []
                        if soft:
                            if kb == 0 and (qc == 0 or ahead1):
                                todo.append(("turn", 17 * qc, 2 * u + 1 + qc))
                            if ahead1:
                                per = 16 // len(halves[qc])
                                todo += [("s", qc, per * kb + n) for n in range(per)]

                        def run(task):
                            if task[0] == "turn":
                                turn_max(u, task[1], task[2])
                            else:
                                scores(u, (par + 1) % 3, task[1], task[2])

                        for j in range(GROUP):
                            n = (par * 4 * NS + 4 * at + j) % 3
                            pe.wait_ge(s.ex, u * 4 * NS + 4 * at + j + 1)
                            diag = not full and kb >= 4 * qc
                            last = nc.tensor.matmul(
                                ps[:, ST_RING + n, off:CHUNK], Kop[par][0:KR, j, kb * P:(kb + 1) * P],
                                Qop[par][0:KR, j, qc * CHUNK + off:(qc + 1) * CHUNK],
                                start=True, stop=not (diag and soft))
                            if diag and soft:
                                last = nc.tensor.matmul(ps[:, ST_RING + n, off:off + P], identb[:, :],
                                                        maskb[:, 1, :], start=False, stop=True)
                            last.then_inc(s.st, 1)
                            if j % 2 and todo:
                                run(todo.pop(0))
                        for task in todo:
                            run(task)
                        if at:
                            attend(u, par, at - 1)
                    attend(u, par, NS - 1)

                pe.wait_ge(s.vcp, CHUNKS)
                pe.wait_ge(s.rem1, 2 * CHUNKS)
                pe.wait_ge(s.ops0, 16 * N_OPS)
                if soft:
                    for k in range(16):
                        scores(-1, 0, 0, k, fresh=True)
                    wait_slot(-1, 17)
                    turn_max(-1, 17, 0, fresh=True)
                    for k in range(16):
                        scores(-1, 0, 1, k)
                loops(pe, unit)

                if double:
                    for ch in range(CHUNKS):
                        pe.wait_ge(s.oT, ch + 1)
                        if ch >= 2:
                            pe.wait_ge(s.x, ch - 1)
                        t = slice(ch * CHUNK, (ch + 1) * CHUNK)
                        for n in range(TPC):
                            tn = slice(ch * CHUNK + n * P, ch * CHUNK + (n + 1) * P)
                            nc.tensor.matmul(ps[:, ch % 2, n * P:(n + 1) * P], wproj[:, 3, :],
                                             num[:, tn], start=True, stop=False)
                            r = slice(ch * CHUNK + n * D, ch * CHUNK + (n + 1) * D)
                            last = nc.tensor.matmul(ps[:, ch % 2, n * P:(n + 1) * P], res[:, r],
                                                    ident[:, :], start=False, stop=True)
                        last.then_inc(s.y, 1)
                    pe.wait_ge(s.x, CHUNKS)
                    xf = xnT.rearrange("p (m t) -> p m t", m=2)

                    def up(e):
                        for f in range(FT):
                            if e:
                                pe.wait_ge(s.gel, 4 * (e - 1) + f + 1)
                            nc.tensor.matmul(ps[:, 2 + f, 0:2 * P], w1[:, e * FF + f * P:e * FF + (f + 1) * P],
                                             xf[:, :, e * P:(e + 1) * P], start=True, stop=True)\
                                .then_inc(s.up, 1)

                    def dn(e):
                        pe.wait_ge(s.gel, 4 * e + 4)
                        if e >= 2:
                            pe.wait_ge(s.x, CHUNKS + e - 1)
                        for m in range(2):
                            at = ps[:, e % 2, m * P:(m + 1) * P]
                            for f in range(FT):
                                nc.tensor.matmul(at, hT2[:, e % 2, f, m * P:(m + 1) * P],
                                                 w2[:, (e * FT + f) * D:(e * FT + f + 1) * D],
                                                 start=f == 0, stop=False)
                            last = nc.tensor.matmul(at, ones[0:1, :], row(ROW_B2 + e), start=False,
                                                    stop=True)
                        last.then_inc(s.y, 1)

                    up(0)
                    for e in range(EXPERTS):
                        if e + 1 < EXPERTS:
                            up(e + 1)
                        dn(e)
                else:
                    for ch in range(CHUNKS):
                        pe.wait_ge(s.oT, ch + 1)
                        if ch >= 2:
                            pe.wait_ge(s.x, ch - 1)
                        for n in range(TPC):
                            at = ps[:, ch % 2, n * P:(n + 1) * P]
                            t = slice(ch * CHUNK + n * P, ch * CHUNK + (n + 1) * P)
                            if has_wo:
                                last = nc.tensor.matmul(at, num[:, t], wproj[:, 3, :], start=True,
                                                        stop=True)
                            else:
                                last = nc.tensor.transpose(at, num[:, t], ident[:, :])
                        last.then_inc(s.y, 1)

            bias = tag == "a0"
            bias_v = bias

            def scalar(act):
                act.sem_inc(s.ex, 3)
                act.sem_inc(s.ocp, 1)
                for ch in range(CHUNKS):
                    act.wait_ge(s.tp, ch + 1)
                    t = slice(ch * CHUNK, (ch + 1) * CHUNK)
                    if double:
                        nc.scalar.activation(xnT[:, t], ps[:, TP, :], ACT.Identity,
                                             bias=col("ln_b"), scale=col("ln_g")).then_inc(s.xT, 1)
                    else:
                        nc.scalar.activation(xnT[:, t], ps[:, TP, :], ACT.Copy).then_inc(s.xT, 1)
                    for side in range(2):
                        sc = scale if side == 0 else 1.0
                        if rope:
                            act.wait_ge(s.rope, 2 * ch + side + 1)
                            src = rot[:, side, :]
                        else:
                            act.wait_ge(s.proj, 2 * ch + side + 1)
                            src = ps[:, 1 + 2 * side, :]
                        if ch:
                            act.wait_ge(cut_stored[side], 48 * ch)
                        nc.scalar.activation(cut[side][:, 0, :], src, ACT.Copy, scale=sc)\
                            .then_inc(s.cut0, 1)
                        act.wait_ge(s.rem1, 2 * ch + side + 1)
                        nc.scalar.activation(cut[side][:, 1, :], rem[:, side, :], ACT.Copy)\
                            .then_inc(s.cut1, 1)
                    act.wait_ge(s.vps, ch + 1)
                    b, k0 = ch // 2, (ch % 2) * 4
                    for n in range(TPC):
                        last = nc.scalar.activation(
                            v_un[:, b * HG:(b + 1) * HG, k0 + n, :],
                            ps[:, 5, n * P:(n + 1) * P].rearrange("p (g r) -> p g r", g=HG), ACT.Copy)
                    last.then_inc(s.vcp, 1)

                def copy_max(hn, pos):
                    act.wait_ge(s.mtp, hn + 1)
                    act.wait_ge(s.mps, hn)
                    b = S_SLOT + 2 * (pos % 2)
                    nc.scalar.activation(mT[0:16, :], ps[0:16, b, 0:P], ACT.Copy).then_inc(s.mcp, 1)

                def copy_out(u, qc):
                    act.wait_ge(s.av, u * NS + ends[qc] + 1 + 2)
                    act.wait_ge(sums_stored[qc], 64 * u + 1)
                    nc.scalar.activation(osb[:, qc, :], ps[:, O_BANK, :], ACT.Copy).then_inc(s.ocp, 1)

                def unit(u, third, par, ahead2, ahead1):
                    for at, (qc, kb, off) in enumerate(steps):
                        for j in range(GROUP):
                            n = (par * 4 * NS + 4 * at + j) % 3
                            act.wait_ge(s.st, u * 4 * NS + 4 * at + j + 1 + 1)
                            if j == 0:
                                act.wait_ge(s.av, u * NS + at + 1)
                            nc.scalar.activation(pr[:, (at % 2) * 4 + j, off:CHUNK],
                                                 ps[:, ST_RING + n, off:CHUNK],
                                                 ACT.Exp if soft else ACT.Copy).then_inc(s.ex, 1)
                        if soft and kb == 0 and (qc == 0 or ahead1):
                            copy_max(2 * u + 1 + qc, 17 * qc)
                        if qc == 1 and kb == 0:
                            copy_out(u, 0)
                    copy_out(u, 1)

                if soft:
                    act.wait_ge(s.mtp, 1)
                    nc.scalar.activation(mT[0:16, :], ps[0:16, S_SLOT + 2, 0:P], ACT.Copy)\
                        .then_inc(s.mcp, 1)
                loops(act, unit)
                if double:
                    for e in range(EXPERTS):
                        for f in range(FT):
                            act.wait_ge(s.up, 4 * e + f + 1)
                            if e >= 2:
                                act.wait_ge(s.y, CHUNKS + e - 1)
                            nc.scalar.activation(hT2[:, e % 2, f, :], ps[:, 2 + f, 0:2 * P], ACT.Gelu,
                                                 bias=col("b1_l1", FT * e + f)).then_inc(s.gel, 1)

            if double:
                hT2 = hid2.rearrange("p (n f t) -> p n f t", n=2, f=FT)

            def gpsimd(pool):
                t = Tally(s.pool)
                for ch in range(CHUNKS * (2 if double else 1)):
                    norm_gpsimd(pool, s, t, ch)
                pool.wait_ge(s.qst, 16 * 3 * CHUNKS)
                pool.wait_ge(s.kst, 16 * 3 * CHUNKS)
                for par in range(3):
                    nc.gpsimd.memset(Kop[par], -1.0).then_inc(s.kneg, 1)
                    nc.gpsimd.memset(vx[par], 1.0).then_inc(s.vset, 1)
                pool.wait_ge(s.vset, 3)
                pool.wait_ge(s.vcp, CHUNKS)

                def values(u, par):
                    nc.gpsimd.tensor_tensor(
                        vx[par][:, :, :, 0:hd],
                        v_sb[:, bass.ds(u * KB * rows4, KB * rows4)]
                        .rearrange("p (k j d) -> p k j d", k=KB, j=GROUP),
                        ones[:, 0:1].unsqueeze(2).unsqueeze(3).to_broadcast([P, KB, GROUP, hd]),
                        ALU.mult).then_inc(s.vx, 1)

                def cut_max(u, qc):
                    hn = 2 * u + qc
                    pool.wait_ge(s.mcp, hn + 1)
                    pool.wait_ge(max_placed[qc], 16 * 12 * u + 1)
                    m = [ms[0:16, qc, i, :] for i in range(3)]
                    t = Tally(s.msk, 3 * hn)
                    t.settle(pool, nc.gpsimd.tensor_tensor(m[0], mT[0:16, :], ones[0:16, :], ALU.mult))
                    t.settle(pool, nc.gpsimd.tensor_tensor(mr[0:16, :], mT[0:16, :], m[0],
                                                           ALU.subtract))
                    t.settle(pool, nc.gpsimd.tensor_tensor(m[1], mr[0:16, :], ones[0:16, :], ALU.mult))
                    nc.gpsimd.tensor_tensor(m[2], mr[0:16, :], m[1], ALU.subtract)\
                        .then_inc(s.mps, 1)

                def unit(u, third, par, ahead2, ahead1):
                    if ahead1:
                        pool.wait_ge(s.av, u * NS + 1 + 1)
                        values(u + 1, (par + 1) % 3)
                    if soft:
                        cut_max(u, 1)
                        if ahead1:
                            cut_max(u + 1, 0)
                    else:
                        for qc in range(2):
                            for kb in range(4 * qc, 4 * qc + 4):
                                at = steps.index((qc, kb, (kb - 4 * qc) * P))
                                off = steps[at][2]
                                for j in range(GROUP):
                                    pool.wait_ge(s.ex, u * 4 * NS + 4 * at + j + 1 + 3)
                                    w = pr[:, (at % 2) * 4 + j, off:off + P]
                                    last = nc.gpsimd.tensor_tensor(w, w, masks[:, 2, :], ALU.mult)
                                last.then_inc(s.msk, 1)

                values(0, 0)
                if soft:
                    cut_max(0, 0)
                loops(pool, unit)

            def vector(dve):
                dve.sem_inc(s.av, 2)
                dve.sem_inc(s.st, 1)
                for sem in sums_stored + max_placed:
                    dve.sem_inc(sem, 1)
                t = Tally(s.vec)
                if rope:
                    dve.wait_ge(s.tab, 16)
                for ch in range(CHUNKS):
                    t0 = ch * CHUNK

                    def tile(n):
                        return x[:, t0 + n * D:t0 + (n + 1) * D]

                    def kept(n):
                        return res[:, t0 + n * D:t0 + (n + 1) * D]

                    def normed(n):
                        return xn[:, n, :]

                    if ch:
                        dve.wait_ge(s.tp, ch)
                    if double:
                        t.settle(dve, norm_vector(dve, s, t, tile, kept, 2 * ch))
                        last = norm_vector(dve, s, t, kept, normed, 2 * ch + 1)
                    else:
                        last = norm_vector(dve, s, t, tile, normed, ch)
                    last.then_inc(s.xn, 1)
                    tt = slice((ch % 2) * CHUNK, (ch % 2 + 1) * CHUNK)
                    for side in range(2):
                        sc = scale if side == 0 else 1.0
                        dve.wait_ge(s.proj, 2 * ch + side + 1)
                        src = ps[:, 1 + 2 * side, :]
                        if rope:
                            b = [col("b_q"), col("b_qs")] if side == 0 else [col("b_k"), col("b_ks")]
                            if bias:
                                nc.vector.scalar_tensor_tensor(rot[:, side, :], src, b[0], tab[:, 0, tt],
                                                               ALU.add, ALU.mult)
                                t.settle(dve, nc.vector.scalar_tensor_tensor(
                                    rem[:, side, :], ps[:, 2 + 2 * side, :], b[1], tab[:, 1, tt],
                                    ALU.add, ALU.mult))
                            else:
                                nc.vector.tensor_tensor(rot[:, side, :], src, tab[:, 0, tt], ALU.mult)
                                t.settle(dve, nc.vector.tensor_tensor(
                                    rem[:, side, :], ps[:, 2 + 2 * side, :], tab[:, 1, tt], ALU.mult))
                            nc.vector.tensor_tensor(rot[:, side, :], rot[:, side, :], rem[:, side, :],
                                                    ALU.add).then_inc(s.rope, 1)
                            src = rot[:, side, :]
                        dve.wait_ge(s.cut0, 2 * ch + side + 1)
                        nc.vector.scalar_tensor_tensor(rem[:, side, :], src, sc, cut[side][:, 0, :],
                                                       ALU.mult, ALU.subtract).then_inc(s.rem1, 1)
                        dve.wait_ge(s.cut1, 2 * ch + side + 1)
                        nc.vector.tensor_tensor(cut[side][:, 2, :], rem[:, side, :],
                                                cut[side][:, 1, :], ALU.subtract).then_inc(s.cut2, 1)

                def maxima(base, half):
                    for k, (j, qb) in enumerate(s_tasks(half)):
                        pos = 1 + k + 17 * half
                        dve.wait_ge(s.s, base + 16 * half + k + 1)
                        b = S_SLOT + 2 * (pos % 2)
                        width = SEQ if full else half * CHUNK + (qb + 1) * P
                        src = ps[:, b:b + 2, :].rearrange("p b t -> p (b t)")[:, 0:width]
                        nc.vector.tensor_reduce(mq[:, half, j * 4 + qb:j * 4 + qb + 1], src, AXX,
                                                ALU.max).then_inc(s.sread, 1)

                def unit(u, third, par, ahead2, ahead1):
                    if ahead1:
                        maxima((u + 1) * 32, 0)
                        maxima((u + 1) * 32, 1)

                if soft:
                    maxima(0, 0)
                    maxima(0, 1)
                    loops(dve, unit)

                if soft:
                    for b in range(BATCH):
                        bb = slice(b * SEQ, (b + 1) * SEQ)
                        dve.wait_ge(sums_loaded[b], 32)
                        t.settle(dve, nc.vector.reciprocal(den[:, bb], den[:, bb]))
                        for h in range(2):
                            r = slice(b * SEQ + h * CHUNK, b * SEQ + (h + 1) * CHUNK)
                            nc.vector.tensor_tensor(num[:, r], num[:, r], den[:, r], ALU.mult)\
                                .then_inc(s.oT, 1)
                else:
                    dve.wait_ge(s.nl0, 16)
                    dve.wait_ge(s.nl1, 16)
                    for ch in range(CHUNKS):
                        dve.sem_inc(s.oT, 1)
                for ch in range(CHUNKS):
                    dve.wait_ge(s.y, ch + 1)
                    r = slice(ch * CHUNK, (ch + 1) * CHUNK)
                    if double:
                        nc.vector.tensor_copy(xnT[:, r], ps[:, ch % 2, :]).then_inc(s.x, 1)
                    else:
                        nc.vector.tensor_tensor(x[:, r], x[:, r], ps[:, ch % 2, :], ALU.add)\
                            .then_inc(s.x, 1)
                if double:
                    xm = x.rearrange("p (m e d) -> p m e d", m=2, e=EXPERTS)
                    for e in range(EXPERTS):
                        dve.wait_ge(s.y, CHUNKS + e + 1)
                        nc.vector.scalar_tensor_tensor(
                            xm[:, :, e, :], ps[:, e % 2, 0:2 * P].rearrange("p (m d) -> p m d", m=2),
                            0.5, xm[:, :, e, :], ALU.mult, ALU.add).then_inc(s.x, 1)

            return dict(sync=sync, tensor=tensor, scalar=scalar, gpsimd=gpsimd, vector=vector, sems=s)

        wprs = sb("wprs", [P, 2, D])
        hid2 = sb("hid2", [P, 2 * FT * 2 * P])

        def ternary_mlp(tag):
            c = Carve()
            hh = c(2 * FF).rearrange("p (n f) -> p n f", n=2)
            hn = c(2 * FF).rearrange("p (n f) -> p n f", n=2)
            hT = c(2 * FF).rearrange("p (n f) -> p n f", n=2)
            st = c(2 * 6).rearrange("p (n f) -> p n f", n=2)
            m2 = c(2 * 2).rearrange("p (n f) -> p n f", n=2)
            v2 = c(2)
            r2 = c(2)
            s = sems(tag, "stats rstd xn tp xT vec pool up gel st2 r2 hn htp hT y x")

            def tensor(pe):
                def up(n):
                    if n >= 2:
                        pe.wait_ge(s.gel, n - 1)
                    nc.tensor.matmul(ps[:, 1 + n % 2, :], xnT[:, n * P:(n + 1) * P], w2fc[:, :],
                                     start=True, stop=True).then_inc(s.up, 1)

                def turn(n):
                    pe.wait_ge(s.hn, n + 1)
                    if n >= 2:
                        pe.wait_ge(s.hT, n - 1)
                    for f in range(FT):
                        last = nc.tensor.transpose(ps[:, 3 + n % 2, f * P:(f + 1) * P],
                                                   hn[:, n % 2, f * P:(f + 1) * P], ident[:, :])
                    last.then_inc(s.htp, 1)

                def down(n):
                    pe.wait_ge(s.hT, n + 1)
                    if n >= 2 * TPC:
                        pe.wait_ge(s.x, n // TPC - 1)
                    for f in range(FT):
                        last = nc.tensor.matmul(ps[:, 5 + n // TPC % 2, n % TPC * P:(n % TPC + 1) * P],
                                                hT[:, n % 2, f * P:(f + 1) * P], w2pj[:, f, :],
                                                start=f == 0, stop=f == FT - 1)
                    last.then_inc(s.y, 1)

                for ch in range(CHUNKS):
                    norm_tensor(pe, s, ch)
                pe.wait_ge(s.xT, CHUNKS)
                for n in range(TILES + 3):
                    if n < TILES:
                        up(n)
                    if 2 <= n < TILES + 2:
                        turn(n - 2)
                    if n >= 3:
                        down(n - 3)

            def scalar(act):
                for ch in range(CHUNKS):
                    act.wait_ge(s.tp, ch + 1)
                    nc.scalar.activation(xnT[:, ch * CHUNK:(ch + 1) * CHUNK], ps[:, TP, :], ACT.Copy)\
                        .then_inc(s.xT, 1)
                for n in range(TILES + 2):
                    if n < TILES:
                        act.wait_ge(s.up, n + 1)
                        if n >= 2:
                            act.wait_ge(s.hn, n - 1)
                        nc.scalar.activation(hh[:, n % 2, :], ps[:, 1 + n % 2, :], ACT.Gelu)\
                            .then_inc(s.gel, 1)
                    if n >= 2:
                        k = n - 2
                        act.wait_ge(s.htp, k + 1)
                        if k >= 2:
                            act.wait_ge(s.y, k - 1)
                        for f in range(FT):
                            last = nc.scalar.activation(hT[:, k % 2, f * P:(f + 1) * P],
                                                        ps[:, 3 + k % 2, f * P:(f + 1) * P],
                                                        ACT.Identity, bias=col("l2_b", f),
                                                        scale=col("l2_w", f))
                        last.then_inc(s.hT, 1)

            def gpsimd(pool):
                t = Tally(s.pool)
                for ch in range(CHUNKS):
                    norm_gpsimd(pool, s, t, ch)
                for n in range(TILES):
                    k = n % 2
                    pool.wait_ge(s.st2, n + 1)
                    t.settle(pool, nc.gpsimd.tensor_scalar(v2[:, k:k + 1], m2[:, k, 1:2], EPS, None,
                                                           ALU.add))
                    nc.gpsimd.tensor_tensor(r2[:, k:k + 1], v2[:, k:k + 1], neghalf[:, 0:1], ALU.pow)\
                        .then_inc(s.r2, 1)

            def vector(dve):
                t = Tally(s.vec)
                for ch in range(CHUNKS):
                    if ch:
                        dve.wait_ge(s.tp, ch)
                    last = norm_vector(dve, s, t,
                                       lambda n: x[:, ch * CHUNK + n * D:ch * CHUNK + (n + 1) * D],
                                       lambda n: xn[:, n, :], ch)
                    last.then_inc(s.xn, 1)
                for n in range(TILES + 1):
                    if n < TILES:
                        k = n % 2
                        dve.wait_ge(s.gel, n + 1)
                        t.settle(dve, nc.vector.bn_stats(st[:, k, :], hh[:, k, :]))
                        nc.vector.bn_aggr(m2[:, k, :], st[:, k, :]).then_inc(s.st2, 1)
                    if n:
                        k = (n - 1) % 2
                        dve.wait_ge(s.r2, n)
                        if n >= 3:
                            dve.wait_ge(s.htp, n - 2)
                        nc.vector.tensor_scalar(hn[:, k, :], hh[:, k, :], m2[:, k, 0:1], r2[:, k:k + 1],
                                                ALU.subtract, ALU.mult).then_inc(s.hn, 1)
                    if n >= TPC + 3 and (n - 3) % TPC == 0:
                        add(dve, (n - 3) // TPC - 1)
                add(dve, CHUNKS - 1)

            def add(dve, ch):
                dve.wait_ge(s.y, TPC * (ch + 1))
                r = slice(ch * CHUNK, (ch + 1) * CHUNK)
                nc.vector.scalar_tensor_tensor(x[:, r], ps[:, 5 + ch % 2, :], 0.5, x[:, r],
                                               ALU.mult, ALU.add).then_inc(s.x, 1)

            return dict(tensor=tensor, scalar=scalar, gpsimd=gpsimd, vector=vector, sems=s)

        def mlp_tensor(pe, s, w_in, w_out, b_row, hT):
            def up(ch):
                for f in range(FT):
                    if ch:
                        pe.wait_ge(s.gel, 4 * (ch - 1) + f + 1)
                    nc.tensor.matmul(ps[:, 1 + f, :], w_in[:, f * P:(f + 1) * P],
                                     xnT[:, ch * CHUNK:(ch + 1) * CHUNK], start=True, stop=True)\
                        .then_inc(s.up, 1)

            def down(ch):
                pe.wait_ge(s.gel, 4 * ch + 4)
                if ch >= 2:
                    pe.wait_ge(s.x, ch - 1)
                for n in range(TPC):
                    at = ps[:, 5 + ch % 2, n * P:(n + 1) * P]
                    for f in range(FT):
                        nc.tensor.matmul(at, hT[:, ch % 2, f, n * P:(n + 1) * P], w_out[:, f, :],
                                         start=f == 0, stop=False)
                    last = nc.tensor.matmul(at, ones[0:1, :], row(b_row), start=False, stop=True)
                last.then_inc(s.y, 1)

            for ch in range(CHUNKS + 1):
                if ch < CHUNKS:
                    norm_tensor(pe, s, ch)
                    pe.wait_ge(s.xT, ch + 1)
                    up(ch)
                if ch:
                    down(ch - 1)

        def mlp_gelu(act, s, hT, bias_name, ch):
            for f in range(FT):
                act.wait_ge(s.up, 4 * ch + f + 1)
                if ch >= 2:
                    act.wait_ge(s.y, ch - 1)
                nc.scalar.activation(hT[:, ch % 2, f, :], ps[:, 1 + f, :], ACT.Gelu,
                                     bias=col(bias_name, f)).then_inc(s.gel, 1)

        def binary_mlp(tag):
            c = Carve()
            hT = c(2 * FT * CHUNK).rearrange("p (n f t) -> p n f t", n=2, f=FT)
            s = sems(tag, "stats rstd xn tp xT vec pool up gel y x")

            def tensor(pe):
                mlp_tensor(pe, s, w3a, w3b, ROW_L3B2, hT)

            def scalar(act):
                for ch in range(CHUNKS):
                    act.wait_ge(s.tp, ch + 1)
                    nc.scalar.activation(xnT[:, ch * CHUNK:(ch + 1) * CHUNK], ps[:, TP, :], ACT.Copy)\
                        .then_inc(s.xT, 1)
                    mlp_gelu(act, s, hT, "l3w_b1", ch)

            def gpsimd(pool):
                t = Tally(s.pool)
                for ch in range(CHUNKS):
                    norm_gpsimd(pool, s, t, ch)

            def vector(dve):
                t = Tally(s.vec)
                for ch in range(CHUNKS + 1):
                    if ch < CHUNKS:
                        if ch:
                            dve.wait_ge(s.tp, ch)
                        last = norm_vector(dve, s, t,
                                           lambda n: x[:, ch * CHUNK + n * D:ch * CHUNK + (n + 1) * D],
                                           lambda n: xn[:, n, :], ch)
                        last.then_inc(s.xn, 1)
                    if ch:
                        dve.wait_ge(s.y, ch)
                        r = slice((ch - 1) * CHUNK, ch * CHUNK)
                        nc.vector.scalar_tensor_tensor(x[:, r], ps[:, 5 + (ch - 1) % 2, :], 0.5,
                                                       x[:, r], ALU.mult, ALU.add).then_inc(s.x, 1)

            return dict(tensor=tensor, scalar=scalar, gpsimd=gpsimd, vector=vector, sems=s)

        def lion(tag):
            c = Carve()
            wq, wk, wo, wd = (c(D) for _ in range(4))
            wv = c(8 * D).rearrange("p (e m) -> p e m", e=8)
            f1 = c(FF)
            f2 = c(FF).rearrange("p (f d) -> p f d", f=FT)
            sel = c(8 * P).rearrange("p (e m) -> p e m", e=8)
            same = c(P)
            phq = c(TOKENS)
            phk = c(TOKENS)
            lam = c(TOKENS)
            low = c(CHUNK)
            kv = c(2 * SEQ).rearrange("p (n t) -> p n t", n=2)
            fw = c(2 * SEQ).rearrange("p (n t) -> p n t", n=2)
            bw = c(2 * SEQ).rearrange("p (n t) -> p n t", n=2)
            oT = c(TOKENS)
            rowo = c(2 * D)
            hT = c(2 * FT * CHUNK).rearrange("p (n f t) -> p n f t", n=2, f=FT)
            s = sems(tag, "w stats rstd xn tp xT vec pool pj mn ex lin vps vr g gq acc oT y r up gel x "
                          "bz")

            def sync(sp):
                for dst, name in ((wq, "wq3"), (wk, "wk3"), (wv, "wv3"), (wo, "wo3"), (wd, "wd3"),
                                  (f1, "f13"), (f2, "f23"), (sel, "sel"), (same, "same")):
                    sp.dma_start(dst, a[name]).then_inc(s.w, 16)
                sp.dma_start(rowo[0:1, :], a["rows3"]).then_inc(s.w, 16)
            NW = 160

            def tensor(pe):
                pe.wait_ge(s.w, NW)
                for ch in range(CHUNKS):
                    norm_tensor(pe, s, ch)
                    pe.wait_ge(s.xT, ch + 1)
                    t = slice(ch * CHUNK, (ch + 1) * CHUNK)
                    for k, w in enumerate((wq, wk, wd)):
                        if ch:
                            pe.wait_ge(s.mn, 3 * (ch - 1) + k + 1)
                        nc.tensor.matmul(ps[:, 1 + k, :], w, xnT[:, t], start=True, stop=True)\
                            .then_inc(s.pj, 1)

                def value(n):
                    b, e = divmod(n, 8)
                    if n >= 2:
                        pe.wait_ge(s.vr, n - 1)
                    for h in range(2):
                        last = nc.tensor.matmul(ps[:, 2 * (n % 2) + h, :],
                                                wv[:, e, :],
                                                xnT[:, b * SEQ + h * CHUNK:b * SEQ + (h + 1) * CHUNK],
                                                start=True, stop=True)
                    last.then_inc(s.vps, 1)

                def gather(n):
                    b, e = divmod(n, 9)
                    pe.wait_ge(s.gq, n + 1)
                    if b and e == 0:
                        pe.wait_ge(s.oT, 1)
                    for h in range(2):
                        w = sel[:, e, :] if e < 8 else same
                        last = nc.tensor.matmul(ps[:, (4 if e < 8 else 6) + h, :], w,
                                                fw[:, n % 2, h * CHUNK:(h + 1) * CHUNK],
                                                start=e in (0, 8), stop=e in (7, 8),
                                                skip_group_check=True)
                    last.then_inc(s.acc, 1)

                pe.wait_ge(s.mn, 3 * CHUNKS)
                value(0)
                value(1)
                nv = 2
                for n in range(18):
                    gather(n)
                    if n % 9 < 8 and nv < 16:
                        value(nv)
                        nv += 1
                for ch in range(CHUNKS):
                    if ch % 2 == 0:
                        pe.wait_ge(s.oT, ch // 2 + 1)
                    if ch >= 2:
                        pe.wait_ge(s.r, ch - 1)
                    for n in range(TPC):
                        t = slice(ch * CHUNK + n * P, ch * CHUNK + (n + 1) * P)
                        at = ps[:, 2 + ch % 2, n * P:(n + 1) * P]
                        nc.tensor.matmul(at, oT[:, t], wo, start=True, stop=False)
                        last = nc.tensor.matmul(at, ones[0:1, :], rowo[0:1, 0:D], start=False, stop=True)
                    last.then_inc(s.y, 1)
                for ch in range(CHUNKS + 1):
                    if ch < CHUNKS:
                        norm_tensor(pe, s, CHUNKS + ch)
                        pe.wait_ge(s.xT, CHUNKS + ch + 1)
                        for f in range(FT):
                            if ch:
                                pe.wait_ge(s.gel, 4 * (ch - 1) + f + 1)
                            nc.tensor.matmul(ps[:, 1 + f, :], f1[:, f * P:(f + 1) * P],
                                             xnT[:, ch * CHUNK:(ch + 1) * CHUNK], start=True, stop=True)\
                                .then_inc(s.up, 1)
                    if ch:
                        k = ch - 1
                        pe.wait_ge(s.gel, 4 * k + 4)
                        if k >= 2:
                            pe.wait_ge(s.x, k - 1)
                        for n in range(TPC):
                            at = ps[:, 5 + k % 2, n * P:(n + 1) * P]
                            for f in range(FT):
                                nc.tensor.matmul(at, hT[:, k % 2, f, n * P:(n + 1) * P], f2[:, f, :],
                                                 start=f == 0, stop=False)
                            last = nc.tensor.matmul(at, ones[0:1, :], rowo[0:1, D:2 * D], start=False,
                                                    stop=True)
                        last.then_inc(s.y, 1)

            def scalar(act):
                for ch in range(CHUNKS):
                    act.wait_ge(s.tp, ch + 1)
                    t = slice(ch * CHUNK, (ch + 1) * CHUNK)
                    nc.scalar.activation(xnT[:, t], ps[:, TP, :], ACT.Identity, bias=col("l3_o1"),
                                         scale=col("l3_g1")).then_inc(s.xT, 1)
                    for k, dst in enumerate((phq, phk, lam)):
                        act.wait_ge(s.mn, 3 * ch + k + 1)
                        nc.scalar.activation(dst[:, t], dst[:, t], ACT.Exp,
                                             scale=-1.0 if k == 2 else 1.0).then_inc(s.ex, 1)
                for ch in range(CHUNKS):
                    act.wait_ge(s.tp, CHUNKS + ch + 1)
                    nc.scalar.activation(xnT[:, ch * CHUNK:(ch + 1) * CHUNK], ps[:, TP, :],
                                         ACT.Identity, bias=col("l3_o2"), scale=col("l3_g2"))\
                        .then_inc(s.xT, 1)
                    for f in range(FT):
                        act.wait_ge(s.up, 4 * ch + f + 1)
                        if ch >= 2:
                            act.wait_ge(s.y, CHUNKS + ch - 1)
                        nc.scalar.activation(hT[:, ch % 2, f, :], ps[:, 1 + f, :], ACT.Gelu,
                                             bias=col("l3_f1b", f)).then_inc(s.gel, 1)

            def gpsimd(pool):
                t = Tally(s.pool)
                for ch in range(2 * CHUNKS):
                    norm_gpsimd(pool, s, t, ch)
                for n in range(18):
                    pool.wait_ge(s.g, n + 1)
                    nc.gpsimd.tensor_tensor(fw[:, n % 2, :], fw[:, n % 2, :],
                                            phq[:, n // 9 * SEQ:(n // 9 + 1) * SEQ], ALU.mult)\
                        .then_inc(s.gq, 1)
                for ch in range(CHUNKS):
                    norm_gpsimd(pool, s, t, 2 * CHUNKS + ch)

            def vector(dve):
                t = Tally(s.vec)
                for ch in range(CHUNKS):
                    t0 = ch * CHUNK
                    tt = slice(t0, t0 + CHUNK)

                    def kept(n):
                        return res[:, t0 + n * D:t0 + (n + 1) * D]

                    if ch:
                        dve.wait_ge(s.tp, ch)
                    t.settle(dve, norm_vector(dve, s, t, lambda n: x[:, t0 + n * D:t0 + (n + 1) * D],
                                              kept, 2 * ch))
                    norm_vector(dve, s, t, kept, lambda n: xn[:, n, :], 2 * ch + 1).then_inc(s.xn, 1)
                    for k, (dst, b) in enumerate(((phq, "l3_qb"), (phk, "l3_kb"), (lam, "l3_db"))):
                        dve.wait_ge(s.pj, 3 * ch + k + 1)
                        src = ps[:, 1 + k, :]
                        if k < 2:
                            if ch or k:
                                t.settle(dve, nc.vector.tensor_scalar(low, src, col(b), 0.0, ALU.add,
                                                                      ALU.max))
                            else:
                                t.settle(dve, nc.vector.tensor_scalar(low, src, col(b), 0.0, ALU.add,
                                                                      ALU.max))
                            nc.vector.tensor_scalar(dst[:, tt], src, col(b), 0.0, ALU.add, ALU.min)\
                                .then_inc(s.mn, 1)
                            dve.wait_ge(s.ex, 3 * ch + k + 1)
                            t.settle(dve, nc.vector.tensor_tensor(dst[:, tt], dst[:, tt], low, ALU.add))
                        else:
                            nc.vector.tensor_scalar(dst[:, tt], src, col(b), None, ALU.add)\
                                .then_inc(s.mn, 1)
                            dve.wait_ge(s.ex, 3 * ch + k + 1)
                            t.settle(dve, nc.vector.tensor_scalar(dst[:, tt], dst[:, tt], 1.0, None,
                                                                  ALU.add))
                            t.settle(dve, nc.vector.reciprocal(dst[:, tt], dst[:, tt]))
                            t.settle(dve, nc.vector.tensor_scalar(dst[:, tt], dst[:, tt], 1e-8, None,
                                                                  ALU.max))
                nc.vector.memset(bw[:, 0, SEQ - 1:SEQ], 0.0)
                t.settle(dve, nc.vector.memset(bw[:, 1, SEQ - 1:SEQ], 0.0))
                for n in range(18):
                    b, e = divmod(n, 9)
                    k = n % 2
                    bb = slice(b * SEQ, (b + 1) * SEQ)
                    if e < 8:
                        v = 8 * b + e
                        dve.wait_ge(s.vps, v + 1)
                        nc.vector.scalar_tensor_tensor(
                            kv[:, k, :],
                            ps[:, 2 * (v % 2):2 * (v % 2) + 2, :].rearrange("p b t -> p (b t)"),
                            col("l3_vb", e), phk[:, bb], ALU.add, ALU.mult).then_inc(s.vr, 1)
                        dve.wait_ge(s.vr, v + 1)
                    else:
                        t.settle(dve, nc.vector.tensor_copy(kv[:, k, :], phk[:, bb]))
                    if n >= 2:
                        dve.wait_ge(s.acc, n - 1)
                    nc.vector.tensor_tensor_scan(fw[:, k, :], lam[:, bb], kv[:, k, :], 0.0,
                                                 ALU.mult, ALU.add)
                    t.settle(dve, nc.vector.tensor_tensor_scan(
                        bw[:, k, 0:SEQ - 1][:, ::-1], kv[:, k, 1:SEQ][:, ::-1],
                        lam[:, b * SEQ + 1:(b + 1) * SEQ][:, ::-1], 0.0, ALU.add, ALU.mult))
                    nc.vector.tensor_tensor(fw[:, k, :], fw[:, k, :], bw[:, k, :], ALU.add)\
                        .then_inc(s.g, 1)
                    if e == 8:
                        dve.wait_ge(s.acc, n + 1)
                        dn = ps[:, 6:8, :].rearrange("p b t -> p (b t)")
                        t.settle(dve, nc.vector.tensor_scalar(oT[:, bb], dn, 1e-6, None, ALU.max))
                        t.settle(dve, nc.vector.reciprocal(oT[:, bb], oT[:, bb]))
                        nc.vector.tensor_tensor(oT[:, bb], oT[:, bb],
                                                ps[:, 4:6, :].rearrange("p b t -> p (b t)"),
                                                ALU.mult).then_inc(s.oT, 1)
                for ch in range(CHUNKS):
                    r = slice(ch * CHUNK, (ch + 1) * CHUNK)
                    dve.wait_ge(s.y, ch + 1)
                    nc.vector.tensor_tensor(res[:, r], res[:, r], ps[:, 2 + ch % 2, :], ALU.add)\
                        .then_inc(s.r, 1)
                dve.wait_ge(s.r, CHUNKS)
                for ch in range(CHUNKS):
                    r = slice(ch * CHUNK, (ch + 1) * CHUNK)
                    last = nc.vector.tensor_tensor(x[:, r], x[:, r], res[:, r], ALU.add)
                t.settle(dve, last)
                for ch in range(CHUNKS + 1):
                    if ch < CHUNKS:
                        dve.wait_ge(s.tp, CHUNKS + ch)
                        norm_vector(dve, s, t,
                                    lambda n: res[:, ch * CHUNK + n * D:ch * CHUNK + (n + 1) * D],
                                    lambda n: xn[:, n, :], 2 * CHUNKS + ch).then_inc(s.xn, 1)
                    if ch:
                        k = ch - 1
                        dve.wait_ge(s.y, CHUNKS + k + 1)
                        r = slice(k * CHUNK, (k + 1) * CHUNK)
                        nc.vector.tensor_tensor(x[:, r], x[:, r], ps[:, 5 + k % 2, :], ALU.add)\
                            .then_inc(s.x, 1)

            return dict(sync=sync, tensor=tensor, scalar=scalar, gpsimd=gpsimd, vector=vector, sems=s)

        cw = Carve()
        raw_fc, raw_pj, raw_a, raw_b = (cw(FF) for _ in range(4))
        tmp_v, tmp_s = cw(FF), cw(FF)
        gam = cw(8)

        def boot_sync(sp):
            for dst, name in ((x, "x"), (ident, "ident"), (masks, "masks"), (lower, "lower"),
                              (cols[:, 0:n_cols - 4], "cols"), (rows[0:1, :], "rows"), (raw_fc, "fc2"),
                              (raw_pj, "pj2"), (raw_a, "w13"), (raw_b, "w23")):
                sp.dma_start(dst, a[name]).then_inc(boot.const, 16)
        NBOOT = 160

        def boot_gpsimd(pool):
            pool.wait_ge(boot.bw, 1)

        def boot_tensor(pe):
            pe.wait_ge(boot.gabs, 1)
            nc.tensor.matmul(ps[:, 0, 0:2], ones[:, :], gam[:, 0:2], start=True, stop=True)\
                .then_inc(boot.gsum, 1)
            pe.wait_ge(boot.gabs, 2)
            nc.tensor.matmul(ps[:, 1, :], ones[:, :], tmp_v, start=True, stop=True)\
                .then_inc(boot.gsum, 1)
            pe.wait_ge(boot.gabs, 3)
            for f in range(FT):
                last = nc.tensor.matmul(ps[:, 2, 0:D], ones[:, :], tmp_v[:, f * D:(f + 1) * D],
                                        start=f == 0, stop=f == FT - 1)
            last.then_inc(boot.gsum, 1)

        def boot_scalar(act):
            act.wait_ge(boot.const, NBOOT)
            nc.scalar.activation(w3a[:, :], raw_a, ACT.Sign).then_inc(boot.bsign, 1)
            nc.scalar.activation(w3b.rearrange("p f d -> p (f d)"), raw_b, ACT.Sign)\
                .then_inc(boot.bsign, 1)

        def boot_vector(dve):
            t = Tally(boot.vec)
            dve.wait_ge(boot.const, NBOOT)
            nc.vector.memset(ones[:, :], 1.0)
            nc.vector.tensor_copy(identb[:, :], ident[:, :])
            nc.vector.tensor_copy(maskb.rearrange("p n t -> p (n t)"),
                                  masks[:, 0:2, :].rearrange("p n t -> p (n t)"))
            for k, src in enumerate((raw_fc, raw_pj)):
                t.settle(dve, nc.vector.scalar_tensor_tensor(tmp_s, src, -1.0, src, ALU.mult, ALU.max))
                last = nc.vector.tensor_reduce(gam[:, k:k + 1], tmp_s, AXX, ALU.add)
                if k == 0:
                    t.settle(dve, last)
            last.then_inc(boot.gabs, 1)
            dve.wait_ge(boot.gsum, 1)
            t.settle(dve, nc.vector.tensor_scalar(gam[:, 2:4], ps[:, 0, 0:2], 1.0 / (D * FF), 1e-6,
                                                  ALU.mult, ALU.add))
            t.settle(dve, nc.vector.tensor_scalar(gam[:, 2:4], gam[:, 2:4], 0.5, None, ALU.mult))
            t.settle(dve, nc.vector.tensor_scalar(gam[:, 4:6], gam[:, 2:4], -1.0, None, ALU.mult))
            for k, (src, dst) in enumerate(((raw_fc, w2fc[:, :]),
                                            (raw_pj, w2pj.rearrange("p f d -> p (f d)")))):
                t.settle(dve, nc.vector.tensor_scalar(tmp_s, src, gam[:, 4 + k:5 + k], None,
                                                      ALU.is_lt))
                t.settle(dve, nc.vector.scalar_tensor_tensor(dst, src, gam[:, 2 + k:3 + k], tmp_s,
                                                             ALU.is_gt, ALU.subtract))
            nc.vector.scalar_tensor_tensor(tmp_v, raw_a, -1.0, raw_a, ALU.mult, ALU.max)\
                .then_inc(boot.gabs, 1)
            dve.wait_ge(boot.gsum, 2)
            dve.wait_ge(boot.bsign, 2)

            def binarise(dst, alpha, src, k):
                t.settle(dve, nc.vector.scalar_tensor_tensor(dst, alpha, k, dst, ALU.mult, ALU.mult))
                t.settle(dve, nc.vector.tensor_tensor(dst, dst, src, ALU.subtract))
                t.settle(dve, nc.vector.tensor_tensor(dst, dst, src, ALU.add))

            binarise(w3a[:, :], ps[:, 1, :], raw_a, 1.0 / D)
            nc.vector.scalar_tensor_tensor(tmp_v, raw_b, -1.0, raw_b, ALU.mult, ALU.max)\
                .then_inc(boot.gabs, 1)
            dve.wait_ge(boot.gsum, 3)
            for f in range(FT):
                binarise(w3b[:, f, :], ps[:, 2, 0:D], raw_b[:, f * D:(f + 1) * D], 1.0 / FF)

            nc.vector.memset(neghalf[:, :], -0.5).then_inc(boot.bw, 1)

        ROOT8 = 1.0 / 8.0 ** 0.5
        softmax1 = ["wqf", "wkf", "wvf", "wof"]
        layers = [
            (moe, ("m0",)),
            (attention, ("a0", 8, "linear", "r0", 1.0, ["wq0", "wk0", "wv0"], False, False)),
            (moe, ("m1",)),
            (attention, ("f1", 4, "full", None, 0.5, softmax1, True, True)),
            (attention, ("a1", 8, "causal", "r1", ROOT8, ["wq1", "wk1", "wv1", "wo1"], True, False)),
            (attention, ("f2", 4, "full", None, 0.5, softmax1, True, True)),
            (ternary_mlp, ("t1",)),
            (attention, ("a2", 8, "causal", "r2", ROOT8, ["wq2", "wk2", "wv2", "wo2"], True, False)),
            (ternary_mlp, ("t2",)),
            (binary_mlp, ("b1",)),
            (lion, ("l3",)),
            (binary_mlp, ("b2",)),
        ]

        last_sems = sems("final", "out")

        def finish_sync(sp):
            sp.dma_start(out.rearrange("(n p) d -> p n d", p=P),
                         x.rearrange("p (n d) -> p n d", d=D)).then_inc(last_sems.out, 16)
            sp.wait_ge(last_sems.out, 16)

        def run(part):
            with nc.Block() as block:
                if "sync" in part:
                    block.sync(part["sync"])
                if "tensor" in part:
                    block.tensor(part["tensor"])
                if "scalar" in part:
                    block.scalar(part["scalar"])
                if "gpsimd" in part:
                    block.gpsimd(part["gpsimd"])
                if "vector" in part:
                    block.vector(part["vector"])
            nc.clear_and_free_semaphores(list(part["sems"]))
            nc.all_engine_barrier()

        run(dict(sync=boot_sync, tensor=boot_tensor, scalar=boot_scalar, vector=boot_vector,
                 sems=boot))
        for make, args in layers:
            run(make(*args))
        run(dict(sync=finish_sync, sems=last_sems))




def _layout(i):
    import numpy as np
    f = np.float32
    c = np.ascontiguousarray
    T = lambda w: c(np.asarray(w).T)
    o = {}
    o["x"] = c(np.asarray(i["L0_attn_x"]).reshape(TILES, P, D).transpose(1, 0, 2)).reshape(P, TILES * D)
    o["ident"] = np.eye(P, dtype=f)
    r, q = np.arange(P)[:, None], np.arange(P)[None, :]
    big = f(-1e30)
    o["masks"] = c(np.stack([np.where(q > r, big, f(0)), np.where(q < r, big, f(0)),
                             np.where(q >= r, f(1), f(0))], 1).astype(f))
    e = np.arange(EXPERTS)
    o["lower"] = np.tile((e[None, :] < e[:, None]).astype(f).reshape(1, -1), (P, 1))

    gu = np.asarray(i["L0_ffn_experts_gate_up"])
    dn = np.asarray(i["L0_ffn_experts_down"])
    sg, su, sd = (np.asarray(i["L0_ffn_shared_" + n + "_w"]) for n in ("gate", "up", "down"))
    G = [gu[k, :INTER] for k in range(EXPERTS)] + [sg[:INTER], sg[INTER:]]
    U = [gu[k, INTER:] for k in range(EXPERTS)] + [su[:INTER], su[INTER:]]
    Dn = [dn[k] for k in range(EXPERTS)] + [sd[:, :INTER], sd[:, INTER:]]
    up = np.zeros((UPS_, P, D), f)
    down = np.zeros((P, PAIRS * 3, D), f)
    for p in range(PAIRS):
        for h in range(2):
            w = 2 * p + h
            up[6 * p + 2 * h] = G[w][:P]
            up[6 * p + 2 * h + 1] = U[w][:P]
            up[6 * p + 4, 64 * h:64 * h + TAIL] = G[w][P:]
            up[6 * p + 5, 64 * h:64 * h + TAIL] = U[w][P:]
            down[:, 3 * p + h] = Dn[w][:, :P].T
            down[64 * h:64 * h + TAIL, 3 * p + 2] = Dn[w][:, P:].T
    o["up0"] = c(up.transpose(2, 0, 1)).reshape(D, UPS_ * P)
    o["down0"] = c(down).reshape(P, PAIRS * 3 * D)
    o["gate0"] = c(np.concatenate([np.asarray(i["L0_ffn_gate_w"]),
                                   np.asarray(i["L0_ffn_shared_expert_gate_w"])], 0).T)

    hd = 8
    feat = np.arange(D)
    inv = (f(1.0) / f(10000.0) ** (np.arange(0, hd, 2, dtype=f) / f(hd))).astype(f)
    ang = (np.arange(SEQ, dtype=f)[:, None] * inv[None, :]).astype(f)
    cos, sin = np.cos(ang).T.astype(f), np.sin(ang).T.astype(f)
    half_perm = feat // hd * hd + (feat % hd + hd // 2) % hd
    pair_perm = feat ^ 1
    sgn_half = np.where(feat % hd < hd // 2, f(-1), f(1))[:, None]
    sgn_pair = np.where(feat % 2 == 0, f(-1), f(1))[:, None]
    o["r0_tab"] = c(np.stack([cos[feat % (hd // 2)], sin[feat % (hd // 2)] * sgn_half], 1).astype(f))
    pair_tab = c(np.stack([cos[feat % hd // 2], sin[feat % hd // 2] * sgn_pair], 1).astype(f))
    o["r1_tab"] = o["r2_tab"] = pair_tab
    wqkv, bqkv = np.asarray(i["L0_attn_W_qkv"]), np.asarray(i["L0_attn_b_qkv"])
    o["wq0"], o["wk0"], o["wv0"] = (T(wqkv[k * D:(k + 1) * D]) for k in range(3))
    o["r0_wqs"], o["r0_wks"] = c(o["wq0"][:, half_perm]), c(o["wk0"][:, half_perm])
    for n in "qkvo":
        o[f"w{n}1"] = c(np.asarray(i["L1_attn_w" + n]))
        o[f"w{n}f"] = c(np.asarray(i["L1_ffn_w" + n]))
        o[f"w{n}2"] = T(i["L2_attn_W" + n])
        o[f"w{n}3"] = c(np.asarray(i[f"L3_attn_{n}_w"]))
    for k in "12":
        o[f"r{k}_wqs"], o[f"r{k}_wks"] = c(o["wq" + k][:, pair_perm]), c(o["wk" + k][:, pair_perm])

    o["w1_1"] = c(np.asarray(i["L1_ffn_w1"]).transpose(1, 0, 2)).reshape(D, EXPERTS * FF)
    o["w2_1"] = c(np.asarray(i["L1_ffn_w2"]).reshape(EXPERTS, FT, P, D).transpose(2, 0, 1, 3))\
        .reshape(P, EXPERTS * FT * D)
    o["fc2"] = T(i["L2_ffn_W_fc"])
    o["pj2"] = c(np.asarray(i["L2_ffn_W_proj"]).T.reshape(FT, P, D).transpose(1, 0, 2)).reshape(P, FF)
    o["w13"] = T(i["L3_ffn_w1"])
    o["w23"] = c(np.asarray(i["L3_ffn_w2"]).T.reshape(FT, P, D).transpose(1, 0, 2)).reshape(P, FF)
    o["wd3"] = c(np.asarray(i["L3_attn_dec_w"])[:, feat // hd])
    o["wv3"] = c(np.stack([o["wv3"][:, feat // hd * hd + k] for k in range(hd)], 1))
    o["f13"] = c(np.asarray(i["L3_attn_f1_w"]))
    o["f23"] = c(np.asarray(i["L3_attn_f2_w"]).reshape(FT, P, D).transpose(1, 0, 2))
    o["rows3"] = np.concatenate([np.asarray(i["L3_attn_o_b"]), np.asarray(i["L3_attn_f2_b"])])[None]
    h_of, e_of = feat // hd, feat % hd
    same = (h_of[:, None] == h_of[None, :]).astype(f)
    o["same"] = same
    o["sel"] = c(np.stack([same * (e_of == k)[None, :].astype(f) for k in range(8)], 1))

    b = {"b_q": bqkv[:D], "b_qs": bqkv[:D][half_perm], "b_k": bqkv[D:2 * D],
         "b_ks": bqkv[D:2 * D][half_perm], "ln_g": i["L1_ffn_ln_g"], "ln_b": i["L1_ffn_ln_b"]}
    parts = [np.asarray(b[n]).reshape(P, 1) for n in ("b_q", "b_qs", "b_k", "b_ks", "ln_g", "ln_b")]
    parts.append(np.asarray(i["L1_ffn_b1"]).reshape(EXPERTS * FT, P).T)
    for n in ("L3_ffn_b1", "L2_ffn_ln_w", "L2_ffn_ln_b", "L3_attn_f1_b"):
        parts.append(np.asarray(i[n]).reshape(FT, P).T)
    parts += [np.asarray(i[f"L3_attn_{n}_b"]).reshape(P, 1) for n in "qk"]
    parts.append(np.repeat(np.asarray(i["L3_attn_dec_b"]), 8).reshape(P, 1))
    parts.append(np.repeat(np.asarray(i["L3_attn_v_b"]).reshape(16, 8), 8, 0))
    parts += [np.asarray(i["L3_attn_ln" + n]).reshape(P, 1) for n in ("1_w", "1_b", "2_w", "2_b")]
    o["cols"] = c(np.concatenate(parts, 1).astype(f))
    o["rows"] = c(np.concatenate([np.asarray(i["L1_ffn_b2"]).reshape(-1), np.asarray(i["L3_ffn_b2"]),
                                  bqkv[2 * D:]])[None])
    return o


UPS_ = 6 * PAIRS


def kernel(**inputs):
    import numpy as _np
    import concourse.bacc as _bacc
    from concourse.bass_utils import run_bass_kernel_spmd as _run

    nc = _bacc.Bacc("TRN2", target_bir_lowering=False, num_devices=1)
    arrays, aps = {}, {}
    for name, v in _layout(inputs).items():
        v = _np.ascontiguousarray(v)
        arrays["in_" + name] = v
        aps[name] = nc.dram_tensor("in_" + name, v.shape, mybir.dt.from_np(v.dtype),
                                   kind="ExternalInput").ap()
    out = nc.dram_tensor("out_x", (TOKENS, D), F32, kind="ExternalOutput").ap()
    macaron(nc, aps, out)
    r = _run(nc, [arrays], core_ids=[0])
    return r.results[0]["out_x"].reshape(BATCH, SEQ, D)
```

```python
import struct
from collections import namedtuple
from contextlib import ExitStack

import concourse.bass as bass
from concourse import mybir

F32 = mybir.dt.float32
BF16 = mybir.dt.bfloat16
ACT = mybir.ActivationFunctionType
ALU = mybir.AluOpType
AXX = mybir.AxisListType.X

P = 128
D = 128
BATCH, SEQ = 2, 1024
TOKENS = BATCH * SEQ
TILES = TOKENS // P
CHUNK = 512
CHUNKS = TOKENS // CHUNK
TPC = CHUNK // P
KB = SEQ // P
EPS = 1e-5
GROUP = 4

EXPERTS, INTER = 8, 176
WAYS = EXPERTS + 2
PAIRS = WAYS // 2
TAIL = INTER - P
FF = 512
FT = FF // P

TP = 0

MINUS_ONES = struct.unpack("<f", bytes([0x80, 0xBF, 0x80, 0xBF]))[0]


class Tally:

    def __init__(self, sem, base=0):
        self.sem, self.base, self.n = sem, base, 0

    def done(self, ins):
        ins.then_inc(self.sem, 1)
        self.n += 1

    def settle(self, eng, ins):
        self.done(ins)
        eng.wait_ge(self.sem, self.base + self.n)


def Sems(nc, tag, names):
    names = names.split()
    return namedtuple("Sems", names)(*[nc.alloc_semaphore(name=f"{tag}_{n}") for n in names])


def macaron(nc, a, out):
    with ExitStack() as ctx:
        def sb(name, shape, dt=F32):
            return ctx.enter_context(nc.sbuf_tensor(name, shape, dt))[tuple([slice(None)] * len(shape))]

        def dram(name, shape, dt=F32):
            return nc.dram_tensor(name, shape, dt, kind="Internal").ap()

        def sems(tag, names):
            return Sems(nc, tag, names)

        ps = ctx.enter_context(nc.psum_tensor("ps", [P, 8, 512], F32))[:, :, :]

        x = sb("x", [P, TILES * D])
        xnT = sb("xnT", [P, TOKENS])
        res = sb("res", [P, TILES * D])
        xn = sb("xn", [P, 2, TPC, D])
        stat = sb("stat", [P, CHUNKS, TPC, 6])
        mv = sb("mv", [P, CHUNKS, TPC, 2])
        var = sb("var", [P, CHUNKS, TPC])
        rstd = sb("rstd", [P, CHUNKS, TPC])
        neghalf = sb("neghalf", [P, TPC])

        ident = sb("ident", [P, P])
        identb = sb("identb", [P, P], BF16)
        masks = sb("masks", [P, 3, P])
        maskb = sb("maskb", [P, 2, P], BF16)
        ones = sb("ones", [P, P])
        lower = sb("lower", [P, EXPERTS * EXPERTS])
        cols = sb("cols", [P, 96])
        rows = sb("rows", [1, 10 * D])

        w2fc = sb("w2fc", [P, FF])
        w2pj = sb("w2pj", [P, FT, D])
        w3a = sb("w3a", [P, FF])
        w3b = sb("w3b", [P, FT, D])
        wproj = sb("wproj", [P, 4, D])

        ARENA = 31 * 1024
        arena = sb("arena", [P, ARENA])

        class Carve:
            def __init__(self):
                self.at = 0

            def __call__(self, n, dt=F32):
                words = n if dt == F32 else n // 2
                view = arena[:, self.at:self.at + words]
                self.at += words
                assert self.at <= ARENA, self.at
                return view if dt == F32 else view.bitcast(dt)

        names = ["b_q", "b_qs", "b_k", "b_ks", "ln_g", "ln_b"]
        col_at = {n: i for i, n in enumerate(names)}
        n_cols = len(names)
        for n, k in (("b_v", 0), ("b1_l1", EXPERTS * FT), ("l3w_b1", FT), ("l2_w", FT), ("l2_b", FT),
                     ("l3_f1b", FT), ("l3_qb", 1), ("l3_kb", 1), ("l3_db", 1), ("l3_vb", 8),
                     ("l3_g1", 1), ("l3_o1", 1), ("l3_g2", 1), ("l3_o2", 1), ("scr", 4)):
            col_at[n] = n_cols
            n_cols += k
        assert n_cols <= 96, n_cols

        def col(name, k=0):
            return cols[:, col_at[name] + k:col_at[name] + k + 1]

        def row(k):
            return rows[0:1, k * D:(k + 1) * D]

        ROW_B2, ROW_L3B2 = 0, 8

        boot = sems("boot", "const cols zero ones gsum gabs gcol quant bsign bsum bw vec pool")
        COLS_SHARED = ["ln_g", "ln_b", "b1_l1", "l3w_b1", "l2_w", "l2_b", "l3_f1b", "l3_qb", "l3_kb",
                       "l3_db", "l3_vb", "l3_g1", "l3_o1", "l3_g2", "l3_o2"]

        def norm_stats(dve, s, t, src, g):
            b = g % CHUNKS
            for n in range(TPC):
                last = nc.vector.bn_stats(stat[:, b, n, :], src(n))
            t.settle(dve, last)
            for n in range(TPC):
                last = nc.vector.bn_aggr(mv[:, b, n, :], stat[:, b, n, :])
            last.then_inc(s.stats, 1)

        def norm_apply(dve, s, src, dst, g):
            b = g % CHUNKS
            dve.wait_ge(s.rstd, g + 1)
            for n in range(TPC):
                last = nc.vector.tensor_scalar(dst(n), src(n), mv[:, b, n, 0:1],
                                               rstd[:, b, n:n + 1], ALU.subtract, ALU.mult)
            return last

        def norm_chunk(dve, s, t, rows_of, ch, g0=0, k0=0):
            if ch == 0:
                norm_stats(dve, s, t, rows_of(0), g0)
            if ch + 1 < CHUNKS:
                norm_stats(dve, s, t, rows_of(ch + 1), g0 + ch + 1)
            k = k0 + ch
            if k >= 2:
                dve.wait_ge(s.tp, k - 1)
            norm_apply(dve, s, rows_of(ch), lambda n: xn[:, k % 2, n, :], g0 + ch).then_inc(s.xn, 1)

        def norm_twice(dve, s, t, ch):
            if ch == 0:
                norm_stats(dve, s, t, x_rows(0), 0)
            t.settle(dve, norm_apply(dve, s, x_rows(ch), res_rows(ch), 2 * ch))
            norm_stats(dve, s, t, res_rows(ch), 2 * ch + 1)
            if ch + 1 < CHUNKS:
                norm_stats(dve, s, t, x_rows(ch + 1), 2 * ch + 2)
            if ch >= 2:
                dve.wait_ge(s.tp, ch - 1)
            norm_apply(dve, s, res_rows(ch), lambda n: xn[:, ch % 2, n, :], 2 * ch + 1)\
                .then_inc(s.xn, 1)

        def x_rows(ch):
            return lambda n: x[:, ch * CHUNK + n * D:ch * CHUNK + (n + 1) * D]

        def res_rows(ch):
            return lambda n: res[:, ch * CHUNK + n * D:ch * CHUNK + (n + 1) * D]

        def norm_gpsimd(pool, s, t, g):
            b = g % CHUNKS
            pool.wait_ge(s.stats, g + 1)
            t.settle(pool, nc.gpsimd.tensor_scalar(var[:, b, :], mv[:, b, :, 1], EPS, None, ALU.add))
            nc.gpsimd.tensor_tensor(rstd[:, b, :], var[:, b, :], neghalf[:, :], ALU.pow)\
                .then_inc(s.rstd, 1)

        def norm_tensor(pe, s, k):
            pe.wait_ge(s.xn, k + 1)
            if k:
                pe.wait_ge(s.xT, k)
            for n in range(TPC):
                last = nc.tensor.transpose(ps[:, TP, n * P:(n + 1) * P], xn[:, k % 2, n, :],
                                           ident[:, :])
            last.then_inc(s.tp, 1)

        UPS = 6 * PAIRS
        ALL_PAIRS = CHUNKS * PAIRS
        RING, FIRST_UP, FIRST_Y = 5, 1, 6
        GATE = 7

        def moe(tag):
            c = Carve()
            up_w = c(UPS * P)
            dn_w = c(PAIRS * 3 * D)
            gate_w = c(EXPERTS + 1)
            hid = c(6 * CHUNK).rearrange("p (n t) -> p n t", n=6)
            sg = c(3 * CHUNK).rearrange("p (n t) -> p n t", n=3)
            gT = c(TOKENS)
            lg = c(TILES * 9).rearrange("p (n e) -> p n e", e=9)
            ex = c(TILES * 9).rearrange("p (n e) -> p n e", e=9)
            mx = c(TILES)
            den = c(TILES)
            cmp = c(TILES * 64).rearrange("p (n e f) -> p n e f", e=8, f=8)
            eq = c(TILES * 64).rearrange("p (n e f) -> p n e f", e=8, f=8)
            rank = c(TILES * 8).rearrange("p (n e) -> p n e", e=8)
            wts = c(TILES * WAYS).rearrange("p (n e) -> p n e", e=WAYS)
            s = sems(tag, "wg wu wd stats rstd xn tp xT vec pool gmm gcopy gtp shift gexp up silu h y "
                          "yused")

            def sync(sp):
                sp.dma_start(gate_w, a["gate0"]).then_inc(s.wg, 16)
                sp.dma_start(up_w, a["up0"]).then_inc(s.wu, 16)
                sp.dma_start(dn_w, a["down0"]).then_inc(s.wd, 16)

            def tensor(pe):
                def up(q, first, end):
                    ch = q // PAIRS
                    for k in range(first, end):
                        tile = 6 * q + k
                        before = tile - RING
                        if before >= 0 and before % 2 == 0:
                            pe.wait_ge(s.silu, before // 2 + 1)
                        elif before >= 0:
                            pe.wait_ge(s.h, before // 2 + 1)
                        w = (q % PAIRS * 6 + k) * P
                        nc.tensor.matmul(ps[:, FIRST_UP + tile % RING, :], up_w[:, w:w + P],
                                         xnT[:, ch * CHUNK:(ch + 1) * CHUNK], start=True, stop=True)\
                            .then_inc(s.up, 1)

                def down(q):
                    p = q % PAIRS
                    pe.wait_ge(s.h, 3 * q + 3)
                    if q == 0:
                        pe.wait_ge(s.shift, 1)
                    for half in range(2):
                        if q:
                            pe.wait_ge(s.yused, 2 * (q - 1) + half + 1)
                        bank = FIRST_Y + half
                        r = slice(64 * half, 64 * half + 64)
                        for n in range(TPC):
                            t = slice(n * P, (n + 1) * P)
                            nc.tensor.matmul(ps[:, bank, t], hid[:, 3 * (q % 2) + half, t],
                                             dn_w[:, (3 * p + half) * D:(3 * p + half + 1) * D],
                                             start=True, stop=False)
                            last = nc.tensor.matmul(ps[:, bank, t], hid[r, 3 * (q % 2) + 2, t],
                                                    dn_w[r, (3 * p + 2) * D:(3 * p + 3) * D],
                                                    start=False, stop=True)
                        last.then_inc(s.y, 1)

                pe.wait_ge(s.wg, 16)
                for ch in range(CHUNKS):
                    norm_tensor(pe, s, ch)
                    pe.wait_ge(s.xT, ch + 1)
                    if ch:
                        pe.wait_ge(s.gcopy, ch)
                    nc.tensor.matmul(ps[0:9, GATE, :], gate_w, xnT[:, ch * CHUNK:(ch + 1) * CHUNK],
                                     start=True, stop=True).then_inc(s.gmm, 1)
                    if ch == 0:
                        pe.wait_ge(s.wu, 16)
                    if ch < 2:
                        up(0, 2 * ch, 2 * ch + 2)
                for ch in range(CHUNKS):
                    pe.wait_ge(s.gcopy, ch + 1)
                    for n in range(ch * TPC, (ch + 1) * TPC):
                        last = nc.tensor.transpose(ps[:, FIRST_Y, n * 16:n * 16 + 9],
                                                   gT[0:9, n * P:(n + 1) * P], ident[0:9, 0:9])
                last.then_inc(s.gtp, 1)
                up(0, 4, 6)
                pe.wait_ge(s.wd, 16)
                for q in range(ALL_PAIRS):
                    if q + 1 < ALL_PAIRS:
                        up(q + 1, 0, 6)
                    down(q)

            def scalar(act):
                for ch in range(CHUNKS):
                    t = slice(ch * CHUNK, (ch + 1) * CHUNK)
                    act.wait_ge(s.tp, ch + 1)
                    nc.scalar.activation(xnT[:, t], ps[:, TP, :], ACT.Copy).then_inc(s.xT, 1)
                    act.wait_ge(s.gmm, ch + 1)
                    nc.scalar.activation(gT[0:9, t], ps[0:9, GATE, :], ACT.Copy).then_inc(s.gcopy, 1)
                act.wait_ge(s.shift, 1)
                nc.scalar.activation(ex, lg, ACT.Exp).then_inc(s.gexp, 1)
                for n in range(3 * ALL_PAIRS):
                    act.wait_ge(s.up, 2 * n + 1)
                    if n >= 3:
                        act.wait_ge(s.h, n - 2)
                    nc.scalar.activation(sg[:, n % 3, :], ps[:, FIRST_UP + (2 * n) % RING, :],
                                         ACT.Silu).then_inc(s.silu, 1)

            def gpsimd(pool):
                t = Tally(s.pool)
                for ch in range(CHUNKS):
                    norm_gpsimd(pool, s, t, ch)

            def vector(dve):
                t = Tally(s.vec)
                for ch in range(CHUNKS):
                    norm_chunk(dve, s, t, x_rows, ch)
                dve.wait_ge(s.gtp, 1)
                zp = ps[:, FIRST_Y, 0:TILES * 16].rearrange("p (n e) -> p n e", e=16)
                nc.vector.tensor_reduce(mx, zp[:, :, 0:8], AXX, ALU.max)
                t.settle(dve, nc.vector.tensor_scalar(lg[:, :, 8:9], zp[:, :, 8:9], -1.0, None,
                                                      ALU.mult))
                nc.vector.tensor_tensor(lg[:, :, 0:8], zp[:, :, 0:8],
                                        mx.unsqueeze(2).to_broadcast([P, TILES, 8]),
                                        ALU.subtract).then_inc(s.shift, 1)
                dve.wait_ge(s.gexp, 1)
                t.settle(dve, nc.vector.tensor_reduce(den, ex[:, :, 0:8], AXX, ALU.add))
                t.settle(dve, nc.vector.reciprocal(den, den))
                t.settle(dve, nc.vector.tensor_tensor(
                    ex[:, :, 0:8], ex[:, :, 0:8], den.unsqueeze(2).to_broadcast([P, TILES, 8]),
                    ALU.mult))
                e_of = ex[:, :, 0:8].unsqueeze(3).to_broadcast([P, TILES, 8, 8])
                f_of = ex[:, :, 0:8].unsqueeze(2).to_broadcast([P, TILES, 8, 8])
                low = lower.rearrange("p (e f) -> p e f", e=8).unsqueeze(1)\
                    .to_broadcast([P, TILES, 8, 8])
                nc.vector.tensor_tensor(cmp, f_of, e_of, ALU.is_gt)
                t.settle(dve, nc.vector.tensor_tensor(eq, f_of, e_of, ALU.is_equal))
                t.settle(dve, nc.vector.tensor_tensor(eq, eq, low, ALU.mult))
                t.settle(dve, nc.vector.tensor_tensor(
                    cmp.rearrange("p n e f -> p (n e f)"), cmp.rearrange("p n e f -> p (n e f)"),
                    eq.rearrange("p n e f -> p (n e f)"), ALU.add))
                t.settle(dve, nc.vector.tensor_reduce(rank, cmp, AXX, ALU.add))
                t.settle(dve, nc.vector.tensor_scalar(rank, rank, 1.5, 0.5, ALU.is_lt, ALU.mult))
                nc.vector.tensor_tensor(wts[:, :, 0:8], rank, ex[:, :, 0:8], ALU.mult)
                t.settle(dve, nc.vector.tensor_scalar(wts[:, :, 8:9], ex[:, :, 8:9], 1.0, 2.0,
                                                      ALU.add, ALU.mult))
                t.settle(dve, nc.vector.reciprocal(wts[:, :, 8:9], wts[:, :, 8:9]))
                t.settle(dve, nc.vector.tensor_copy(wts[:, :, 9:10], wts[:, :, 8:9]))

                def gated(q):
                    for n in range(3 * q, 3 * q + 3):
                        dve.wait_ge(s.silu, n + 1)
                        dve.wait_ge(s.up, 2 * n + 2)
                        if n % 3 == 0 and q >= 2:
                            dve.wait_ge(s.y, 2 * q - 2)
                        nc.vector.tensor_tensor(hid[:, n % 6, :], sg[:, n % 3, :],
                                                ps[:, FIRST_UP + (2 * n + 1) % RING, :], ALU.mult)\
                            .then_inc(s.h, 1)

                def add(q, half):
                    way = 2 * (q % PAIRS) + half
                    dve.wait_ge(s.y, 2 * q + half + 1)
                    if way:
                        dve.wait_ge(s.yused, 2 * q + half)
                    for n in range(TPC):
                        tile = q // PAIRS * TPC + n
                        xt = x[:, tile * D:(tile + 1) * D]
                        last = nc.vector.scalar_tensor_tensor(
                            xt, ps[:, FIRST_Y + half, n * P:(n + 1) * P],
                            wts[:, tile, way:way + 1], xt, ALU.mult, ALU.add)
                    last.then_inc(s.yused, 1)

                gated(0)
                for q in range(ALL_PAIRS):
                    if q + 1 < ALL_PAIRS:
                        gated(q + 1)
                    add(q, 0)
                    add(q, 1)

            return dict(sync=sync, tensor=tensor, scalar=scalar, gpsimd=gpsimd, vector=vector, sems=s)

        S_SLOT = 0
        ST_RING = 4
        O_BANK = 7

        def attention(tag, hd, kind, rope, scale, weights, has_wo, double):
            heads = D // hd
            HG = heads // GROUP
            UNITS = BATCH * HG
            R = 9 * hd
            MAX_ROW = 96
            rows4 = GROUP * hd
            soft = kind != "linear"
            full = kind == "full"
            halves = []
            for qc in range(2):
                kbs = range(KB) if full else range(4 * qc + 4)
                halves.append([(qc, kb, 0 if full or kb < 4 * qc else (kb - 4 * qc) * P)
                               for kb in kbs])
            steps = halves[0] + halves[1]
            NS = len(steps)
            ends = [len(halves[0]) - 1, NS - 1]

            qs = dram(f"{tag}_q", [UNITS, 3, rows4, SEQ], BF16)
            ks = dram(f"{tag}_k", [UNITS, 3, rows4, SEQ], BF16)
            mt = dram(f"{tag}_m", [2, 3, GROUP * CHUNK], BF16)
            ot = dram(f"{tag}_o", [UNITS * GROUP * (hd + 1), SEQ])

            c = Carve()
            if double:
                w1 = c(EXPERTS * FF)
                w2 = c(EXPERTS * FF)
            v_sb = c(UNITS * KB * rows4)
            v_un = v_sb.rearrange("p (u k r) -> p u k r", u=UNITS, k=KB)
            ops_at = c.at
            Qop = [c(GROUP * SEQ, BF16).rearrange("p (j t) -> p j t", j=GROUP) for _ in range(3)]
            Kop = [c(GROUP * SEQ, BF16).rearrange("p (j t) -> p j t", j=GROUP) for _ in range(3)]
            base = c.at
            pr = c(8 * CHUNK).rearrange("p (n t) -> p n t", n=8)
            vx = [c(KB * GROUP * 32).rearrange("p (k j c) -> p k j c", k=KB, j=GROUP) for _ in range(3)]
            osb = c(2 * CHUNK).rearrange("p (n t) -> p n t", n=2)
            mq = c(2 * 16).rearrange("p (n m) -> p n m", n=2)
            mT = c(P)
            mr = c(P)
            ms = c(2 * 3 * P, BF16).rearrange("p (n a t) -> p n a t", n=2, a=3)
            c.at = base
            tab = c(2 * SEQ).rearrange("p (n t) -> p n t", n=2)
            rot = c(2 * CHUNK).rearrange("p (n t) -> p n t", n=2)
            rem = c(2 * CHUNK).rearrange("p (n t) -> p n t", n=2)
            cut = [c(3 * CHUNK, BF16).rearrange("p (a t) -> p a t", a=3) for _ in range(2)]
            num, den = xnT, hid2

            s = sems(tag, "w we tab stats rstd xn tp xT vec pool proj rope cut0 rem1 cut1 cut2 qst0 kst0 qst1 kst1 "
                          "vps vcp ops0 ops1 ops2 kneg vset vx s sread mtp mcp mps ml0 ml1 mst0 mst1 st ex msk "
                          "av ocp ost0 ost1 nl0 nl1 nl2 nl3 oT y x up gel")
            cut_stored = ((s.qst0, s.kst0), (s.qst1, s.kst1))
            operands = (s.ops0, s.ops1, s.ops2)
            max_placed = (s.ml0, s.ml1)
            max_stored = (s.mst0, s.mst1)
            sums_stored = (s.ost0, s.ost1)
            sums_loaded = (s.nl0, s.nl1, s.nl2, s.nl3)
            N_OPS = 4

            def words(op):
                return op.rearrange("p j t -> p (j t)").bitcast(F32)

            def sync(sp):
                for n, w in enumerate(weights):
                    sp.dma_start(wproj[:, n, :], a[w]).then_inc(s.w, 16)
                if rope:
                    sp.dma_start(wprs[:, 0, :], a[rope + "_wqs"]).then_inc(s.w, 16)
                    sp.dma_start(wprs[:, 1, :], a[rope + "_wks"]).then_inc(s.w, 16)
                    sp.dma_start(tab, a[rope + "_tab"]).then_inc(s.tab, 16)
                def load(u, par):
                    q, k = (w.rearrange("u a (d j) t -> u a d (j t)", j=GROUP) for w in (qs, ks))
                    sp.dma_start(Qop[par][0:R], q.rearrange("u a d t -> u (a d) t")[bass.ds(u, 1)]
                                 .to_broadcast([3, 3 * hd, GROUP * SEQ])).then_inc(operands[par], 16)
                    for n in range(3):
                        sp.dma_start(Kop[par][3 * n * hd:3 * (n + 1) * hd], k[bass.ds(u, 1), n]
                                     .to_broadcast([3, hd, GROUP * SEQ])).then_inc(operands[par], 16)

                def put_max(u, par, qc):
                    sp.wait_ge(s.mps, 2 * u + qc + 1)
                    sp.dma_start(mt[qc].rearrange("i (r t) -> r i t", t=P), ms[0:16, qc, :, :])\
                        .then_inc(max_stored[qc], 16)
                    sp.wait_ge(max_stored[qc], 16 * (u + 1))
                    sp.dma_start(Qop[par][MAX_ROW:MAX_ROW + 3, :, qc * CHUNK:(qc + 1) * CHUNK],
                                 mt[qc].rearrange("i (j t) -> i j t", j=GROUP))\
                        .then_inc(max_placed[qc], 16)

                def store(u, qc):
                    sp.wait_ge(s.ocp, 2 * u + qc + 1 + 1)
                    for j in range(GROUP):
                        sp.dma_start(ot[bass.ds((u * GROUP + j) * (hd + 1), hd + 1),
                                        qc * CHUNK:(qc + 1) * CHUNK],
                                     osb[32 * j:32 * j + hd + 1, qc, :]).then_inc(sums_stored[qc], 16)

                def unit(u, third, par, ahead2, ahead1):
                    if soft:
                        put_max(u, par, 1)
                    if ahead2:
                        sp.wait_ge(s.st, u * 4 * NS + 1)
                        load(u + 2, (par + 2) % 3)
                    store(u, 0)
                    if not ahead1:
                        sp.wait_ge(s.ost0, 64 * UNITS + 1)
                        load_sums(2)
                    if soft and ahead1:
                        put_max(u + 1, (par + 1) % 3, 0)
                    store(u, 1)
                    if ahead1 and not ahead2:
                        sp.wait_ge(s.ost0, 64 * (UNITS - 1) + 1)
                        sp.wait_ge(s.ost1, 64 * (UNITS - 1) + 1)
                        load_sums(0)
                        load_sums(1)

                def load_sums(ch):
                    b, half = divmod(ch, 2)
                    src = ot.rearrange("(b h d) t -> b h d t", b=BATCH, d=hd + 1)[b][
                        :, :, half * CHUNK:(half + 1) * CHUNK]
                    r = slice(ch * CHUNK, (ch + 1) * CHUNK)
                    sp.dma_start(num[:, r], src[:, 0:hd, :]).then_inc(sums_loaded[ch], 16)
                    if soft:
                        sp.dma_start(den[:, r], src[:, hd:hd + 1, :].to_broadcast([heads, hd, CHUNK]))\
                            .then_inc(sums_loaded[ch], 16)

                for ch in range(CHUNKS):
                    b, t0 = ch // 2, (ch % 2) * CHUNK
                    for side, to in ((0, qs), (1, ks)):
                        sp.wait_ge(s.cut2, 2 * ch + side + 1)
                        for part in range(3):
                            sp.dma_start(to[b * HG:(b + 1) * HG, part, :, t0:t0 + CHUNK],
                                         cut[side][:, part, :]).then_inc(cut_stored[b][side], 16)
                    if ch == 1:
                        sp.wait_ge(s.qst0, 16 * 3 * CHUNKS // BATCH)
                        sp.wait_ge(s.kst0, 16 * 3 * CHUNKS // BATCH)
                        sp.wait_ge(s.kneg, 1)
                        load(0, 0)
                sp.wait_ge(s.kneg, 2)
                load(1, 1)
                sp.wait_ge(s.kneg, 3)
                if double:
                    sp.dma_start(w1, a["w1_1"]).then_inc(s.we, 16)
                    sp.dma_start(w2, a["w2_1"]).then_inc(s.we, 16)
                sp.wait_ge(s.qst1, 16 * 3 * CHUNKS // BATCH)
                sp.wait_ge(s.kst1, 16 * 3 * CHUNKS // BATCH)
                if soft:
                    put_max(0, 0, 0)
                loops(sp, unit)
                sp.wait_ge(s.ost1, 64 * UNITS + 1)
                load_sums(3)

            def loops(eng, unit):
                whole = (UNITS - 2) // 3
                with eng.Fori(0, whole) as i:
                    for par in range(3):
                        unit(i * 3 + par, i, par, True, True)
                for u in range(3 * whole, UNITS):
                    unit(u, u // 3, u % 3, u + 2 < UNITS, u + 1 < UNITS)

            def s_tasks(half):
                return [(j, qb) for qb in range(4) for j in range(GROUP)]

            def tensor(pe):
                norm_tensor(pe, s, 0)
                pe.wait_ge(s.w, 16 * (len(weights) + (2 if rope else 0)))
                for ch in range(CHUNKS):
                    pe.wait_ge(s.xT, ch + 1)
                    t = slice(ch * CHUNK, (ch + 1) * CHUNK)
                    for side in range(2):
                        if side and ch + 1 < CHUNKS:
                            norm_tensor(pe, s, ch + 1)
                        if ch:
                            pe.wait_ge(s.rem1, 2 * (ch - 1) + side + 1)
                        last = nc.tensor.matmul(ps[:, 1 + 2 * side, :], wproj[:, side, :], xnT[:, t],
                                                start=True, stop=True)
                        if rope:
                            last = nc.tensor.matmul(ps[:, 2 + 2 * side, :], wprs[:, side, :],
                                                    xnT[:, t], start=True, stop=True)
                        last.then_inc(s.proj, 1)
                    if ch:
                        pe.wait_ge(s.vcp, ch)
                    for n in range(TPC):
                        last = nc.tensor.matmul(ps[:, 5, n * P:(n + 1) * P],
                                                xnT[:, ch * CHUNK + n * P:ch * CHUNK + (n + 1) * P],
                                                wproj[:, 2, :], start=True, stop=not bias_v)
                        if bias_v:
                            last = nc.tensor.matmul(ps[:, 5, n * P:(n + 1) * P], ones[0:1, :],
                                                    row(9), start=False, stop=True)
                    last.then_inc(s.vps, 1)

                def slot(pos):
                    b = S_SLOT + 2 * (pos % 2)
                    return ps[:, b:b + 2, :]

                def wait_slot(u, pos):
                    q = pos - 2
                    uu = u if q >= 0 else u - 1
                    q %= 34
                    if q in (0, 17):
                        pe.wait_ge(s.mcp, 2 * uu + (3 if q == 17 else 2))
                    else:
                        pe.wait_ge(s.sread, (uu + 1) * 32 + (q - 1 if q < 17 else q - 2) + 1)

                def scores(u, par, half, k, fresh=False):
                    j, qb = s_tasks(half)[k]
                    pos = 1 + k + 17 * half
                    if not (fresh and pos < 3):
                        wait_slot(u, pos)
                    q0 = half * CHUNK + qb * P
                    width = SEQ if full else q0 + P
                    at = slot(pos)
                    last = None
                    for k0 in range(0, width, CHUNK):
                        n = min(CHUNK, width - k0)
                        last = nc.tensor.matmul(at[:, k0 // CHUNK, 0:n], Qop[par][0:MAX_ROW, j, q0:q0 + P],
                                                Kop[par][0:MAX_ROW, j, k0:k0 + n], start=True,
                                                stop=full or k0 + n < width)
                    if not full:
                        off = (width - P) % CHUNK
                        last = nc.tensor.matmul(at[:, (width - 1) // CHUNK, off:off + P], identb[:, :],
                                                maskb[:, 0, :], start=False, stop=True)
                    last.then_inc(s.s, 1)

                def turn_max(u, pos, hn, fresh=False):
                    if not fresh:
                        wait_slot(u, pos)
                    pe.wait_ge(s.sread, 16 * (hn + 1))
                    nc.tensor.transpose(slot(pos)[0:16, 0, 0:P], mq[:, 0 if pos else 1, :],
                                        ident[:, :]).then_inc(s.mtp, 1)

                def attend(u, vpar, at):
                    qc, kb, off = steps[at]
                    pe.wait_ge(s.ex, u * 4 * NS + 4 * at + 4 + 3)
                    if not soft and (kb >= 4 * qc):
                        pe.wait_ge(s.msk, (u * 8 + kb + 1))
                    if kb == 0:
                        pe.wait_ge(s.vx, u + 1)
                        pe.wait_ge(s.ocp, 2 * u + qc + 1)
                    for j in range(GROUP):
                        last = nc.tensor.matmul(ps[32 * j:32 * j + 32, O_BANK, off:CHUNK],
                                                vx[vpar][:, kb, j, :],
                                                pr[:, (at % 2) * 4 + j, off:CHUNK],
                                                start=kb == 0, stop=at in ends,
                                                tile_position=(0, 32 * j), skip_group_check=True)
                    last.then_inc(s.av, 1)

                def unit(u, third, par, ahead2, ahead1):
                    for at, (qc, kb, off) in enumerate(steps):
                        if soft and kb == 0:
                            pe.wait_ge(max_placed[qc], 16 * (u + 1) + 1)
                        if at == 0:
                            if soft:
                                if ahead1:
                                    pe.wait_ge(operands[(par + 1) % 3],
                                               16 * N_OPS * (third + 1 + par // 2))
                            else:
                                pe.wait_ge(operands[par], 16 * N_OPS * (third + 1))
                        todo = []
                        if soft:
                            if kb == 0 and (qc == 0 or ahead1):
                                todo.append(("turn", 17 * qc, 2 * u + 1 + qc))
                            if ahead1:
                                per = 16 // len(halves[qc])
                                todo += [("s", qc, per * kb + n) for n in range(per)]

                        def run(task):
                            if task[0] == "turn":
                                turn_max(u, task[1], task[2])
                            else:
                                scores(u, (par + 1) % 3, task[1], task[2])

                        for j in range(GROUP):
                            n = (par * 4 * NS + 4 * at + j) % 3
                            pe.wait_ge(s.ex, u * 4 * NS + 4 * at + j + 1)
                            diag = not full and kb >= 4 * qc
                            last = nc.tensor.matmul(
                                ps[:, ST_RING + n, off:CHUNK], Kop[par][:, j, kb * P:(kb + 1) * P],
                                Qop[par][:, j, qc * CHUNK + off:(qc + 1) * CHUNK],
                                start=True, stop=not (diag and soft))
                            if diag and soft:
                                last = nc.tensor.matmul(ps[:, ST_RING + n, off:off + P], identb[:, :],
                                                        maskb[:, 1, :], start=False, stop=True)
                            last.then_inc(s.st, 1)
                            if j % 2 and todo:
                                run(todo.pop(0))
                        for task in todo:
                            run(task)
                        if at:
                            attend(u, par, at - 1)
                    attend(u, par, NS - 1)

                pe.wait_ge(s.vcp, CHUNKS)
                pe.wait_ge(s.rem1, 2 * CHUNKS)
                pe.wait_ge(s.ops0, 16 * N_OPS)
                if soft:
                    for k in range(16):
                        scores(-1, 0, 0, k, fresh=True)
                    wait_slot(-1, 17)
                    turn_max(-1, 17, 0, fresh=True)
                    for k in range(16):
                        scores(-1, 0, 1, k)
                loops(pe, unit)

                if double:
                    for ch in range(CHUNKS):
                        pe.wait_ge(s.oT, ch + 1)
                        if ch >= 2:
                            pe.wait_ge(s.x, ch - 1)
                        t = slice(ch * CHUNK, (ch + 1) * CHUNK)
                        for n in range(TPC):
                            tn = slice(ch * CHUNK + n * P, ch * CHUNK + (n + 1) * P)
                            nc.tensor.matmul(ps[:, ch % 2, n * P:(n + 1) * P], wproj[:, 3, :],
                                             num[:, tn], start=True, stop=False)
                            r = slice(ch * CHUNK + n * D, ch * CHUNK + (n + 1) * D)
                            last = nc.tensor.matmul(ps[:, ch % 2, n * P:(n + 1) * P], res[:, r],
                                                    ident[:, :], start=False, stop=True)
                        last.then_inc(s.y, 1)
                    pe.wait_ge(s.x, CHUNKS)
                    xf = xnT.rearrange("p (m t) -> p m t", m=2)

                    def up(e):
                        for f in range(FT):
                            if e:
                                pe.wait_ge(s.gel, 4 * (e - 1) + f + 1)
                            nc.tensor.matmul(ps[:, 2 + f, 0:2 * P], w1[:, e * FF + f * P:e * FF + (f + 1) * P],
                                             xf[:, :, e * P:(e + 1) * P], start=True, stop=True)\
                                .then_inc(s.up, 1)

                    def dn(e):
                        pe.wait_ge(s.gel, 4 * e + 4)
                        if e >= 2:
                            pe.wait_ge(s.x, CHUNKS + e - 1)
                        for m in range(2):
                            at = ps[:, e % 2, m * P:(m + 1) * P]
                            for f in range(FT):
                                nc.tensor.matmul(at, hT2[:, e % 2, f, m * P:(m + 1) * P],
                                                 w2[:, (e * FT + f) * D:(e * FT + f + 1) * D],
                                                 start=f == 0, stop=False)
                            last = nc.tensor.matmul(at, ones[0:1, :], row(ROW_B2 + e), start=False,
                                                    stop=True)
                        last.then_inc(s.y, 1)

                    pe.wait_ge(s.we, 32)
                    up(0)
                    for e in range(EXPERTS):
                        if e + 1 < EXPERTS:
                            up(e + 1)
                        dn(e)
                else:
                    for ch in range(CHUNKS):
                        pe.wait_ge(s.oT, ch + 1)
                        if ch >= 2:
                            pe.wait_ge(s.x, ch - 1)
                        for n in range(TPC):
                            at = ps[:, ch % 2, n * P:(n + 1) * P]
                            t = slice(ch * CHUNK + n * P, ch * CHUNK + (n + 1) * P)
                            if has_wo:
                                last = nc.tensor.matmul(at, num[:, t], wproj[:, 3, :], start=True,
                                                        stop=True)
                            else:
                                last = nc.tensor.transpose(at, num[:, t], ident[:, :])
                        last.then_inc(s.y, 1)

            bias = tag == "a0"
            bias_v = bias

            def scalar(act):
                act.sem_inc(s.ex, 3)
                act.sem_inc(s.ocp, 1)
                def copy_turned(ch):
                    act.wait_ge(s.tp, ch + 1)
                    t = slice(ch * CHUNK, (ch + 1) * CHUNK)
                    if double:
                        nc.scalar.activation(xnT[:, t], ps[:, TP, :], ACT.Identity,
                                             bias=col("ln_b"), scale=col("ln_g")).then_inc(s.xT, 1)
                    else:
                        nc.scalar.activation(xnT[:, t], ps[:, TP, :], ACT.Copy).then_inc(s.xT, 1)

                copy_turned(0)
                for ch in range(CHUNKS):
                    for side in range(2):
                        if side and ch + 1 < CHUNKS:
                            copy_turned(ch + 1)
                        sc = scale if side == 0 else 1.0
                        if rope:
                            act.wait_ge(s.rope, 2 * ch + side + 1)
                            src = rot[:, side, :]
                        else:
                            act.wait_ge(s.proj, 2 * ch + side + 1)
                            src = ps[:, 1 + 2 * side, :]
                        if ch:
                            act.wait_ge(cut_stored[(ch - 1) // 2][side], 48 * ((ch - 1) % 2 + 1))
                        nc.scalar.activation(cut[side][:, 0, :], src, ACT.Copy, scale=sc)\
                            .then_inc(s.cut0, 1)
                        act.wait_ge(s.rem1, 2 * ch + side + 1)
                        nc.scalar.activation(cut[side][:, 1, :], rem[:, side, :], ACT.Copy)\
                            .then_inc(s.cut1, 1)
                    act.wait_ge(s.vps, ch + 1)
                    b, k0 = ch // 2, (ch % 2) * 4
                    for n in range(TPC):
                        last = nc.scalar.activation(
                            v_un[:, b * HG:(b + 1) * HG, k0 + n, :],
                            ps[:, 5, n * P:(n + 1) * P].rearrange("p (g r) -> p g r", g=HG), ACT.Copy)
                    last.then_inc(s.vcp, 1)

                def copy_max(hn, pos):
                    act.wait_ge(s.mtp, hn + 1)
                    act.wait_ge(s.mps, hn)
                    b = S_SLOT + 2 * (pos % 2)
                    nc.scalar.activation(mT[0:16, :], ps[0:16, b, 0:P], ACT.Copy).then_inc(s.mcp, 1)

                def copy_out(u, qc):
                    act.wait_ge(s.av, u * NS + ends[qc] + 1 + 2)
                    act.wait_ge(sums_stored[qc], 64 * u + 1)
                    nc.scalar.activation(osb[:, qc, :], ps[:, O_BANK, :], ACT.Copy).then_inc(s.ocp, 1)

                def unit(u, third, par, ahead2, ahead1):
                    for at, (qc, kb, off) in enumerate(steps):
                        for j in range(GROUP):
                            n = (par * 4 * NS + 4 * at + j) % 3
                            act.wait_ge(s.st, u * 4 * NS + 4 * at + j + 1 + 1)
                            if j == 0:
                                act.wait_ge(s.av, u * NS + at + 1)
                            nc.scalar.activation(pr[:, (at % 2) * 4 + j, off:CHUNK],
                                                 ps[:, ST_RING + n, off:CHUNK],
                                                 ACT.Exp if soft else ACT.Copy).then_inc(s.ex, 1)
                        if soft and kb == 0 and (qc == 0 or ahead1):
                            copy_max(2 * u + 1 + qc, 17 * qc)
                        if qc == 1 and kb == 0:
                            copy_out(u, 0)
                    copy_out(u, 1)

                act.wait_ge(s.qst1, 16 * 3 * CHUNKS // BATCH)
                act.wait_ge(s.kst1, 16 * 3 * CHUNKS // BATCH)
                act.wait_ge(s.cut2, 2 * CHUNKS)
                if soft:
                    act.wait_ge(s.mtp, 1)
                    nc.scalar.activation(mT[0:16, :], ps[0:16, S_SLOT + 2, 0:P], ACT.Copy)\
                        .then_inc(s.mcp, 1)
                loops(act, unit)
                if double:
                    for e in range(EXPERTS):
                        for f in range(FT):
                            act.wait_ge(s.up, 4 * e + f + 1)
                            if e >= 2:
                                act.wait_ge(s.y, CHUNKS + e - 1)
                            nc.scalar.activation(hT2[:, e % 2, f, :], ps[:, 2 + f, 0:2 * P], ACT.Gelu,
                                                 bias=col("b1_l1", FT * e + f)).then_inc(s.gel, 1)

            if double:
                hT2 = hid2.rearrange("p (n f t) -> p n f t", n=2, f=FT)

            def gpsimd(pool):
                def third_part(ch):
                    for side in range(2):
                        pool.wait_ge(s.cut1, 2 * ch + side + 1)
                        nc.gpsimd.tensor_tensor(cut[side][:, 2, :], rem[:, side, :],
                                                cut[side][:, 1, :], ALU.subtract).then_inc(s.cut2, 1)

                def preset(par):
                    nc.gpsimd.memset(words(Qop[par]), 0.0)
                    nc.gpsimd.memset(words(Kop[par]), MINUS_ONES).then_inc(s.kneg, 1)

                t = Tally(s.pool)
                preset(0)
                norms = CHUNKS * (2 if double else 1)
                ahead = 5 if double else 3
                for g in range(ahead):
                    norm_gpsimd(pool, s, t, g)
                    if g == 1:
                        preset(1)
                for ch in range(CHUNKS):
                    third_part(ch)
                    for g in range(ahead, min(ahead + norms // CHUNKS, norms)):
                        norm_gpsimd(pool, s, t, g)
                        ahead += 1
                preset(2)
                pool.wait_ge(s.vset, 3)
                pool.wait_ge(s.vcp, CHUNKS)

                def values(u, par):
                    nc.gpsimd.tensor_tensor(
                        vx[par][:, :, :, 0:hd],
                        v_sb[:, bass.ds(u * KB * rows4, KB * rows4)]
                        .rearrange("p (k j d) -> p k j d", k=KB, j=GROUP),
                        ones[:, 0:1].unsqueeze(2).unsqueeze(3).to_broadcast([P, KB, GROUP, hd]),
                        ALU.mult).then_inc(s.vx, 1)

                def cut_max(u, qc):
                    hn = 2 * u + qc
                    pool.wait_ge(s.mcp, hn + 1)
                    pool.wait_ge(max_placed[qc], 16 * u + 1)
                    m = [ms[0:16, qc, i, :] for i in range(3)]
                    t = Tally(s.msk, 3 * hn)
                    t.settle(pool, nc.gpsimd.tensor_tensor(m[0], mT[0:16, :], ones[0:16, :], ALU.mult))
                    t.settle(pool, nc.gpsimd.tensor_tensor(mr[0:16, :], mT[0:16, :], m[0],
                                                           ALU.subtract))
                    t.settle(pool, nc.gpsimd.tensor_tensor(m[1], mr[0:16, :], ones[0:16, :], ALU.mult))
                    nc.gpsimd.tensor_tensor(m[2], mr[0:16, :], m[1], ALU.subtract)\
                        .then_inc(s.mps, 1)

                def unit(u, third, par, ahead2, ahead1):
                    if ahead1:
                        pool.wait_ge(s.av, u * NS + 1 + 1)
                        values(u + 1, (par + 1) % 3)
                    if soft:
                        cut_max(u, 1)
                        if ahead1:
                            cut_max(u + 1, 0)
                    else:
                        for qc in range(2):
                            for kb in range(4 * qc, 4 * qc + 4):
                                at = steps.index((qc, kb, (kb - 4 * qc) * P))
                                off = steps[at][2]
                                for j in range(GROUP):
                                    pool.wait_ge(s.ex, u * 4 * NS + 4 * at + j + 1 + 3)
                                    w = pr[:, (at % 2) * 4 + j, off:off + P]
                                    last = nc.gpsimd.tensor_tensor(w, w, masks[:, 2, :], ALU.mult)
                                last.then_inc(s.msk, 1)

                values(0, 0)
                if soft:
                    cut_max(0, 0)
                loops(pool, unit)

            def vector(dve):
                dve.sem_inc(s.av, 2)
                dve.sem_inc(s.st, 1)
                for sem in sums_stored + max_placed:
                    dve.sem_inc(sem, 1)
                t = Tally(s.vec)
                if rope:
                    dve.wait_ge(s.tab, 16)
                def normed(ch):
                    if double:
                        norm_twice(dve, s, t, ch)
                    else:
                        norm_chunk(dve, s, t, x_rows, ch)

                normed(0)
                for ch in range(CHUNKS):
                    if ch + 1 < CHUNKS:
                        normed(ch + 1)
                    tt = slice((ch % 2) * CHUNK, (ch % 2 + 1) * CHUNK)
                    for side in range(2):
                        if rope:
                            dve.wait_ge(s.proj, 2 * ch + side + 1)
                            if ch:
                                dve.wait_ge(s.cut2, 2 * (ch - 1) + side + 1)
                            b = [col("b_q"), col("b_qs")] if side == 0 else [col("b_k"), col("b_ks")]
                            src = ps[:, 1 + 2 * side, :]
                            if bias:
                                nc.vector.scalar_tensor_tensor(rot[:, side, :], src, b[0], tab[:, 0, tt],
                                                               ALU.add, ALU.mult)
                                t.settle(dve, nc.vector.scalar_tensor_tensor(
                                    rem[:, side, :], ps[:, 2 + 2 * side, :], b[1], tab[:, 1, tt],
                                    ALU.add, ALU.mult))
                            else:
                                nc.vector.tensor_tensor(rot[:, side, :], src, tab[:, 0, tt], ALU.mult)
                                t.settle(dve, nc.vector.tensor_tensor(
                                    rem[:, side, :], ps[:, 2 + 2 * side, :], tab[:, 1, tt], ALU.mult))
                            nc.vector.tensor_tensor(rot[:, side, :], rot[:, side, :], rem[:, side, :],
                                                    ALU.add).then_inc(s.rope, 1)
                    for side in range(2):
                        src = rot[:, side, :] if rope else ps[:, 1 + 2 * side, :]
                        dve.wait_ge(s.cut0, 2 * ch + side + 1)
                        if ch and not rope:
                            dve.wait_ge(s.cut2, 2 * (ch - 1) + side + 1)
                        nc.vector.scalar_tensor_tensor(rem[:, side, :], src, scale if side == 0 else 1.0,
                                                       cut[side][:, 0, :], ALU.mult,
                                                       ALU.subtract).then_inc(s.rem1, 1)
                dve.wait_ge(s.qst1, 16 * 3 * CHUNKS // BATCH)
                dve.wait_ge(s.kst1, 16 * 3 * CHUNKS // BATCH)
                for par in range(3):
                    nc.vector.memset(vx[par], 1.0).then_inc(s.vset, 1)

                def maxima(base, half):
                    for k, (j, qb) in enumerate(s_tasks(half)):
                        pos = 1 + k + 17 * half
                        dve.wait_ge(s.s, base + 16 * half + k + 1)
                        b = S_SLOT + 2 * (pos % 2)
                        width = SEQ if full else half * CHUNK + (qb + 1) * P
                        src = ps[:, b:b + 2, :].rearrange("p b t -> p (b t)")[:, 0:width]
                        nc.vector.tensor_reduce(mq[:, half, j * 4 + qb:j * 4 + qb + 1], src, AXX,
                                                ALU.max).then_inc(s.sread, 1)

                def unit(u, third, par, ahead2, ahead1):
                    if ahead1:
                        maxima((u + 1) * 32, 0)
                        maxima((u + 1) * 32, 1)

                if soft:
                    maxima(0, 0)
                    maxima(0, 1)
                    loops(dve, unit)

                for ch in range(CHUNKS):
                    r = slice(ch * CHUNK, (ch + 1) * CHUNK)
                    dve.wait_ge(sums_loaded[ch], 32 if soft else 16)
                    if soft:
                        t.settle(dve, nc.vector.reciprocal(den[:, r], den[:, r]))
                        nc.vector.tensor_tensor(num[:, r], num[:, r], den[:, r], ALU.mult)\
                            .then_inc(s.oT, 1)
                    else:
                        dve.sem_inc(s.oT, 1)
                for ch in range(CHUNKS):
                    dve.wait_ge(s.y, ch + 1)
                    r = slice(ch * CHUNK, (ch + 1) * CHUNK)
                    if double:
                        nc.vector.tensor_copy(xnT[:, r], ps[:, ch % 2, :]).then_inc(s.x, 1)
                    else:
                        nc.vector.tensor_tensor(x[:, r], x[:, r], ps[:, ch % 2, :], ALU.add)\
                            .then_inc(s.x, 1)
                if double:
                    xm = x.rearrange("p (m e d) -> p m e d", m=2, e=EXPERTS)
                    for e in range(EXPERTS):
                        dve.wait_ge(s.y, CHUNKS + e + 1)
                        nc.vector.scalar_tensor_tensor(
                            xm[:, :, e, :], ps[:, e % 2, 0:2 * P].rearrange("p (m d) -> p m d", m=2),
                            0.5, xm[:, :, e, :], ALU.mult, ALU.add).then_inc(s.x, 1)

            return dict(sync=sync, tensor=tensor, scalar=scalar, gpsimd=gpsimd, vector=vector, sems=s)

        wprs = sb("wprs", [P, 2, D])
        hid2 = sb("hid2", [P, 2 * FT * 2 * P])

        def ternary_mlp(tag):
            c = Carve()
            hh = c(2 * FF).rearrange("p (n f) -> p n f", n=2)
            hn = c(2 * FF).rearrange("p (n f) -> p n f", n=2)
            hT = c(2 * FF).rearrange("p (n f) -> p n f", n=2)
            st = c(2 * 6).rearrange("p (n f) -> p n f", n=2)
            m2 = c(2 * 2).rearrange("p (n f) -> p n f", n=2)
            v2 = c(2)
            r2 = c(2)
            s = sems(tag, "stats rstd xn tp xT vec pool up gel st2 r2 hn htp hT y x")

            def tensor(pe):
                def up(n):
                    if n >= 2:
                        pe.wait_ge(s.gel, n - 1)
                    nc.tensor.matmul(ps[:, 1 + n % 2, :], xnT[:, n * P:(n + 1) * P], w2fc[:, :],
                                     start=True, stop=True).then_inc(s.up, 1)

                def turn(n):
                    pe.wait_ge(s.hn, n + 1)
                    if n >= 2:
                        pe.wait_ge(s.hT, n - 1)
                    for f in range(FT):
                        last = nc.tensor.transpose(ps[:, 3 + n % 2, f * P:(f + 1) * P],
                                                   hn[:, n % 2, f * P:(f + 1) * P], ident[:, :])
                    last.then_inc(s.htp, 1)

                def down(n):
                    pe.wait_ge(s.hT, n + 1)
                    if n >= 2 * TPC:
                        pe.wait_ge(s.x, n // TPC - 1)
                    for f in range(FT):
                        last = nc.tensor.matmul(ps[:, 5 + n // TPC % 2, n % TPC * P:(n % TPC + 1) * P],
                                                hT[:, n % 2, f * P:(f + 1) * P], w2pj[:, f, :],
                                                start=f == 0, stop=f == FT - 1)
                    last.then_inc(s.y, 1)

                for ch in range(CHUNKS):
                    norm_tensor(pe, s, ch)
                pe.wait_ge(s.xT, CHUNKS)
                for n in range(TILES + 3):
                    if n < TILES:
                        up(n)
                    if 2 <= n < TILES + 2:
                        turn(n - 2)
                    if n >= 3:
                        down(n - 3)

            def scalar(act):
                for ch in range(CHUNKS):
                    act.wait_ge(s.tp, ch + 1)
                    nc.scalar.activation(xnT[:, ch * CHUNK:(ch + 1) * CHUNK], ps[:, TP, :], ACT.Copy)\
                        .then_inc(s.xT, 1)
                for n in range(TILES + 2):
                    if n < TILES:
                        act.wait_ge(s.up, n + 1)
                        if n >= 2:
                            act.wait_ge(s.hn, n - 1)
                        nc.scalar.activation(hh[:, n % 2, :], ps[:, 1 + n % 2, :], ACT.Gelu)\
                            .then_inc(s.gel, 1)
                    if n >= 2:
                        k = n - 2
                        act.wait_ge(s.htp, k + 1)
                        if k >= 2:
                            act.wait_ge(s.y, k - 1)
                        for f in range(FT):
                            last = nc.scalar.activation(hT[:, k % 2, f * P:(f + 1) * P],
                                                        ps[:, 3 + k % 2, f * P:(f + 1) * P],
                                                        ACT.Identity, bias=col("l2_b", f),
                                                        scale=col("l2_w", f))
                        last.then_inc(s.hT, 1)

            def gpsimd(pool):
                t = Tally(s.pool)
                for ch in range(CHUNKS):
                    norm_gpsimd(pool, s, t, ch)
                for n in range(TILES):
                    k = n % 2
                    pool.wait_ge(s.st2, n + 1)
                    t.settle(pool, nc.gpsimd.tensor_scalar(v2[:, k:k + 1], m2[:, k, 1:2], EPS, None,
                                                           ALU.add))
                    nc.gpsimd.tensor_tensor(r2[:, k:k + 1], v2[:, k:k + 1], neghalf[:, 0:1], ALU.pow)\
                        .then_inc(s.r2, 1)

            def vector(dve):
                t = Tally(s.vec)
                for ch in range(CHUNKS):
                    norm_chunk(dve, s, t, x_rows, ch)
                for n in range(TILES + 1):
                    if n < TILES:
                        k = n % 2
                        dve.wait_ge(s.gel, n + 1)
                        t.settle(dve, nc.vector.bn_stats(st[:, k, :], hh[:, k, :]))
                        nc.vector.bn_aggr(m2[:, k, :], st[:, k, :]).then_inc(s.st2, 1)
                    if n:
                        k = (n - 1) % 2
                        dve.wait_ge(s.r2, n)
                        if n >= 3:
                            dve.wait_ge(s.htp, n - 2)
                        nc.vector.tensor_scalar(hn[:, k, :], hh[:, k, :], m2[:, k, 0:1], r2[:, k:k + 1],
                                                ALU.subtract, ALU.mult).then_inc(s.hn, 1)
                    if n >= TPC + 3 and (n - 3) % TPC == 0:
                        add(dve, (n - 3) // TPC - 1)
                add(dve, CHUNKS - 1)

            def add(dve, ch):
                dve.wait_ge(s.y, TPC * (ch + 1))
                r = slice(ch * CHUNK, (ch + 1) * CHUNK)
                nc.vector.scalar_tensor_tensor(x[:, r], ps[:, 5 + ch % 2, :], 0.5, x[:, r],
                                               ALU.mult, ALU.add).then_inc(s.x, 1)

            return dict(tensor=tensor, scalar=scalar, gpsimd=gpsimd, vector=vector, sems=s)

        def mlp_tensor(pe, s, w_in, w_out, b_row, hT):
            def up(ch):
                for f in range(FT):
                    if ch:
                        pe.wait_ge(s.gel, 4 * (ch - 1) + f + 1)
                    nc.tensor.matmul(ps[:, 1 + f, :], w_in[:, f * P:(f + 1) * P],
                                     xnT[:, ch * CHUNK:(ch + 1) * CHUNK], start=True, stop=True)\
                        .then_inc(s.up, 1)

            def down(ch):
                pe.wait_ge(s.gel, 4 * ch + 4)
                if ch >= 2:
                    pe.wait_ge(s.x, ch - 1)
                for n in range(TPC):
                    at = ps[:, 5 + ch % 2, n * P:(n + 1) * P]
                    for f in range(FT):
                        nc.tensor.matmul(at, hT[:, ch % 2, f, n * P:(n + 1) * P], w_out[:, f, :],
                                         start=f == 0, stop=False)
                    last = nc.tensor.matmul(at, ones[0:1, :], row(b_row), start=False, stop=True)
                last.then_inc(s.y, 1)

            norm_tensor(pe, s, 0)
            for ch in range(CHUNKS + 1):
                if ch + 1 < CHUNKS:
                    norm_tensor(pe, s, ch + 1)
                if ch < CHUNKS:
                    pe.wait_ge(s.xT, ch + 1)
                    up(ch)
                if ch:
                    down(ch - 1)

        def mlp_gelu(act, s, hT, bias_name, ch):
            for f in range(FT):
                act.wait_ge(s.up, 4 * ch + f + 1)
                if ch >= 2:
                    act.wait_ge(s.y, ch - 1)
                nc.scalar.activation(hT[:, ch % 2, f, :], ps[:, 1 + f, :], ACT.Gelu,
                                     bias=col(bias_name, f)).then_inc(s.gel, 1)

        def binary_mlp(tag):
            c = Carve()
            hT = c(2 * FT * CHUNK).rearrange("p (n f t) -> p n f t", n=2, f=FT)
            s = sems(tag, "stats rstd xn tp xT vec pool up gel y x")

            def tensor(pe):
                mlp_tensor(pe, s, w3a, w3b, ROW_L3B2, hT)

            def scalar(act):
                for ch in range(CHUNKS + 1):
                    if ch < CHUNKS:
                        act.wait_ge(s.tp, ch + 1)
                        nc.scalar.activation(xnT[:, ch * CHUNK:(ch + 1) * CHUNK], ps[:, TP, :],
                                             ACT.Copy).then_inc(s.xT, 1)
                    if ch:
                        mlp_gelu(act, s, hT, "l3w_b1", ch - 1)

            def gpsimd(pool):
                t = Tally(s.pool)
                for ch in range(CHUNKS):
                    norm_gpsimd(pool, s, t, ch)

            def vector(dve):
                t = Tally(s.vec)
                norm_chunk(dve, s, t, x_rows, 0)
                norm_chunk(dve, s, t, x_rows, 1)
                for ch in range(CHUNKS):
                    if ch + 2 < CHUNKS:
                        norm_chunk(dve, s, t, x_rows, ch + 2)
                    dve.wait_ge(s.y, ch + 1)
                    r = slice(ch * CHUNK, (ch + 1) * CHUNK)
                    nc.vector.scalar_tensor_tensor(x[:, r], ps[:, 5 + ch % 2, :], 0.5,
                                                   x[:, r], ALU.mult, ALU.add).then_inc(s.x, 1)

            return dict(tensor=tensor, scalar=scalar, gpsimd=gpsimd, vector=vector, sems=s)

        def lion(tag):
            c = Carve()
            wq, wk, wo, wd = (c(D) for _ in range(4))
            wv = c(8 * D).rearrange("p (e m) -> p e m", e=8)
            f1 = c(FF)
            f2 = c(FF).rearrange("p (f d) -> p f d", f=FT)
            sel = c(8 * P).rearrange("p (e m) -> p e m", e=8)
            same = c(P)
            phq = c(TOKENS)
            phk = c(TOKENS)
            lam = c(TOKENS)
            low = c(2 * CHUNK).rearrange("p (n t) -> p n t", n=2)
            kv = c(2 * SEQ).rearrange("p (n t) -> p n t", n=2)
            fw = c(3 * SEQ).rearrange("p (n t) -> p n t", n=3)
            bw = c(2 * SEQ).rearrange("p (n t) -> p n t", n=2)
            oT = c(TOKENS)
            rowo = c(2 * D)
            hT = c(2 * FT * CHUNK).rearrange("p (n f t) -> p n f t", n=2, f=FT)
            s = sems(tag, "w stats rstd xn tp xT vec pool pj mn ex lin vps vr g gq acc oT y r up gel x "
                          "bz")

            def sync(sp):
                for dst, name in ((wq, "wq3"), (wk, "wk3"), (wv, "wv3"), (wo, "wo3"), (wd, "wd3"),
                                  (f1, "f13"), (f2, "f23"), (sel, "sel"), (same, "same")):
                    sp.dma_start(dst, a[name]).then_inc(s.w, 16)
                sp.dma_start(rowo[0:1, :], a["rows3"]).then_inc(s.w, 16)
            NW = 160

            def tensor(pe):
                pe.wait_ge(s.w, NW)
                norm_tensor(pe, s, 0)
                for ch in range(CHUNKS):
                    pe.wait_ge(s.xT, ch + 1)
                    t = slice(ch * CHUNK, (ch + 1) * CHUNK)
                    for k, w in enumerate((wq, wk, wd)):
                        if k == 1 and ch + 1 < CHUNKS:
                            norm_tensor(pe, s, ch + 1)
                        if ch:
                            pe.wait_ge(s.ex, 3 * (ch - 1) + k + 1)
                        nc.tensor.matmul(ps[:, 1 + k, :], w, xnT[:, t], start=True, stop=True)\
                            .then_inc(s.pj, 1)

                def value(n):
                    b, e = divmod(n, 8)
                    if n >= 2:
                        pe.wait_ge(s.vr, n - 1)
                    for h in range(2):
                        last = nc.tensor.matmul(ps[:, 2 * (n % 2) + h, :],
                                                wv[:, e, :],
                                                xnT[:, b * SEQ + h * CHUNK:b * SEQ + (h + 1) * CHUNK],
                                                start=True, stop=True)
                    last.then_inc(s.vps, 1)

                def gather(n):
                    b, e = divmod(n, 9)
                    pe.wait_ge(s.gq, n + 1)
                    if b and e == 0:
                        pe.wait_ge(s.oT, 1)
                    for h in range(2):
                        w = sel[:, e, :] if e < 8 else same
                        last = nc.tensor.matmul(ps[:, (4 if e < 8 else 6) + h, :], w,
                                                fw[:, n % 3, h * CHUNK:(h + 1) * CHUNK],
                                                start=e in (0, 8), stop=e in (7, 8),
                                                skip_group_check=True)
                    last.then_inc(s.acc, 1)

                pe.wait_ge(s.ex, 3 * CHUNKS)
                value(0)
                value(1)
                nv = 2
                for n in range(18):
                    if n % 9 < 8 and nv < 16:
                        value(nv)
                        nv += 1
                    gather(n)
                for ch in range(CHUNKS):
                    if ch % 2 == 0:
                        pe.wait_ge(s.oT, ch // 2 + 1)
                    if ch >= 2:
                        pe.wait_ge(s.r, ch - 1)
                    for n in range(TPC):
                        t = slice(ch * CHUNK + n * P, ch * CHUNK + (n + 1) * P)
                        at = ps[:, 2 + ch % 2, n * P:(n + 1) * P]
                        nc.tensor.matmul(at, oT[:, t], wo, start=True, stop=False)
                        last = nc.tensor.matmul(at, ones[0:1, :], rowo[0:1, 0:D], start=False, stop=True)
                    last.then_inc(s.y, 1)
                norm_tensor(pe, s, CHUNKS)
                for ch in range(CHUNKS + 1):
                    if ch + 1 < CHUNKS:
                        norm_tensor(pe, s, CHUNKS + ch + 1)
                    if ch < CHUNKS:
                        pe.wait_ge(s.xT, CHUNKS + ch + 1)
                        for f in range(FT):
                            if ch:
                                pe.wait_ge(s.gel, 4 * (ch - 1) + f + 1)
                            nc.tensor.matmul(ps[:, 1 + f, :], f1[:, f * P:(f + 1) * P],
                                             xnT[:, ch * CHUNK:(ch + 1) * CHUNK], start=True, stop=True)\
                                .then_inc(s.up, 1)
                    if ch:
                        k = ch - 1
                        pe.wait_ge(s.gel, 4 * k + 4)
                        if k >= 2:
                            pe.wait_ge(s.x, k - 1)
                        for n in range(TPC):
                            at = ps[:, 5 + k % 2, n * P:(n + 1) * P]
                            for f in range(FT):
                                nc.tensor.matmul(at, hT[:, k % 2, f, n * P:(n + 1) * P], f2[:, f, :],
                                                 start=f == 0, stop=False)
                            last = nc.tensor.matmul(at, ones[0:1, :], rowo[0:1, D:2 * D], start=False,
                                                    stop=True)
                        last.then_inc(s.y, 1)

            def scalar(act):
                def copy_turned(k, gain, offset):
                    act.wait_ge(s.tp, k + 1)
                    t = slice(k % CHUNKS * CHUNK, (k % CHUNKS + 1) * CHUNK)
                    nc.scalar.activation(xnT[:, t], ps[:, TP, :], ACT.Identity, bias=col(offset),
                                         scale=col(gain)).then_inc(s.xT, 1)

                copy_turned(0, "l3_g1", "l3_o1")
                for ch in range(CHUNKS):
                    t = slice(ch * CHUNK, (ch + 1) * CHUNK)
                    for k, dst in enumerate((phq, phk, lam)):
                        if k == 1 and ch + 1 < CHUNKS:
                            copy_turned(ch + 1, "l3_g1", "l3_o1")
                        if k < 2:
                            act.wait_ge(s.mn, 2 * ch + k + 1)
                            nc.scalar.activation(dst[:, t], ps[:, 1 + k, :], ACT.Exp,
                                                 bias=col(("l3_qb", "l3_kb")[k])).then_inc(s.ex, 1)
                        else:
                            act.wait_ge(s.pj, 3 * ch + 3)
                            nc.scalar.activation(dst[:, t], ps[:, 3, :], ACT.Sigmoid,
                                                 bias=col("l3_db")).then_inc(s.ex, 1)
                copy_turned(CHUNKS, "l3_g2", "l3_o2")
                for ch in range(CHUNKS):
                    if ch + 1 < CHUNKS:
                        copy_turned(CHUNKS + ch + 1, "l3_g2", "l3_o2")
                    for f in range(FT):
                        act.wait_ge(s.up, 4 * ch + f + 1)
                        if ch >= 2:
                            act.wait_ge(s.y, CHUNKS + ch - 1)
                        nc.scalar.activation(hT[:, ch % 2, f, :], ps[:, 1 + f, :], ACT.Gelu,
                                             bias=col("l3_f1b", f)).then_inc(s.gel, 1)

            def gpsimd(pool):
                t = Tally(s.pool)
                for ch in range(2 * CHUNKS):
                    norm_gpsimd(pool, s, t, ch)
                for n in range(18):
                    pool.wait_ge(s.g, n + 1)
                    nc.gpsimd.tensor_tensor(fw[:, n % 3, :], fw[:, n % 3, :],
                                            phq[:, n // 9 * SEQ:(n // 9 + 1) * SEQ], ALU.mult)\
                        .then_inc(s.gq, 1)
                for ch in range(CHUNKS):
                    norm_gpsimd(pool, s, t, 2 * CHUNKS + ch)

            def vector(dve):
                t = Tally(s.vec)
                norm_twice(dve, s, t, 0)
                for ch in range(CHUNKS):
                    tt = slice(ch * CHUNK, (ch + 1) * CHUNK)
                    if ch + 1 < CHUNKS:
                        norm_twice(dve, s, t, ch + 1)
                    for k, b in enumerate(("l3_qb", "l3_kb")):
                        dve.wait_ge(s.pj, 3 * ch + k + 1)
                        nc.vector.tensor_scalar(low[:, k, :], ps[:, 1 + k, :], col(b), 0.0, ALU.add,
                                                ALU.max).then_inc(s.mn, 1)
                    for k, dst in enumerate((phq, phk)):
                        dve.wait_ge(s.ex, 3 * ch + k + 1)
                        last = nc.vector.scalar_tensor_tensor(dst[:, tt], dst[:, tt], 1.0,
                                                              low[:, k, :], ALU.min, ALU.add)
                    dve.wait_ge(s.ex, 3 * ch + 3)
                    t.settle(dve, nc.vector.tensor_scalar(lam[:, tt], lam[:, tt], 1e-8, None,
                                                          ALU.max))
                nc.vector.memset(bw[:, 0, SEQ - 1:SEQ], 0.0)
                t.settle(dve, nc.vector.memset(bw[:, 1, SEQ - 1:SEQ], 0.0))
                for n in range(18):
                    b, e = divmod(n, 9)
                    k = n % 2
                    bb = slice(b * SEQ, (b + 1) * SEQ)
                    if e < 8:
                        v = 8 * b + e
                        dve.wait_ge(s.vps, v + 1)
                        nc.vector.scalar_tensor_tensor(
                            kv[:, k, :],
                            ps[:, 2 * (v % 2):2 * (v % 2) + 2, :].rearrange("p b t -> p (b t)"),
                            col("l3_vb", e), phk[:, bb], ALU.add, ALU.mult).then_inc(s.vr, 1)
                        dve.wait_ge(s.vr, v + 1)
                    else:
                        t.settle(dve, nc.vector.tensor_copy(kv[:, k, :], phk[:, bb]))
                    if n >= 3:
                        dve.wait_ge(s.acc, n - 2)
                    nc.vector.tensor_tensor_scan(fw[:, n % 3, :], lam[:, bb], kv[:, k, :], 0.0,
                                                 ALU.mult, ALU.add)
                    t.settle(dve, nc.vector.tensor_tensor_scan(
                        bw[:, k, 0:SEQ - 1][:, ::-1], kv[:, k, 1:SEQ][:, ::-1],
                        lam[:, b * SEQ + 1:(b + 1) * SEQ][:, ::-1], 0.0, ALU.add, ALU.mult))
                    nc.vector.tensor_tensor(fw[:, n % 3, :], fw[:, n % 3, :], bw[:, k, :],
                                            ALU.add)\
                        .then_inc(s.g, 1)
                    if e == 8:
                        dve.wait_ge(s.acc, n + 1)
                        dn = ps[:, 6:8, :].rearrange("p b t -> p (b t)")
                        t.settle(dve, nc.vector.tensor_scalar(oT[:, bb], dn, 1e-6, None, ALU.max))
                        t.settle(dve, nc.vector.reciprocal(oT[:, bb], oT[:, bb]))
                        nc.vector.tensor_tensor(oT[:, bb], oT[:, bb],
                                                ps[:, 4:6, :].rearrange("p b t -> p (b t)"),
                                                ALU.mult).then_inc(s.oT, 1)
                for ch in range(CHUNKS):
                    r = slice(ch * CHUNK, (ch + 1) * CHUNK)
                    dve.wait_ge(s.y, ch + 1)
                    nc.vector.tensor_tensor(res[:, r], res[:, r], ps[:, 2 + ch % 2, :], ALU.add)\
                        .then_inc(s.r, 1)
                dve.wait_ge(s.r, CHUNKS)
                for ch in range(CHUNKS):
                    r = slice(ch * CHUNK, (ch + 1) * CHUNK)
                    last = nc.vector.tensor_tensor(x[:, r], x[:, r], res[:, r], ALU.add)
                t.settle(dve, last)
                norm_chunk(dve, s, t, res_rows, 0, 2 * CHUNKS, CHUNKS)
                norm_chunk(dve, s, t, res_rows, 1, 2 * CHUNKS, CHUNKS)
                for ch in range(CHUNKS):
                    if ch + 2 < CHUNKS:
                        norm_chunk(dve, s, t, res_rows, ch + 2, 2 * CHUNKS, CHUNKS)
                    dve.wait_ge(s.y, CHUNKS + ch + 1)
                    r = slice(ch * CHUNK, (ch + 1) * CHUNK)
                    nc.vector.tensor_tensor(x[:, r], x[:, r], ps[:, 5 + ch % 2, :], ALU.add)\
                        .then_inc(s.x, 1)

            return dict(sync=sync, tensor=tensor, scalar=scalar, gpsimd=gpsimd, vector=vector, sems=s)

        cw = Carve()
        raw_fc, raw_pj, raw_a, raw_b = (cw(FF) for _ in range(4))
        tmp_v, tmp_s = cw(FF), cw(FF)
        gam = cw(8)

        def boot_sync(sp):
            for dst, name in ((x, "x"), (ident, "ident"), (masks, "masks"), (lower, "lower"),
                              (cols[:, 0:n_cols - 4], "cols"), (rows[0:1, :], "rows"), (raw_fc, "fc2"),
                              (raw_pj, "pj2"), (raw_a, "w13"), (raw_b, "w23")):
                sp.dma_start(dst, a[name]).then_inc(boot.const, 16)
        NBOOT = 160

        def boot_gpsimd(pool):
            pool.wait_ge(boot.bw, 1)

        def boot_tensor(pe):
            pe.wait_ge(boot.gabs, 1)
            nc.tensor.matmul(ps[:, 0, 0:2], ones[:, :], gam[:, 0:2], start=True, stop=True)\
                .then_inc(boot.gsum, 1)
            pe.wait_ge(boot.gabs, 2)
            nc.tensor.matmul(ps[:, 1, :], ones[:, :], tmp_v, start=True, stop=True)\
                .then_inc(boot.gsum, 1)
            pe.wait_ge(boot.gabs, 3)
            for f in range(FT):
                last = nc.tensor.matmul(ps[:, 2, 0:D], ones[:, :], tmp_v[:, f * D:(f + 1) * D],
                                        start=f == 0, stop=f == FT - 1)
            last.then_inc(boot.gsum, 1)

        def boot_scalar(act):
            act.wait_ge(boot.const, NBOOT)
            nc.scalar.activation(w3a[:, :], raw_a, ACT.Sign).then_inc(boot.bsign, 1)
            nc.scalar.activation(w3b.rearrange("p f d -> p (f d)"), raw_b, ACT.Sign)\
                .then_inc(boot.bsign, 1)

        def boot_vector(dve):
            t = Tally(boot.vec)
            dve.wait_ge(boot.const, NBOOT)
            nc.vector.memset(ones[:, :], 1.0)
            nc.vector.tensor_copy(identb[:, :], ident[:, :])
            nc.vector.tensor_copy(maskb.rearrange("p n t -> p (n t)"),
                                  masks[:, 0:2, :].rearrange("p n t -> p (n t)"))
            for k, src in enumerate((raw_fc, raw_pj)):
                t.settle(dve, nc.vector.scalar_tensor_tensor(tmp_s, src, -1.0, src, ALU.mult, ALU.max))
                last = nc.vector.tensor_reduce(gam[:, k:k + 1], tmp_s, AXX, ALU.add)
                if k == 0:
                    t.settle(dve, last)
            last.then_inc(boot.gabs, 1)
            dve.wait_ge(boot.gsum, 1)
            t.settle(dve, nc.vector.tensor_scalar(gam[:, 2:4], ps[:, 0, 0:2], 1.0 / (D * FF), 1e-6,
                                                  ALU.mult, ALU.add))
            t.settle(dve, nc.vector.tensor_scalar(gam[:, 2:4], gam[:, 2:4], 0.5, None, ALU.mult))
            t.settle(dve, nc.vector.tensor_scalar(gam[:, 4:6], gam[:, 2:4], -1.0, None, ALU.mult))
            for k, (src, dst) in enumerate(((raw_fc, w2fc[:, :]),
                                            (raw_pj, w2pj.rearrange("p f d -> p (f d)")))):
                t.settle(dve, nc.vector.tensor_scalar(tmp_s, src, gam[:, 4 + k:5 + k], None,
                                                      ALU.is_lt))
                t.settle(dve, nc.vector.scalar_tensor_tensor(dst, src, gam[:, 2 + k:3 + k], tmp_s,
                                                             ALU.is_gt, ALU.subtract))
            nc.vector.scalar_tensor_tensor(tmp_v, raw_a, -1.0, raw_a, ALU.mult, ALU.max)\
                .then_inc(boot.gabs, 1)
            dve.wait_ge(boot.gsum, 2)
            dve.wait_ge(boot.bsign, 2)

            def binarise(dst, alpha, src, k):
                t.settle(dve, nc.vector.scalar_tensor_tensor(dst, alpha, k, dst, ALU.mult, ALU.mult))
                t.settle(dve, nc.vector.tensor_tensor(dst, dst, src, ALU.subtract))
                t.settle(dve, nc.vector.tensor_tensor(dst, dst, src, ALU.add))

            binarise(w3a[:, :], ps[:, 1, :], raw_a, 1.0 / D)
            nc.vector.scalar_tensor_tensor(tmp_v, raw_b, -1.0, raw_b, ALU.mult, ALU.max)\
                .then_inc(boot.gabs, 1)
            dve.wait_ge(boot.gsum, 3)
            for f in range(FT):
                binarise(w3b[:, f, :], ps[:, 2, 0:D], raw_b[:, f * D:(f + 1) * D], 1.0 / FF)

            nc.vector.memset(neghalf[:, :], -0.5).then_inc(boot.bw, 1)

        ROOT8 = 1.0 / 8.0 ** 0.5
        softmax1 = ["wqf", "wkf", "wvf", "wof"]
        layers = [
            (moe, ("m0",)),
            (attention, ("a0", 8, "linear", "r0", 1.0, ["wq0", "wk0", "wv0"], False, False)),
            (moe, ("m1",)),
            (attention, ("f1", 4, "full", None, 0.5, softmax1, True, True)),
            (attention, ("a1", 8, "causal", "r1", ROOT8, ["wq1", "wk1", "wv1", "wo1"], True, False)),
            (attention, ("f2", 4, "full", None, 0.5, softmax1, True, True)),
            (ternary_mlp, ("t1",)),
            (attention, ("a2", 8, "causal", "r2", ROOT8, ["wq2", "wk2", "wv2", "wo2"], True, False)),
            (ternary_mlp, ("t2",)),
            (binary_mlp, ("b1",)),
            (lion, ("l3",)),
            (binary_mlp, ("b2",)),
        ]

        last_sems = sems("final", "out")

        def finish_sync(sp):
            sp.dma_start(out.rearrange("(n p) d -> p n d", p=P),
                         x.rearrange("p (n d) -> p n d", d=D)).then_inc(last_sems.out, 16)
            sp.wait_ge(last_sems.out, 16)

        def run(part):
            with nc.Block() as block:
                if "sync" in part:
                    block.sync(part["sync"])
                if "tensor" in part:
                    block.tensor(part["tensor"])
                if "scalar" in part:
                    block.scalar(part["scalar"])
                if "gpsimd" in part:
                    block.gpsimd(part["gpsimd"])
                if "vector" in part:
                    block.vector(part["vector"])
            nc.clear_and_free_semaphores(list(part["sems"]))
            nc.all_engine_barrier()

        run(dict(sync=boot_sync, tensor=boot_tensor, scalar=boot_scalar, vector=boot_vector,
                 sems=boot))
        for make, args in layers:
            run(make(*args))
        run(dict(sync=finish_sync, sems=last_sems))




def _layout(i):
    import numpy as np
    f = np.float32
    c = np.ascontiguousarray
    T = lambda w: c(np.asarray(w).T)
    o = {}
    o["x"] = c(np.asarray(i["L0_attn_x"]).reshape(TILES, P, D).transpose(1, 0, 2)).reshape(P, TILES * D)
    o["ident"] = np.eye(P, dtype=f)
    r, q = np.arange(P)[:, None], np.arange(P)[None, :]
    big = f(-1e30)
    o["masks"] = c(np.stack([np.where(q > r, big, f(0)), np.where(q < r, big, f(0)),
                             np.where(q >= r, f(1), f(0))], 1).astype(f))
    e = np.arange(EXPERTS)
    o["lower"] = np.tile((e[None, :] < e[:, None]).astype(f).reshape(1, -1), (P, 1))

    gu = np.asarray(i["L0_ffn_experts_gate_up"])
    dn = np.asarray(i["L0_ffn_experts_down"])
    sg, su, sd = (np.asarray(i["L0_ffn_shared_" + n + "_w"]) for n in ("gate", "up", "down"))
    G = [gu[k, :INTER] for k in range(EXPERTS)] + [sg[:INTER], sg[INTER:]]
    U = [gu[k, INTER:] for k in range(EXPERTS)] + [su[:INTER], su[INTER:]]
    Dn = [dn[k] for k in range(EXPERTS)] + [sd[:, :INTER], sd[:, INTER:]]
    up = np.zeros((UPS_, P, D), f)
    down = np.zeros((P, PAIRS * 3, D), f)
    for p in range(PAIRS):
        for h in range(2):
            w = 2 * p + h
            up[6 * p + 2 * h] = G[w][:P]
            up[6 * p + 2 * h + 1] = U[w][:P]
            up[6 * p + 4, 64 * h:64 * h + TAIL] = G[w][P:]
            up[6 * p + 5, 64 * h:64 * h + TAIL] = U[w][P:]
            down[:, 3 * p + h] = Dn[w][:, :P].T
            down[64 * h:64 * h + TAIL, 3 * p + 2] = Dn[w][:, P:].T
    o["up0"] = c(up.transpose(2, 0, 1)).reshape(D, UPS_ * P)
    o["down0"] = c(down).reshape(P, PAIRS * 3 * D)
    o["gate0"] = c(np.concatenate([np.asarray(i["L0_ffn_gate_w"]),
                                   np.asarray(i["L0_ffn_shared_expert_gate_w"])], 0).T)

    hd = 8
    feat = np.arange(D)
    inv = (f(1.0) / f(10000.0) ** (np.arange(0, hd, 2, dtype=f) / f(hd))).astype(f)
    ang = (np.arange(SEQ, dtype=f)[:, None] * inv[None, :]).astype(f)
    cos, sin = np.cos(ang).T.astype(f), np.sin(ang).T.astype(f)
    def by_dim(hd):
        return feat // (4 * hd) * 4 * hd + feat % 4 * hd + feat % (4 * hd) // 4

    by8, by4 = by_dim(8), by_dim(4)
    half_perm = feat // hd * hd + (feat % hd + hd // 2) % hd
    pair_perm = feat ^ 1
    sgn_half = np.where(feat % hd < hd // 2, f(-1), f(1))[:, None]
    sgn_pair = np.where(feat % 2 == 0, f(-1), f(1))[:, None]
    o["r0_tab"] = c(np.stack([cos[feat % (hd // 2)], sin[feat % (hd // 2)] * sgn_half], 1)[by8].astype(f))
    pair_tab = c(np.stack([cos[feat % hd // 2], sin[feat % hd // 2] * sgn_pair], 1)[by8].astype(f))
    o["r1_tab"] = o["r2_tab"] = pair_tab
    wqkv, bqkv = np.asarray(i["L0_attn_W_qkv"]), np.asarray(i["L0_attn_b_qkv"])
    o["wq0"], o["wk0"], o["wv0"] = (T(wqkv[k * D:(k + 1) * D]) for k in range(3))
    o["r0_wqs"], o["r0_wks"] = c(o["wq0"][:, half_perm[by8]]), c(o["wk0"][:, half_perm[by8]])
    for n in "qkvo":
        o[f"w{n}1"] = c(np.asarray(i["L1_attn_w" + n]))
        o[f"w{n}f"] = c(np.asarray(i["L1_ffn_w" + n]))
        o[f"w{n}2"] = T(i["L2_attn_W" + n])
        o[f"w{n}3"] = c(np.asarray(i[f"L3_attn_{n}_w"]))
    for k in "12":
        o[f"r{k}_wqs"], o[f"r{k}_wks"] = c(o["wq" + k][:, pair_perm[by8]]), c(o["wk" + k][:, pair_perm[by8]])
    for k, by in (("0", by8), ("1", by8), ("2", by8), ("f", by4)):
        o["wq" + k], o["wk" + k] = c(o["wq" + k][:, by]), c(o["wk" + k][:, by])

    o["w1_1"] = c(np.asarray(i["L1_ffn_w1"]).transpose(1, 0, 2)).reshape(D, EXPERTS * FF)
    o["w2_1"] = c(np.asarray(i["L1_ffn_w2"]).reshape(EXPERTS, FT, P, D).transpose(2, 0, 1, 3))\
        .reshape(P, EXPERTS * FT * D)
    o["fc2"] = T(i["L2_ffn_W_fc"])
    o["pj2"] = c(np.asarray(i["L2_ffn_W_proj"]).T.reshape(FT, P, D).transpose(1, 0, 2)).reshape(P, FF)
    o["w13"] = T(i["L3_ffn_w1"])
    o["w23"] = c(np.asarray(i["L3_ffn_w2"]).T.reshape(FT, P, D).transpose(1, 0, 2)).reshape(P, FF)
    o["wd3"] = c(np.asarray(i["L3_attn_dec_w"])[:, feat // hd])
    o["wv3"] = c(np.stack([o["wv3"][:, feat // hd * hd + k] for k in range(hd)], 1))
    o["f13"] = c(np.asarray(i["L3_attn_f1_w"]))
    o["f23"] = c(np.asarray(i["L3_attn_f2_w"]).reshape(FT, P, D).transpose(1, 0, 2))
    o["rows3"] = np.concatenate([np.asarray(i["L3_attn_o_b"]), np.asarray(i["L3_attn_f2_b"])])[None]
    h_of, e_of = feat // hd, feat % hd
    same = (h_of[:, None] == h_of[None, :]).astype(f)
    o["same"] = same
    o["sel"] = c(np.stack([same * (e_of == k)[None, :].astype(f) for k in range(8)], 1))

    b = {"b_q": bqkv[:D][by8], "b_qs": bqkv[:D][half_perm[by8]], "b_k": bqkv[D:2 * D][by8],
         "b_ks": bqkv[D:2 * D][half_perm[by8]], "ln_g": i["L1_ffn_ln_g"], "ln_b": i["L1_ffn_ln_b"]}
    parts = [np.asarray(b[n]).reshape(P, 1) for n in ("b_q", "b_qs", "b_k", "b_ks", "ln_g", "ln_b")]
    parts.append(np.asarray(i["L1_ffn_b1"]).reshape(EXPERTS * FT, P).T)
    for n in ("L3_ffn_b1", "L2_ffn_ln_w", "L2_ffn_ln_b", "L3_attn_f1_b"):
        parts.append(np.asarray(i[n]).reshape(FT, P).T)
    parts += [np.asarray(i[f"L3_attn_{n}_b"]).reshape(P, 1) for n in "qk"]
    parts.append(np.repeat(np.asarray(i["L3_attn_dec_b"]), 8).reshape(P, 1))
    parts.append(np.repeat(np.asarray(i["L3_attn_v_b"]).reshape(16, 8), 8, 0))
    parts += [np.asarray(i["L3_attn_ln" + n]).reshape(P, 1) for n in ("1_w", "1_b", "2_w", "2_b")]
    o["cols"] = c(np.concatenate(parts, 1).astype(f))
    o["rows"] = c(np.concatenate([np.asarray(i["L1_ffn_b2"]).reshape(-1), np.asarray(i["L3_ffn_b2"]),
                                  bqkv[2 * D:]])[None])
    return o


UPS_ = 6 * PAIRS


def kernel(**inputs):
    import numpy as _np
    import concourse.bacc as _bacc
    from concourse.bass_utils import run_bass_kernel_spmd as _run

    nc = _bacc.Bacc("TRN2", target_bir_lowering=False, num_devices=1)
    arrays, aps = {}, {}
    for name, v in _layout(inputs).items():
        v = _np.ascontiguousarray(v)
        arrays["in_" + name] = v
        aps[name] = nc.dram_tensor("in_" + name, v.shape, mybir.dt.from_np(v.dtype),
                                   kind="ExternalInput").ap()
    out = nc.dram_tensor("out_x", (TOKENS, D), F32, kind="ExternalOutput").ap()
    macaron(nc, aps, out)
    r = _run(nc, [arrays], core_ids=[0])
    return r.results[0]["out_x"].reshape(BATCH, SEQ, D)
```

```python
import struct
from collections import namedtuple
from contextlib import ExitStack

import concourse.bass as bass
from concourse import mybir

F32 = mybir.dt.float32
BF16 = mybir.dt.bfloat16
ACT = mybir.ActivationFunctionType
ALU = mybir.AluOpType
AXX = mybir.AxisListType.X

P = 128
D = 128
BATCH, SEQ = 2, 1024
TOKENS = BATCH * SEQ
TILES = TOKENS // P
CHUNK = 512
CHUNKS = TOKENS // CHUNK
TPC = CHUNK // P
KB = SEQ // P
EPS = 1e-5
GROUP = 4

EXPERTS, INTER = 8, 176
WAYS = EXPERTS + 2
PAIRS = WAYS // 2
TAIL = INTER - P
FF = 512
FT = FF // P

TP = 0

MINUS_ONES = struct.unpack("<f", bytes([0x80, 0xBF, 0x80, 0xBF]))[0]


class Tally:

    def __init__(self, sem, base=0):
        self.sem, self.base, self.n = sem, base, 0

    def done(self, ins):
        ins.then_inc(self.sem, 1)
        self.n += 1

    def settle(self, eng, ins):
        self.done(ins)
        eng.wait_ge(self.sem, self.base + self.n)


def Sems(nc, tag, names):
    names = names.split()
    return namedtuple("Sems", names)(*[nc.alloc_semaphore(name=f"{tag}_{n}") for n in names])


def macaron(nc, a, out):
    with ExitStack() as ctx:
        def sb(name, shape, dt=F32):
            return ctx.enter_context(nc.sbuf_tensor(name, shape, dt))[tuple([slice(None)] * len(shape))]

        def dram(name, shape, dt=F32):
            return nc.dram_tensor(name, shape, dt, kind="Internal").ap()

        def sems(tag, names):
            return Sems(nc, tag, names)

        ps = ctx.enter_context(nc.psum_tensor("ps", [P, 8, 512], F32))[:, :, :]

        x = sb("x", [P, TILES * D])
        xnT = sb("xnT", [P, TOKENS])
        res = sb("res", [P, TILES * D])
        xn = sb("xn", [P, 2, TPC, D])
        stat = sb("stat", [P, CHUNKS, TPC, 6])
        mv = sb("mv", [P, CHUNKS, TPC, 2])
        var = sb("var", [P, CHUNKS, TPC])
        rstd = sb("rstd", [P, CHUNKS, TPC])
        neghalf = sb("neghalf", [P, TPC])

        ident = sb("ident", [P, P])
        identb = sb("identb", [P, P], BF16)
        masks = sb("masks", [P, 3, P])
        maskb = sb("maskb", [P, 2, P], BF16)
        ones = sb("ones", [P, P])
        lower = sb("lower", [P, EXPERTS * EXPERTS])
        cols = sb("cols", [P, 96])
        rows = sb("rows", [1, 10 * D])

        w2fc = sb("w2fc", [P, FF])
        w2pj = sb("w2pj", [P, FT, D])
        w3a = sb("w3a", [P, FF])
        w3b = sb("w3b", [P, FT, D])
        wproj = sb("wproj", [P, 2, 4, D])

        wprs = sb("wprs", [P, 2, D])

        WEIGHTS = dict(a0=("wq0 wk0 wv0", "r0"), f1=("wqf wkf wvf wof", None),
                       a1=("wq1 wk1 wv1 wo1", "r1"), f2=("wqf wkf wvf wof", None),
                       a2=("wq2 wk2 wv2 wo2", "r2"))
        WEIGHTS_AT = dict(a0=0, f1=1, a1=0, f2=1, a2=0)

        def load_projections(sp, sem, tag):
            names, rope = WEIGHTS[tag]
            for k, name in enumerate(names.split()):
                sp.dma_start(wproj[:, WEIGHTS_AT[tag], k, :], a[name]).then_inc(sem, 16)
            if rope:
                sp.dma_start(wprs[:, 0, :], a[rope + "_wqs"]).then_inc(sem, 16)
                sp.dma_start(wprs[:, 1, :], a[rope + "_wks"]).then_inc(sem, 16)
            return 16 * (len(names.split()) + (2 if rope else 0))

        ARENA = 31 * 1024
        arena = sb("arena", [P, ARENA])

        class Carve:
            def __init__(self):
                self.at = 0

            def __call__(self, n, dt=F32):
                words = n if dt == F32 else n // 2
                view = arena[:, self.at:self.at + words]
                self.at += words
                assert self.at <= ARENA, self.at
                return view if dt == F32 else view.bitcast(dt)

        names = ["b_q", "b_qs", "b_k", "b_ks", "ln_g", "ln_b"]
        col_at = {n: i for i, n in enumerate(names)}
        n_cols = len(names)
        for n, k in (("b_v", 0), ("b1_l1", EXPERTS * FT), ("l3w_b1", FT), ("l2_w", FT), ("l2_b", FT),
                     ("l3_f1b", FT), ("l3_qb", 1), ("l3_kb", 1), ("l3_db", 1), ("l3_vb", 8),
                     ("l3_g1", 1), ("l3_o1", 1), ("l3_g2", 1), ("l3_o2", 1), ("scr", 4)):
            col_at[n] = n_cols
            n_cols += k
        assert n_cols <= 96, n_cols

        def col(name, k=0):
            return cols[:, col_at[name] + k:col_at[name] + k + 1]

        def row(k):
            return rows[0:1, k * D:(k + 1) * D]

        ROW_B2, ROW_L3B2 = 0, 8

        boot = sems("boot", "const gsum gabs bsign bw vec pool stats rstd")
        def norm_stats(dve, s, t, src, g):
            b = g % CHUNKS
            for n in range(TPC):
                last = nc.vector.bn_stats(stat[:, b, n, :], src(n))
            t.settle(dve, last)
            for n in range(TPC):
                last = nc.vector.bn_aggr(mv[:, b, n, :], stat[:, b, n, :])
            last.then_inc(s.stats, 1)

        def norm_apply(dve, s, src, dst, g):
            b = g % CHUNKS
            dve.wait_ge(s.rstd, g + 1)
            for n in range(TPC):
                last = nc.vector.tensor_scalar(dst(n), src(n), mv[:, b, n, 0:1],
                                               rstd[:, b, n:n + 1], ALU.subtract, ALU.mult)
            return last

        def norm_chunk(dve, s, t, rows_of, ch, g0=0, k0=0):
            if ch == 0 and g0:
                norm_stats(dve, s, t, rows_of(0), g0)
            if ch == 0 and not g0:
                dve.sem_inc(s.stats, 1)
                dve.sem_inc(s.xn, 1)
            if ch + 1 < CHUNKS:
                norm_stats(dve, s, t, rows_of(ch + 1), g0 + ch + 1)
            k = k0 + ch
            if g0 + ch == 0:
                return
            if k >= 2:
                dve.wait_ge(s.tp, k - 1)
            norm_apply(dve, s, rows_of(ch), lambda n: xn[:, k % 2, n, :], g0 + ch).then_inc(s.xn, 1)

        def norm_outer(dve, s, t, ch):
            if ch == 0:
                dve.sem_inc(s.stats, 1)
            else:
                t.settle(dve, norm_apply(dve, s, x_rows(ch), res_rows(ch), 2 * ch))
            norm_stats(dve, s, t, res_rows(ch), 2 * ch + 1)
            if ch + 1 < CHUNKS:
                norm_stats(dve, s, t, x_rows(ch + 1), 2 * ch + 2)

        def norm_inner(dve, s, ch):
            if ch >= 2:
                dve.wait_ge(s.tp, ch - 1)
            norm_apply(dve, s, res_rows(ch), lambda n: xn[:, ch % 2, n, :], 2 * ch + 1)\
                .then_inc(s.xn, 1)

        def x_rows(ch):
            return lambda n: x[:, ch * CHUNK + n * D:ch * CHUNK + (n + 1) * D]

        def res_rows(ch):
            return lambda n: res[:, ch * CHUNK + n * D:ch * CHUNK + (n + 1) * D]

        def ahead_stats(dve, s, t, g, after):
            if after:
                norm_stats(dve, s, t, x_rows(0), g)

        def ahead_apply(dve, s, g, after, turned=CHUNKS):
            if after and turned:
                dve.wait_ge(s.tp, turned)
            if after:
                norm_apply(dve, s, x_rows(0),
                           res_rows(0) if after == "outer" else lambda n: xn[:, 0, n, :], g)

        def norm_gpsimd(pool, s, t, g):
            if g == 0:
                pool.sem_inc(s.rstd, 1)
                return
            rstd_gpsimd(pool, s, t, g)

        def rstd_gpsimd(pool, s, t, g):
            b = g % CHUNKS
            pool.wait_ge(s.stats, g + 1)
            t.settle(pool, nc.gpsimd.tensor_scalar(var[:, b, :], mv[:, b, :, 1], EPS, None, ALU.add))
            nc.gpsimd.tensor_tensor(rstd[:, b, :], var[:, b, :], neghalf[:, :], ALU.pow)\
                .then_inc(s.rstd, 1)

        def norm_tensor(pe, s, k, bank=TP):
            pe.wait_ge(s.xn, k + 1)
            if k:
                pe.wait_ge(s.xT, k)
            for n in range(TPC):
                last = nc.tensor.transpose(ps[:, bank, n * P:(n + 1) * P], xn[:, k % 2, n, :],
                                           ident[:, :])
            last.then_inc(s.tp, 1)

        UPS = 6 * PAIRS
        ALL_PAIRS = CHUNKS * PAIRS
        RING, FIRST_UP, FIRST_Y = 5, 1, 6
        GATE = 7

        def moe(tag, after):
            c = Carve()
            up_w = c(UPS * P)
            dn_w = c(PAIRS * 3 * D)
            gate_w = c(EXPERTS + 1)
            hid = c(6 * CHUNK).rearrange("p (n t) -> p n t", n=6)
            sg = c(3 * CHUNK).rearrange("p (n t) -> p n t", n=3)
            gT = c(TOKENS)
            lg = c(TILES * 9).rearrange("p (n e) -> p n e", e=9)
            ex = c(TILES * 9).rearrange("p (n e) -> p n e", e=9)
            mx = c(TILES)
            den = c(TILES)
            cmp = c(TILES * 64).rearrange("p (n e f) -> p n e f", e=8, f=8)
            eq = c(TILES * 64).rearrange("p (n e f) -> p n e f", e=8, f=8)
            rank = c(TILES * 8).rearrange("p (n e) -> p n e", e=8)
            wts = c(TILES * WAYS).rearrange("p (n e) -> p n e", e=WAYS)
            s = sems(tag, "wg wu wd stats rstd xn tp xT vec pool gmm gcopy gtp shift gexp up silu h y "
                          "yused")

            def sync(sp):
                sp.dma_start(gate_w, a["gate0"]).then_inc(s.wg, 16)
                sp.dma_start(up_w, a["up0"]).then_inc(s.wu, 16)
                sp.dma_start(dn_w, a["down0"]).then_inc(s.wd, 16)

            def tensor(pe):
                def up(q, first, end):
                    ch = q // PAIRS
                    for k in range(first, end):
                        tile = 6 * q + k
                        before = tile - RING
                        if before >= 0 and before % 2 == 0:
                            pe.wait_ge(s.silu, before // 2 + 1)
                        elif before >= 0:
                            pe.wait_ge(s.h, before // 2 + 1)
                        w = (q % PAIRS * 6 + k) * P
                        nc.tensor.matmul(ps[:, FIRST_UP + tile % RING, :], up_w[:, w:w + P],
                                         xnT[:, ch * CHUNK:(ch + 1) * CHUNK], start=True, stop=True)\
                            .then_inc(s.up, 1)

                def down(q):
                    p = q % PAIRS
                    pe.wait_ge(s.h, 3 * q + 3)
                    if q == 0:
                        pe.wait_ge(s.shift, 1)
                    for half in range(2):
                        if q:
                            pe.wait_ge(s.yused, 2 * (q - 1) + half + 1)
                        bank = FIRST_Y + half
                        r = slice(64 * half, 64 * half + 64)
                        for n in range(TPC):
                            t = slice(n * P, (n + 1) * P)
                            nc.tensor.matmul(ps[:, bank, t], hid[:, 3 * (q % 2) + half, t],
                                             dn_w[:, (3 * p + half) * D:(3 * p + half + 1) * D],
                                             start=True, stop=False)
                            last = nc.tensor.matmul(ps[:, bank, t], hid[r, 3 * (q % 2) + 2, t],
                                                    dn_w[r, (3 * p + 2) * D:(3 * p + 3) * D],
                                                    start=False, stop=True)
                        last.then_inc(s.y, 1)

                pe.wait_ge(s.wg, 16)
                norm_tensor(pe, s, 0)
                for ch in range(CHUNKS):
                    pe.wait_ge(s.xT, ch + 1)
                    if ch:
                        pe.wait_ge(s.gcopy, ch)
                    nc.tensor.matmul(ps[0:9, GATE, :], gate_w, xnT[:, ch * CHUNK:(ch + 1) * CHUNK],
                                     start=True, stop=True).then_inc(s.gmm, 1)
                    if ch + 1 < CHUNKS:
                        norm_tensor(pe, s, ch + 1)
                    if ch == 1:
                        pe.wait_ge(s.wu, 16)
                    if 1 <= ch < 3:
                        up(0, 2 * ch - 2, 2 * ch)
                for ch in range(CHUNKS):
                    pe.wait_ge(s.gcopy, ch + 1)
                    for n in range(ch * TPC, (ch + 1) * TPC):
                        last = nc.tensor.transpose(ps[:, FIRST_Y, n * 16:n * 16 + 9],
                                                   gT[0:9, n * P:(n + 1) * P], ident[0:9, 0:9])
                last.then_inc(s.gtp, 1)
                up(0, 4, 6)
                pe.wait_ge(s.wd, 16)
                for q in range(ALL_PAIRS):
                    if q + 1 < ALL_PAIRS:
                        up(q + 1, 0, 6)
                    down(q)

            def scalar(act):
                for ch in range(CHUNKS):
                    t = slice(ch * CHUNK, (ch + 1) * CHUNK)
                    act.wait_ge(s.tp, ch + 1)
                    nc.scalar.activation(xnT[:, t], ps[:, TP, :], ACT.Copy).then_inc(s.xT, 1)
                    act.wait_ge(s.gmm, ch + 1)
                    nc.scalar.activation(gT[0:9, t], ps[0:9, GATE, :], ACT.Copy).then_inc(s.gcopy, 1)
                act.wait_ge(s.shift, 1)
                nc.scalar.activation(ex, lg, ACT.Exp).then_inc(s.gexp, 1)
                for n in range(3 * ALL_PAIRS):
                    act.wait_ge(s.up, 2 * n + 1)
                    if n >= 3:
                        act.wait_ge(s.h, n - 2)
                    nc.scalar.activation(sg[:, n % 3, :], ps[:, FIRST_UP + (2 * n) % RING, :],
                                         ACT.Silu).then_inc(s.silu, 1)

            def gpsimd(pool):
                t = Tally(s.pool)
                for ch in range(CHUNKS):
                    norm_gpsimd(pool, s, t, ch)
                if after:
                    rstd_gpsimd(pool, s, t, CHUNKS)

            def vector(dve):
                t = Tally(s.vec)
                for ch in range(CHUNKS):
                    norm_chunk(dve, s, t, x_rows, ch)
                dve.wait_ge(s.gtp, 1)
                zp = ps[:, FIRST_Y, 0:TILES * 16].rearrange("p (n e) -> p n e", e=16)
                nc.vector.tensor_reduce(mx, zp[:, :, 0:8], AXX, ALU.max)
                t.settle(dve, nc.vector.tensor_scalar(lg[:, :, 8:9], zp[:, :, 8:9], -1.0, None,
                                                      ALU.mult))
                nc.vector.tensor_tensor(lg[:, :, 0:8], zp[:, :, 0:8],
                                        mx.unsqueeze(2).to_broadcast([P, TILES, 8]),
                                        ALU.subtract).then_inc(s.shift, 1)
                dve.wait_ge(s.gexp, 1)
                t.settle(dve, nc.vector.tensor_reduce(den, ex[:, :, 0:8], AXX, ALU.add))
                t.settle(dve, nc.vector.reciprocal(den, den))
                t.settle(dve, nc.vector.tensor_tensor(
                    ex[:, :, 0:8], ex[:, :, 0:8], den.unsqueeze(2).to_broadcast([P, TILES, 8]),
                    ALU.mult))
                e_of = ex[:, :, 0:8].unsqueeze(3).to_broadcast([P, TILES, 8, 8])
                f_of = ex[:, :, 0:8].unsqueeze(2).to_broadcast([P, TILES, 8, 8])
                low = lower.rearrange("p (e f) -> p e f", e=8).unsqueeze(1)\
                    .to_broadcast([P, TILES, 8, 8])
                nc.vector.tensor_tensor(cmp, f_of, e_of, ALU.is_gt)
                t.settle(dve, nc.vector.tensor_tensor(eq, f_of, e_of, ALU.is_equal))
                t.settle(dve, nc.vector.tensor_tensor(eq, eq, low, ALU.mult))
                t.settle(dve, nc.vector.tensor_tensor(
                    cmp.rearrange("p n e f -> p (n e f)"), cmp.rearrange("p n e f -> p (n e f)"),
                    eq.rearrange("p n e f -> p (n e f)"), ALU.add))
                t.settle(dve, nc.vector.tensor_reduce(rank, cmp, AXX, ALU.add))
                t.settle(dve, nc.vector.tensor_scalar(rank, rank, 1.5, 0.5, ALU.is_lt, ALU.mult))
                nc.vector.tensor_tensor(wts[:, :, 0:8], rank, ex[:, :, 0:8], ALU.mult)
                t.settle(dve, nc.vector.tensor_scalar(wts[:, :, 8:9], ex[:, :, 8:9], 1.0, 2.0,
                                                      ALU.add, ALU.mult))
                t.settle(dve, nc.vector.reciprocal(wts[:, :, 8:9], wts[:, :, 8:9]))
                t.settle(dve, nc.vector.tensor_copy(wts[:, :, 9:10], wts[:, :, 8:9]))

                def gated(q):
                    for n in range(3 * q, 3 * q + 3):
                        dve.wait_ge(s.silu, n + 1)
                        dve.wait_ge(s.up, 2 * n + 2)
                        if n % 3 == 0 and q >= 2:
                            dve.wait_ge(s.y, 2 * q - 2)
                        nc.vector.tensor_tensor(hid[:, n % 6, :], sg[:, n % 3, :],
                                                ps[:, FIRST_UP + (2 * n + 1) % RING, :], ALU.mult)\
                            .then_inc(s.h, 1)

                def add(q, half):
                    way = 2 * (q % PAIRS) + half
                    dve.wait_ge(s.y, 2 * q + half + 1)
                    if way:
                        dve.wait_ge(s.yused, 2 * q + half)
                    for n in range(TPC):
                        tile = q // PAIRS * TPC + n
                        xt = x[:, tile * D:(tile + 1) * D]
                        last = nc.vector.scalar_tensor_tensor(
                            xt, ps[:, FIRST_Y + half, n * P:(n + 1) * P],
                            wts[:, tile, way:way + 1], xt, ALU.mult, ALU.add)
                    last.then_inc(s.yused, 1)

                gated(0)
                for q in range(ALL_PAIRS):
                    if q + 1 < ALL_PAIRS:
                        gated(q + 1)
                    if q == ALL_PAIRS - 3:
                        dve.wait_ge(s.yused, 2 * PAIRS)
                        ahead_stats(dve, s, t, CHUNKS, after)
                    if q == ALL_PAIRS - 2:
                        ahead_apply(dve, s, CHUNKS, after)
                    add(q, 0)
                    add(q, 1)

            return dict(sync=sync, tensor=tensor, scalar=scalar, gpsimd=gpsimd, vector=vector, sems=s)

        S_SLOT = 0
        ST_RING = 4
        O_BANK = 7
        TURNED, PROJ, VALUES = 4, 5, 7

        def attention(tag, after, hd, full, rope, scale, double):
            heads = D // hd
            HG = heads // GROUP
            UNITS = BATCH * HG
            R = 9 * hd
            MAX_ROW = 96
            rows4 = GROUP * hd
            halves = []
            for qc in range(2):
                kbs = range(KB) if full else range(4 * qc + 4)
                halves.append([(qc, kb, 0 if full or kb < 4 * qc else (kb - 4 * qc) * P)
                               for kb in kbs])
            steps = halves[0] + halves[1]
            NS = len(steps)
            ends = [len(halves[0]) - 1, NS - 1]
            TURN = 4 if full else 2
            TURNS = (TURN, 17 + TURN)

            def position(half, k):
                return 17 * half + k + (k >= TURN)

            def turn_step(qc):
                return TURN * len(halves[qc]) // 16

            qs = dram(f"{tag}_q", [UNITS, 3, rows4, SEQ], BF16)
            ks = dram(f"{tag}_k", [UNITS, 3, rows4, SEQ], BF16)
            mt = dram(f"{tag}_m", [2, 3, GROUP * CHUNK], BF16)
            ot = dram(f"{tag}_o", [UNITS * GROUP * (hd + 1), SEQ])

            c = Carve()
            wp = wproj[:, WEIGHTS_AT[tag]]
            if double:
                w1 = c(EXPERTS * FF)
                w2 = c(EXPERTS * FF)
            v_sb = c(UNITS * KB * rows4)
            v_un = v_sb.rearrange("p (u k r) -> p u k r", u=UNITS, k=KB)
            ops_at = c.at
            Qop = [c(GROUP * SEQ, BF16).rearrange("p (j t) -> p j t", j=GROUP) for _ in range(3)]
            Kop = [c(GROUP * SEQ, BF16).rearrange("p (j t) -> p j t", j=GROUP) for _ in range(3)]
            base = c.at
            pr = c(8 * CHUNK).rearrange("p (n t) -> p n t", n=8)
            vx = [c(KB * GROUP * 32).rearrange("p (k j c) -> p k j c", k=KB, j=GROUP) for _ in range(3)]
            osb = c(2 * CHUNK).rearrange("p (n t) -> p n t", n=2)
            mq = c(2 * 16).rearrange("p (n m) -> p n m", n=2)
            mT = c(P)
            mr = c(P)
            ms = c(2 * 3 * P, BF16).rearrange("p (n a t) -> p n a t", n=2, a=3)
            c.at = base
            tab = c(2 * SEQ).rearrange("p (n t) -> p n t", n=2)
            rot = c(2 * CHUNK).rearrange("p (n t) -> p n t", n=2)
            rem = c(2 * CHUNK).rearrange("p (n t) -> p n t", n=2)
            cut = [c(3 * CHUNK, BF16).rearrange("p (a t) -> p a t", a=3) for _ in range(2)]
            num, den = xnT, hid2

            s = sems(tag, "we tab stats rstd xn tp xT vec pool proj rope cut0 rem1 cut1 cut2 qst0 kst0 qst1 kst1 "
                          "vps vcp ops0 ops1 ops2 kneg vset vx s sread mtp mcp mps ml0 ml1 mst0 mst1 st ex msk "
                          "av ocp ost0 ost1 nl0 nl1 nl2 nl3 oT y x up gel")
            cut_stored = ((s.qst0, s.kst0), (s.qst1, s.kst1))
            operands = (s.ops0, s.ops1, s.ops2)
            max_placed = (s.ml0, s.ml1)
            max_stored = (s.mst0, s.mst1)
            sums_stored = (s.ost0, s.ost1)
            sums_loaded = (s.nl0, s.nl1, s.nl2, s.nl3)
            N_OPS = 4

            def words(op):
                return op.rearrange("p j t -> p (j t)").bitcast(F32)

            def sync(sp):
                if rope:
                    sp.dma_start(tab, a[rope + "_tab"]).then_inc(s.tab, 16)
                def load(u, par):
                    q, k = (w.rearrange("u a (d j) t -> u a d (j t)", j=GROUP) for w in (qs, ks))
                    sp.dma_start(Qop[par][0:R], q.rearrange("u a d t -> u (a d) t")[bass.ds(u, 1)]
                                 .to_broadcast([3, 3 * hd, GROUP * SEQ])).then_inc(operands[par], 16)
                    for n in range(3):
                        sp.dma_start(Kop[par][3 * n * hd:3 * (n + 1) * hd], k[bass.ds(u, 1), n]
                                     .to_broadcast([3, hd, GROUP * SEQ])).then_inc(operands[par], 16)

                def put_max(u, par, qc):
                    sp.wait_ge(s.mps, 2 * u + qc + 1)
                    sp.dma_start(mt[qc].rearrange("i (r t) -> r i t", t=P), ms[0:16, qc, :, :])\
                        .then_inc(max_stored[qc], 16)
                    sp.wait_ge(max_stored[qc], 16 * (u + 1))
                    sp.dma_start(Qop[par][MAX_ROW:MAX_ROW + 3, :, qc * CHUNK:(qc + 1) * CHUNK],
                                 mt[qc].rearrange("i (j t) -> i j t", j=GROUP))\
                        .then_inc(max_placed[qc], 16)

                def store(u, qc):
                    sp.wait_ge(s.ocp, 2 * u + qc + 1 + 1)
                    for j in range(GROUP):
                        sp.dma_start(ot[bass.ds((u * GROUP + j) * (hd + 1), hd + 1),
                                        qc * CHUNK:(qc + 1) * CHUNK],
                                     osb[32 * j:32 * j + hd + 1, qc, :]).then_inc(sums_stored[qc], 16)

                def unit(u, third, par, ahead2, ahead1):
                    put_max(u, par, 1)
                    if ahead2:
                        sp.wait_ge(s.st, u * 4 * NS + 1)
                        load(u + 2, (par + 2) % 3)
                    store(u, 0)
                    if not ahead1:
                        sp.wait_ge(s.ost0, 64 * UNITS + 1)
                        load_sums(2)
                    if ahead1:
                        put_max(u + 1, (par + 1) % 3, 0)
                    store(u, 1)
                    if ahead1 and not ahead2:
                        sp.wait_ge(s.ost0, 64 * (UNITS - 1) + 1)
                        sp.wait_ge(s.ost1, 64 * (UNITS - 1) + 1)
                        load_sums(0)
                        load_sums(1)

                def load_sums(ch):
                    b, half = divmod(ch, 2)
                    src = ot.rearrange("(b h d) t -> b h d t", b=BATCH, d=hd + 1)[b][
                        :, :, half * CHUNK:(half + 1) * CHUNK]
                    r = slice(ch * CHUNK, (ch + 1) * CHUNK)
                    sp.dma_start(num[:, r], src[:, 0:hd, :]).then_inc(sums_loaded[ch], 16)
                    sp.dma_start(den[:, r], src[:, hd:hd + 1, :].to_broadcast([heads, hd, CHUNK]))\
                        .then_inc(sums_loaded[ch], 16)

                for ch in range(CHUNKS):
                    b, t0 = ch // 2, (ch % 2) * CHUNK
                    for side, to in ((0, qs), (1, ks)):
                        sp.wait_ge(s.cut2, 2 * ch + side + 1)
                        for part in range(3):
                            sp.dma_start(to[b * HG:(b + 1) * HG, part, :, t0:t0 + CHUNK],
                                         cut[side][:, part, :]).then_inc(cut_stored[b][side], 16)
                    if ch == 1:
                        sp.wait_ge(s.qst0, 16 * 3 * CHUNKS // BATCH)
                        sp.wait_ge(s.kst0, 16 * 3 * CHUNKS // BATCH)
                        sp.wait_ge(s.kneg, 1)
                        load(0, 0)
                    if ch == 2:
                        put_max(0, 0, 0)
                sp.wait_ge(s.kneg, 2)
                load(1, 1)
                sp.wait_ge(s.kneg, 3)
                if double:
                    sp.dma_start(w1, a["w1_1"]).then_inc(s.we, 16)
                    sp.dma_start(w2, a["w2_1"]).then_inc(s.we, 16)
                sp.wait_ge(s.qst1, 16 * 3 * CHUNKS // BATCH)
                sp.wait_ge(s.kst1, 16 * 3 * CHUNKS // BATCH)
                loops(sp, unit)
                sp.wait_ge(s.ost1, 64 * UNITS + 1)
                load_sums(3)

            def loops(eng, unit):
                whole = (UNITS - 2) // 3
                with eng.Fori(0, whole) as i:
                    for par in range(3):
                        unit(i * 3 + par, i, par, True, True)
                for u in range(3 * whole, UNITS):
                    unit(u, u // 3, u % 3, u + 2 < UNITS, u + 1 < UNITS)

            def s_tasks(half):
                return [(j, qb) for qb in range(4) for j in range(GROUP)]

            def tensor(pe):
                def project(ch):
                    pe.wait_ge(s.xT, ch + 1)
                    t = slice(ch * CHUNK, (ch + 1) * CHUNK)
                    for side in range(2):
                        if rope:
                            if ch or side:
                                pe.wait_ge(s.rope, 2 * ch + side)
                            nc.tensor.matmul(ps[:, PROJ, :], wp[:, side, :], xnT[:, t],
                                             start=True, stop=True)
                            last = nc.tensor.matmul(ps[:, PROJ + 1, :], wprs[:, side, :],
                                                    xnT[:, t], start=True, stop=True)
                        else:
                            if ch:
                                pe.wait_ge(s.rem1, 2 * (ch - 1) + side + 1)
                            last = nc.tensor.matmul(ps[:, PROJ + side, :], wp[:, side, :],
                                                    xnT[:, t], start=True, stop=True)
                        last.then_inc(s.proj, 1)
                        if side == (1 if rope else 0):
                            continue
                        if ch + 1 < CHUNKS:
                            norm_tensor(pe, s, ch + 1, TURNED)
                        if ch:
                            pe.wait_ge(s.vcp, ch)
                        for n in range(TPC):
                            last = nc.tensor.matmul(ps[:, VALUES, n * P:(n + 1) * P],
                                                    xnT[:, ch * CHUNK + n * P:ch * CHUNK + (n + 1) * P],
                                                    wp[:, 2, :], start=True, stop=True)
                        last.then_inc(s.vps, 1)

                def slot(pos):
                    b = S_SLOT + 2 * (pos % 2)
                    return ps[:, b:b + 2, :]

                def wait_slot(u, pos):
                    q = pos - 2
                    uu = u if q >= 0 else u - 1
                    q %= 34
                    if q in TURNS:
                        pe.wait_ge(s.mcp, 2 * uu + (3 if q == TURNS[1] else 2))
                    else:
                        half, k = divmod(q, 17)
                        pe.wait_ge(s.sread, (uu + 1) * 32 + 16 * half + k - (k > TURN) + 1)

                def scores(u, par, half, k, fresh=False):
                    j, qb = s_tasks(half)[k]
                    pos = position(half, k)
                    if not (fresh and pos < 2):
                        wait_slot(u, pos)
                    q0 = half * CHUNK + qb * P
                    width = SEQ if full else q0 + P
                    at = slot(pos)
                    for k0 in range(0, width, CHUNK):
                        n = min(CHUNK, width - k0)
                        last = nc.tensor.matmul(at[:, k0 // CHUNK, 0:n], Qop[par][0:MAX_ROW, j, q0:q0 + P],
                                                Kop[par][0:MAX_ROW, j, k0:k0 + n], start=True,
                                                stop=full or k0 + n < width)
                    if not full:
                        off = (width - P) % CHUNK
                        last = nc.tensor.matmul(at[:, (width - 1) // CHUNK, off:off + P], identb[:, :],
                                                maskb[:, 0, :], start=False, stop=True)
                    last.then_inc(s.s, 1)

                def turn_max(u, pos, hn, fresh=False):
                    if not fresh:
                        wait_slot(u, pos)
                    pe.wait_ge(s.sread, 16 * (hn + 1))
                    nc.tensor.transpose(slot(pos)[0:16, 0, 0:P], mq[:, TURNS.index(pos) ^ 1, :],
                                        ident[:, :]).then_inc(s.mtp, 1)

                def attend(u, vpar, at):
                    qc, kb, off = steps[at]
                    pe.wait_ge(s.ex, u * 4 * NS + 4 * at + 4 + 3)
                    if kb == 0:
                        pe.wait_ge(s.vx, u + 1)
                        pe.wait_ge(s.ocp, 2 * u + qc + 1)
                    for j in range(GROUP):
                        last = nc.tensor.matmul(ps[32 * j:32 * j + 32, O_BANK, off:CHUNK],
                                                vx[vpar][:, kb, j, :],
                                                pr[:, (at % 2) * 4 + j, off:CHUNK],
                                                start=kb == 0, stop=at in ends,
                                                tile_position=(0, 32 * j), skip_group_check=True)
                    last.then_inc(s.av, 1)

                def unit(u, third, par, ahead2, ahead1):
                    for at, (qc, kb, off) in enumerate(steps):
                        if kb == 0:
                            pe.wait_ge(max_placed[qc], 16 * (u + 1) + 1)
                        if at == 0 and ahead1:
                            pe.wait_ge(operands[(par + 1) % 3], 16 * N_OPS * (third + 1 + par // 2))
                        todo = []
                        if ahead1:
                            per = 16 // len(halves[qc])
                            for k in range(per * kb, per * kb + per):
                                if k == TURN:
                                    todo.append(("turn", TURNS[qc], 2 * u + 1 + qc))
                                todo.append(("s", qc, k))
                        elif qc == 0 and kb == 0:
                            todo.append(("turn", TURNS[0], 2 * u + 1))

                        def run(task):
                            if task[0] == "turn":
                                turn_max(u, task[1], task[2], not ahead1)
                            else:
                                scores(u, (par + 1) % 3, task[1], task[2])

                        for j in range(GROUP):
                            n = (par * 4 * NS + 4 * at + j) % 3
                            pe.wait_ge(s.ex, u * 4 * NS + 4 * at + j + 1)
                            diag = not full and kb >= 4 * qc
                            last = nc.tensor.matmul(
                                ps[:, ST_RING + n, off:CHUNK], Kop[par][:, j, kb * P:(kb + 1) * P],
                                Qop[par][:, j, qc * CHUNK + off:(qc + 1) * CHUNK],
                                start=True, stop=not diag)
                            if diag:
                                last = nc.tensor.matmul(ps[:, ST_RING + n, off:off + P], identb[:, :],
                                                        maskb[:, 1, :], start=False, stop=True)
                            last.then_inc(s.st, 1)
                            if j % 2 and todo:
                                run(todo.pop(0))
                        for task in todo:
                            run(task)
                        if at:
                            attend(u, par, at - 1)
                    attend(u, par, NS - 1)

                norm_tensor(pe, s, 0, TURNED)
                for ch in range(CHUNKS - 1):
                    project(ch)
                pe.wait_ge(s.ops0, 16 * N_OPS)
                for k in range(16):
                    scores(-1, 0, 0, k, fresh=True)
                turn_max(-1, TURNS[1], 0, fresh=True)
                project(CHUNKS - 1)
                pe.wait_ge(s.mcp, 1)
                for k in range(16):
                    scores(-1, 0, 1, k)
                pe.wait_ge(s.vcp, CHUNKS)
                pe.wait_ge(s.rem1, 2 * CHUNKS)
                loops(pe, unit)

                if double:
                    for ch in range(CHUNKS):
                        pe.wait_ge(s.oT, ch + 1)
                        if ch >= 2:
                            pe.wait_ge(s.x, ch - 1)
                        t = slice(ch * CHUNK, (ch + 1) * CHUNK)
                        for n in range(TPC):
                            tn = slice(ch * CHUNK + n * P, ch * CHUNK + (n + 1) * P)
                            nc.tensor.matmul(ps[:, ch % 2, n * P:(n + 1) * P], wp[:, 3, :],
                                             num[:, tn], start=True, stop=False)
                            r = slice(ch * CHUNK + n * D, ch * CHUNK + (n + 1) * D)
                            last = nc.tensor.matmul(ps[:, ch % 2, n * P:(n + 1) * P], res[:, r],
                                                    ident[:, :], start=False, stop=True)
                        last.then_inc(s.y, 1)
                    pe.wait_ge(s.x, CHUNKS)
                    xf = xnT.rearrange("p (m t) -> p m t", m=2)

                    def up(e):
                        for f in range(FT):
                            if e:
                                pe.wait_ge(s.gel, 4 * (e - 1) + f + 1)
                            nc.tensor.matmul(ps[:, 2 + f, 0:2 * P], w1[:, e * FF + f * P:e * FF + (f + 1) * P],
                                             xf[:, :, e * P:(e + 1) * P], start=True, stop=True)\
                                .then_inc(s.up, 1)

                    def dn(e):
                        pe.wait_ge(s.gel, 4 * e + 4)
                        if e >= 2:
                            pe.wait_ge(s.x, CHUNKS + e - 1)
                        for m in range(2):
                            at = ps[:, e % 2, m * P:(m + 1) * P]
                            for f in range(FT):
                                nc.tensor.matmul(at, hT2[:, e % 2, f, m * P:(m + 1) * P],
                                                 w2[:, (e * FT + f) * D:(e * FT + f + 1) * D],
                                                 start=f == 0, stop=False)
                            last = nc.tensor.matmul(at, ones[0:1, :], row(ROW_B2 + e), start=False,
                                                    stop=True)
                        last.then_inc(s.y, 1)

                    pe.wait_ge(s.we, 32)
                    up(0)
                    for e in range(EXPERTS):
                        if e + 1 < EXPERTS:
                            up(e + 1)
                        dn(e)
                else:
                    for ch in range(CHUNKS):
                        pe.wait_ge(s.oT, ch + 1)
                        if ch >= 2:
                            pe.wait_ge(s.x, ch - 1)
                        for n in range(TPC):
                            at = ps[:, ch % 2, n * P:(n + 1) * P]
                            t = slice(ch * CHUNK + n * P, ch * CHUNK + (n + 1) * P)
                            last = nc.tensor.matmul(at, num[:, t], wp[:, 3, :], start=True,
                                                    stop=True)
                        last.then_inc(s.y, 1)

            def scalar(act):
                act.sem_inc(s.ex, 3)
                act.sem_inc(s.ocp, 1)

                def copy_turned(ch):
                    act.wait_ge(s.tp, ch + 1)
                    t = slice(ch * CHUNK, (ch + 1) * CHUNK)
                    if double:
                        nc.scalar.activation(xnT[:, t], ps[:, TURNED, :], ACT.Identity,
                                             bias=col("ln_b"), scale=col("ln_g")).then_inc(s.xT, 1)
                    else:
                        nc.scalar.activation(xnT[:, t], ps[:, TURNED, :], ACT.Copy).then_inc(s.xT, 1)

                copy_turned(0)
                for ch in range(CHUNKS):
                    if ch == CHUNKS - 1:
                        act.wait_ge(s.mtp, 1)
                        nc.scalar.activation(mT[0:16, :], ps[0:16, S_SLOT + 2, 0:P], ACT.Copy)\
                            .then_inc(s.mcp, 1)
                    for side in range(2):
                        if side and ch + 1 < CHUNKS and rope:
                            copy_turned(ch + 1)
                        sc = scale if side == 0 else 1.0
                        if rope:
                            act.wait_ge(s.rope, 2 * ch + side + 1)
                            src = rot[:, side, :]
                        else:
                            act.wait_ge(s.proj, 2 * ch + side + 1)
                            src = ps[:, PROJ + side, :]
                        if ch:
                            act.wait_ge(cut_stored[(ch - 1) // 2][side], 48 * ((ch - 1) % 2 + 1))
                        nc.scalar.activation(cut[side][:, 0, :], src, ACT.Copy, scale=sc)\
                            .then_inc(s.cut0, 1)
                        act.wait_ge(s.rem1, 2 * ch + side + 1)
                        nc.scalar.activation(cut[side][:, 1, :], rem[:, side, :], ACT.Copy)\
                            .then_inc(s.cut1, 1)
                    if ch + 1 < CHUNKS and not rope:
                        copy_turned(ch + 1)
                    act.wait_ge(s.vps, ch + 1)
                    b, k0 = ch // 2, (ch % 2) * 4
                    for n in range(TPC):
                        last = nc.scalar.activation(
                            v_un[:, b * HG:(b + 1) * HG, k0 + n, :],
                            ps[:, VALUES, n * P:(n + 1) * P].rearrange("p (g r) -> p g r", g=HG), ACT.Copy)
                    last.then_inc(s.vcp, 1)

                def copy_max(hn, pos):
                    act.wait_ge(s.mtp, hn + 1)
                    act.wait_ge(s.mps, hn)
                    b = S_SLOT + 2 * (pos % 2)
                    nc.scalar.activation(mT[0:16, :], ps[0:16, b, 0:P], ACT.Copy).then_inc(s.mcp, 1)

                def copy_out(u, qc):
                    act.wait_ge(s.av, u * NS + ends[qc] + 1 + 2)
                    act.wait_ge(sums_stored[qc], 64 * u + 1)
                    nc.scalar.activation(osb[:, qc, :], ps[:, O_BANK, :], ACT.Copy).then_inc(s.ocp, 1)

                def unit(u, third, par, ahead2, ahead1):
                    for at, (qc, kb, off) in enumerate(steps):
                        for j in range(GROUP):
                            n = (par * 4 * NS + 4 * at + j) % 3
                            act.wait_ge(s.st, u * 4 * NS + 4 * at + j + 1 + 1)
                            if j == 0:
                                act.wait_ge(s.av, u * NS + at + 1)
                            nc.scalar.activation(pr[:, (at % 2) * 4 + j, off:CHUNK],
                                                 ps[:, ST_RING + n, off:CHUNK],
                                                 ACT.Exp).then_inc(s.ex, 1)
                            first = TURN * len(halves[qc]) % 16 == 0 or not ahead1
                            if j == (1 if first else 3) and (
                                    (kb == turn_step(qc) and ahead1) or (at == 0 and not ahead1)):
                                copy_max(2 * u + 1 + qc, TURNS[qc])
                        if qc == 1 and kb == 0:
                            copy_out(u, 0)
                    copy_out(u, 1)

                act.wait_ge(s.qst1, 16 * 3 * CHUNKS // BATCH)
                act.wait_ge(s.kst1, 16 * 3 * CHUNKS // BATCH)
                act.wait_ge(s.cut2, 2 * CHUNKS)
                loops(act, unit)
                if double:
                    for e in range(EXPERTS):
                        for f in range(FT):
                            act.wait_ge(s.up, 4 * e + f + 1)
                            if e >= 2:
                                act.wait_ge(s.y, CHUNKS + e - 1)
                            nc.scalar.activation(hT2[:, e % 2, f, :], ps[:, 2 + f, 0:2 * P], ACT.Gelu,
                                                 bias=col("b1_l1", FT * e + f)).then_inc(s.gel, 1)

            if double:
                hT2 = hid2.rearrange("p (n f t) -> p n f t", n=2, f=FT)

            def gpsimd(pool):
                def third_part(ch):
                    for side in range(2):
                        pool.wait_ge(s.cut1, 2 * ch + side + 1)
                        nc.gpsimd.tensor_tensor(cut[side][:, 2, :], rem[:, side, :],
                                                cut[side][:, 1, :], ALU.subtract).then_inc(s.cut2, 1)

                def preset(par):
                    nc.gpsimd.memset(words(Qop[par]), 0.0)
                    nc.gpsimd.memset(words(Kop[par]), MINUS_ONES).then_inc(s.kneg, 1)

                def values(u, par):
                    nc.gpsimd.tensor_tensor(
                        vx[par][:, :, :, 0:hd],
                        v_sb[:, bass.ds(u * KB * rows4, KB * rows4)]
                        .rearrange("p (k j d) -> p k j d", k=KB, j=GROUP),
                        ones[:, 0:1].unsqueeze(2).unsqueeze(3).to_broadcast([P, KB, GROUP, hd]),
                        ALU.mult).then_inc(s.vx, 1)

                def cut_max(u, qc):
                    hn = 2 * u + qc
                    pool.wait_ge(s.mcp, hn + 1)
                    pool.wait_ge(max_placed[qc], 16 * u + 1)
                    m = [ms[0:16, qc, i, :] for i in range(3)]
                    t = Tally(s.msk, 3 * hn)
                    t.settle(pool, nc.gpsimd.tensor_tensor(m[0], mT[0:16, :], ones[0:16, :], ALU.mult))
                    t.settle(pool, nc.gpsimd.tensor_tensor(mr[0:16, :], mT[0:16, :], m[0],
                                                           ALU.subtract))
                    t.settle(pool, nc.gpsimd.tensor_tensor(m[1], mr[0:16, :], ones[0:16, :], ALU.mult))
                    nc.gpsimd.tensor_tensor(m[2], mr[0:16, :], m[1], ALU.subtract)\
                        .then_inc(s.mps, 1)

                t = Tally(s.pool)
                norms = CHUNKS * (2 if double else 1)
                ahead = 5 if double else 3
                for g in range(ahead):
                    norm_gpsimd(pool, s, t, g)
                    if g == 1:
                        preset(0)
                for ch in range(CHUNKS):
                    if ch == CHUNKS - 1:
                        cut_max(0, 0)
                    third_part(ch)
                    for g in range(ahead, min(ahead + norms // CHUNKS, norms)):
                        norm_gpsimd(pool, s, t, g)
                        ahead += 1
                    if ch == 0:
                        preset(1)
                preset(2)
                pool.wait_ge(s.vset, 3)
                pool.wait_ge(s.vcp, CHUNKS)

                def unit(u, third, par, ahead2, ahead1):
                    if ahead1:
                        pool.wait_ge(s.av, u * NS + 1 + 1)
                        values(u + 1, (par + 1) % 3)
                    cut_max(u, 1)
                    if ahead1:
                        cut_max(u + 1, 0)

                values(0, 0)
                loops(pool, unit)
                if after:
                    rstd_gpsimd(pool, s, t, norms)

            def vector(dve):
                dve.sem_inc(s.av, 2)
                dve.sem_inc(s.st, 1)
                for sem in sums_stored + max_placed:
                    dve.sem_inc(sem, 1)
                t = Tally(s.vec)

                def maxima(base, half):
                    for k, (j, qb) in enumerate(s_tasks(half)):
                        pos = position(half, k)
                        dve.wait_ge(s.s, base + 16 * half + k + 1)
                        b = S_SLOT + 2 * (pos % 2)
                        width = SEQ if full else half * CHUNK + (qb + 1) * P
                        src = ps[:, b:b + 2, :].rearrange("p b t -> p (b t)")[:, 0:width]
                        nc.vector.tensor_reduce(mq[:, half, j * 4 + qb:j * 4 + qb + 1], src, AXX,
                                                ALU.max).then_inc(s.sread, 1)

                if double:
                    norm_outer(dve, s, t, 0)
                    norm_inner(dve, s, 0)
                else:
                    norm_chunk(dve, s, t, x_rows, 0)
                for ch in range(CHUNKS):
                    if ch + 1 < CHUNKS and double:
                        norm_outer(dve, s, t, ch + 1)
                    elif ch + 1 < CHUNKS:
                        norm_chunk(dve, s, t, x_rows, ch + 1)
                    tt = slice((ch % 2) * CHUNK, (ch % 2 + 1) * CHUNK)
                    if rope and ch == 0:
                        dve.wait_ge(s.tab, 16)
                    for side in range(2):
                        if rope:
                            dve.wait_ge(s.proj, 2 * ch + side + 1)
                            if ch:
                                dve.wait_ge(s.cut2, 2 * (ch - 1) + side + 1)
                            nc.vector.tensor_tensor(rot[:, side, :], ps[:, PROJ, :], tab[:, 0, tt],
                                                    ALU.mult)
                            t.settle(dve, nc.vector.tensor_tensor(
                                rem[:, side, :], ps[:, PROJ + 1, :], tab[:, 1, tt], ALU.mult))
                            nc.vector.tensor_tensor(rot[:, side, :], rot[:, side, :], rem[:, side, :],
                                                    ALU.add).then_inc(s.rope, 1)
                    for side in range(2):
                        src = rot[:, side, :] if rope else ps[:, PROJ + side, :]
                        dve.wait_ge(s.cut0, 2 * ch + side + 1)
                        if ch and not rope:
                            dve.wait_ge(s.cut2, 2 * (ch - 1) + side + 1)
                        nc.vector.scalar_tensor_tensor(rem[:, side, :], src, scale if side == 0 else 1.0,
                                                       cut[side][:, 0, :], ALU.mult,
                                                       ALU.subtract).then_inc(s.rem1, 1)
                    if ch + 1 < CHUNKS and double:
                        norm_inner(dve, s, ch + 1)
                    if ch == CHUNKS - 2:
                        maxima(0, 0)
                maxima(0, 1)
                dve.wait_ge(s.qst1, 16 * 3 * CHUNKS // BATCH)
                dve.wait_ge(s.kst1, 16 * 3 * CHUNKS // BATCH)
                for par in range(3):
                    nc.vector.memset(vx[par], 1.0).then_inc(s.vset, 1)

                def unit(u, third, par, ahead2, ahead1):
                    if ahead1:
                        maxima((u + 1) * 32, 0)
                        maxima((u + 1) * 32, 1)

                loops(dve, unit)

                for ch in range(CHUNKS):
                    r = slice(ch * CHUNK, (ch + 1) * CHUNK)
                    dve.wait_ge(sums_loaded[ch], 32)
                    t.settle(dve, nc.vector.reciprocal(den[:, r], den[:, r]))
                    nc.vector.tensor_tensor(num[:, r], num[:, r], den[:, r], ALU.mult)\
                        .then_inc(s.oT, 1)
                for ch in range(CHUNKS):
                    dve.wait_ge(s.y, ch + 1)
                    r = slice(ch * CHUNK, (ch + 1) * CHUNK)
                    if double:
                        nc.vector.tensor_copy(xnT[:, r], ps[:, ch % 2, :]).then_inc(s.x, 1)
                    else:
                        nc.vector.tensor_tensor(x[:, r], x[:, r], ps[:, ch % 2, :], ALU.add)\
                            .then_inc(s.x, 1)
                        if ch == 1:
                            dve.wait_ge(s.x, 1)
                            ahead_stats(dve, s, t, CHUNKS, after)
                        if ch == 2:
                            ahead_apply(dve, s, CHUNKS, after)
                if double:
                    xm = x.rearrange("p (m e d) -> p m e d", m=2, e=EXPERTS)
                    for e in range(EXPERTS):
                        dve.wait_ge(s.y, CHUNKS + e + 1)
                        nc.vector.scalar_tensor_tensor(
                            xm[:, :, e, :], ps[:, e % 2, 0:2 * P].rearrange("p (m d) -> p m d", m=2),
                            0.5, xm[:, :, e, :], ALU.mult, ALU.add).then_inc(s.x, 1)
                        if e == TPC:
                            dve.wait_ge(s.x, CHUNKS + TPC)
                            ahead_stats(dve, s, t, 2 * CHUNKS, after)
                        if e == TPC + 1:
                            ahead_apply(dve, s, 2 * CHUNKS, after)

            return dict(sync=sync, tensor=tensor, scalar=scalar, gpsimd=gpsimd, vector=vector, sems=s)

        hid2 = sb("hid2", [P, 2 * FT * 2 * P])

        def retention(tag, after):
            c = Carve()
            wp = wproj[:, WEIGHTS_AT[tag]]
            tab = c(2 * SEQ).rearrange("p (n t) -> p n t", n=2)
            qT, kT = c(TOKENS), c(TOKENS)
            vt = c(TOKENS).rearrange("p (n d) -> p n d", d=D)
            kt = c(TOKENS).rearrange("p (n d) -> p n d", d=D)
            qz = c(3 * GROUP * CHUNK).rearrange("p (n j t) -> p n j t", n=3, j=GROUP)
            pr = c(8 * CHUNK).rearrange("p (n j t) -> p n j t", n=8, j=GROUP)
            tmp = c(2 * CHUNK).rearrange("p (n t) -> p n t", n=2)
            blocks = c(P)
            masked = c(P)
            state = c(TILES * P).rearrange("p (n d) -> p n d", n=TILES)
            own = c(8 * CHUNK).rearrange("p (n t) -> p n t", n=8)
            place = c(GROUP * P).rearrange("p (g d) -> p g d", g=GROUP)
            HEADS = 4 * GROUP
            one_of = c(HEADS + 1)
            s = sems(tag, "tab stats rstd xn tp xT vec pool proj rope ktp ktc vps vcp qz st pm u sd "
                          "zero av oc y x")
            PER_BATCH = SEQ // P
            OUTER = 3
            OWN, SUM = (4, 5), (6, 7)
            STEPS = CHUNKS * GROUP * TPC

            def states(n):
                return n // PER_BATCH * (PER_BATCH - 1) + n % PER_BATCH

            def sync(sp):
                for dst, name in ((tab, "r0_tab"), (blocks, "same"), (one_of, "one_of"),
                                  (place, "place")):
                    sp.dma_start(dst, a[name]).then_inc(s.tab, 16)

            def tensor(pe):
                def turn_keys(ch):
                    pe.wait_ge(s.rope, 2 * ch + 2)
                    if ch:
                        pe.wait_ge(s.ktc, ch)
                    for n in range(ch * TPC, (ch + 1) * TPC):
                        last = nc.tensor.transpose(ps[:, 6, n % TPC * P:(n % TPC + 1) * P],
                                                   kT[:, n * P:(n + 1) * P], ident[:, :])
                    last.then_inc(s.ktp, 1)

                norm_tensor(pe, s, 0)
                for ch in range(CHUNKS):
                    pe.wait_ge(s.xT, ch + 1)
                    t = slice(ch * CHUNK, (ch + 1) * CHUNK)
                    for side in range(2):
                        if side and ch + 1 < CHUNKS:
                            norm_tensor(pe, s, ch + 1)
                        if ch:
                            pe.wait_ge(s.rope, 2 * (ch - 1) + side + 1)
                        nc.tensor.matmul(ps[:, 1 + 2 * side, :], wp[:, side, :], xnT[:, t],
                                         start=True, stop=True)
                        nc.tensor.matmul(ps[:, 2 + 2 * side, :], wprs[:, side, :], xnT[:, t],
                                         start=True, stop=True).then_inc(s.proj, 1)
                    if ch:
                        pe.wait_ge(s.vcp, ch)
                    for n in range(TPC):
                        at = ps[:, 5, n * P:(n + 1) * P]
                        nc.tensor.matmul(at, xnT[:, ch * CHUNK + n * P:ch * CHUNK + (n + 1) * P],
                                         wp[:, 2, :], start=True, stop=False)
                        last = nc.tensor.matmul(at, ones[0:1, :], row(9), start=False, stop=True)
                    last.then_inc(s.vps, 1)
                    if ch:
                        turn_keys(ch - 1)
                turn_keys(CHUNKS - 1)

                def own_scores(k):
                    w, i = divmod(k, TPC)
                    n = w // GROUP * TPC + i
                    if i == 0:
                        pe.wait_ge(s.qz, w + 1)
                    if k >= 3:
                        pe.wait_ge(s.pm, k - 2)
                    nc.tensor.matmul(ps[:, k % 3, :].rearrange("p (j t) -> p j t", j=GROUP),
                                     kT[:, n * P:(n + 1) * P], qz[:, w % 3, :, i * P:(i + 1) * P],
                                     start=True, stop=True).then_inc(s.st, 1)

                def own_values(k):
                    w, i = divmod(k, TPC)
                    n, g = w // GROUP * TPC + i, w % GROUP
                    if i == 0 and w >= 2:
                        pe.wait_ge(s.oc, w - 1)
                    pe.wait_ge(s.pm, k + 1)
                    for j in range(GROUP):
                        h = GROUP * g + j
                        last = nc.tensor.matmul(ps[32 * j:32 * j + 8, OWN[w % 2], i * P:(i + 1) * P],
                                                vt[:, n, 8 * h:8 * h + 8], pr[:, k % 8, j, :],
                                                start=True, stop=True, tile_position=(0, 32 * j))
                    last.then_inc(s.av, 1)

                def outer(n):
                    if n % PER_BATCH < PER_BATCH - 1:
                        if states(n):
                            pe.wait_ge(s.sd, states(n))
                        nc.tensor.matmul(ps[:, OUTER, 0:P], kt[:, n, :], vt[:, n, :], start=True,
                                         stop=True).then_inc(s.u, 1)

                def results(ch):
                    pe.wait_ge(s.oc, GROUP * (ch + 1))
                    if ch >= 2:
                        pe.wait_ge(s.x, ch - 1)
                    for n in range(ch * TPC, (ch + 1) * TPC):
                        at = ps[:, SUM[ch % 2], n % TPC * P:(n % TPC + 1) * P]
                        first = n % PER_BATCH == 0
                        if not first:
                            pe.wait_ge(s.sd, states(n))
                            nc.tensor.matmul(at, qT[:, n * P:(n + 1) * P], state[:, n, :],
                                             start=True, stop=False)
                        for g in range(GROUP):
                            last = nc.tensor.matmul(at, own[:, (GROUP * ch + g) % 8,
                                                            n % TPC * P:(n % TPC + 1) * P],
                                                    place[:, g, :], start=first and g == 0,
                                                    stop=g == GROUP - 1)
                    last.then_inc(s.y, 1)

                pe.wait_ge(s.ktc, CHUNKS)
                pe.wait_ge(s.vcp, CHUNKS)
                pe.wait_ge(s.rope, 2 * CHUNKS)
                own_scores(0)
                pe.wait_ge(s.zero, 1)
                for w in range(CHUNKS * GROUP):
                    outer(w)
                    for k in range(w * TPC, (w + 1) * TPC):
                        if k + 1 < STEPS:
                            own_scores(k + 1)
                        own_values(k)
                    if w % GROUP == 0 and w:
                        results(w // GROUP - 1)
                results(CHUNKS - 1)

            def scalar(act):
                def copy_turned(ch):
                    act.wait_ge(s.tp, ch + 1)
                    nc.scalar.activation(xnT[:, ch * CHUNK:(ch + 1) * CHUNK], ps[:, TP, :], ACT.Copy)\
                        .then_inc(s.xT, 1)

                copy_turned(0)
                act.wait_ge(s.tab, 64)
                for ch in range(CHUNKS):
                    if ch + 1 < CHUNKS:
                        copy_turned(ch + 1)
                    tiles = slice(ch * TPC, (ch + 1) * TPC)
                    act.wait_ge(s.vps, ch + 1)
                    nc.scalar.activation(vt[:, tiles, :].rearrange("p n d -> p (n d)"), ps[:, 5, :],
                                         ACT.Copy).then_inc(s.vcp, 1)
                    act.wait_ge(s.ktp, ch + 1)
                    nc.scalar.activation(kt[:, tiles, :].rearrange("p n d -> p (n d)"), ps[:, 6, :],
                                         ACT.Copy).then_inc(s.ktc, 1)

                def single_heads(w):
                    ch, g = divmod(w, GROUP)
                    act.wait_ge(s.rope, 2 * ch + 1)
                    if w >= 3:
                        act.wait_ge(s.st, TPC * (w - 2))
                    for j in range(GROUP):
                        h = GROUP * g + j
                        last = nc.scalar.activation(qz[:, w % 3, j, :],
                                                    qT[:, ch * CHUNK:(ch + 1) * CHUNK], ACT.Identity,
                                                    bias=one_of[:, HEADS:HEADS + 1],
                                                    scale=one_of[:, h:h + 1])
                    last.then_inc(s.qz, 1)

                for w in range(3):
                    single_heads(w)
                for w in range(CHUNKS * GROUP):
                    act.wait_ge(s.av, TPC * (w + 1))
                    if w >= 2 * GROUP:
                        act.wait_ge(s.y, w // GROUP - 1)
                    nc.scalar.activation(own[:, w % 8, :], ps[:, OWN[w % 2], :], ACT.Copy)\
                        .then_inc(s.oc, 1)
                    if w + 3 < CHUNKS * GROUP:
                        single_heads(w + 3)

            def gpsimd(pool):
                t = Tally(s.pool)
                for ch in range(CHUNKS):
                    norm_gpsimd(pool, s, t, ch)
                if after:
                    rstd_gpsimd(pool, s, t, CHUNKS)

            def vector(dve):
                t = Tally(s.vec)
                norm_chunk(dve, s, t, x_rows, 0)
                for ch in range(CHUNKS):
                    if ch + 1 < CHUNKS:
                        norm_chunk(dve, s, t, x_rows, ch + 1)
                    tt = slice((ch % 2) * CHUNK, (ch % 2 + 1) * CHUNK)
                    if ch == 0:
                        dve.wait_ge(s.tab, 64)
                    for side, dst, b in ((0, qT, ("b_q", "b_qs")), (1, kT, ("b_k", "b_ks"))):
                        r = slice(ch * CHUNK, (ch + 1) * CHUNK)
                        dve.wait_ge(s.proj, 2 * ch + side + 1)
                        nc.vector.scalar_tensor_tensor(dst[:, r], ps[:, 1 + 2 * side, :], col(b[0]),
                                                       tab[:, 0, tt], ALU.add, ALU.mult)
                        t.settle(dve, nc.vector.scalar_tensor_tensor(
                            tmp[:, side, :], ps[:, 2 + 2 * side, :], col(b[1]), tab[:, 1, tt],
                            ALU.add, ALU.mult))
                        nc.vector.tensor_tensor(dst[:, r], dst[:, r], tmp[:, side, :], ALU.add)\
                            .then_inc(s.rope, 1)

                def mask(k):
                    dve.wait_ge(s.st, k + 1)
                    if k >= 8:
                        dve.wait_ge(s.av, k - 7)
                    nc.vector.tensor_tensor(
                        pr[:, k % 8], ps[:, k % 3, :].rearrange("p (j t) -> p j t", j=GROUP),
                        masks[:, 2, :].unsqueeze(1).to_broadcast([P, GROUP, P]), ALU.mult)\
                        .then_inc(s.pm, 1)

                def next_state(n):
                    i = n % PER_BATCH
                    if i == PER_BATCH - 1:
                        return
                    dve.wait_ge(s.u, states(n) + 1)
                    if i == 0:
                        nc.vector.tensor_tensor(state[:, n + 1, :], ps[:, OUTER, 0:P], blocks,
                                                ALU.mult).then_inc(s.sd, 1)
                    else:
                        t.settle(dve, nc.vector.tensor_tensor(masked, ps[:, OUTER, 0:P], blocks,
                                                              ALU.mult))
                        nc.vector.tensor_tensor(state[:, n + 1, :], state[:, n, :], masked, ALU.add)\
                            .then_inc(s.sd, 1)

                def add(ch):
                    dve.wait_ge(s.y, ch + 1)
                    r = slice(ch * CHUNK, (ch + 1) * CHUNK)
                    nc.vector.tensor_tensor(x[:, r], x[:, r], ps[:, SUM[ch % 2], :], ALU.add)\
                        .then_inc(s.x, 1)

                dve.wait_ge(s.vcp, CHUNKS)
                nc.vector.memset(ps[:, OWN[0]:OWN[1] + 1, :], 0.0).then_inc(s.zero, 1)
                mask(0)
                for w in range(CHUNKS * GROUP):
                    next_state(w)
                    for k in range(w * TPC, (w + 1) * TPC):
                        if k + 1 < STEPS:
                            mask(k + 1)
                    if w % GROUP == 1 and w > 1:
                        add(w // GROUP - 1)
                    if w == CHUNKS * GROUP - 3:
                        dve.wait_ge(s.x, 1)
                        ahead_stats(dve, s, t, CHUNKS, after)
                    if w == CHUNKS * GROUP - 2:
                        ahead_apply(dve, s, CHUNKS, after)
                add(CHUNKS - 1)

            return dict(sync=sync, tensor=tensor, scalar=scalar, gpsimd=gpsimd, vector=vector, sems=s)

        def ternary_mlp(tag, after):
            c = Carve()
            hh = c(2 * FF).rearrange("p (n f) -> p n f", n=2)
            hn = c(2 * FF).rearrange("p (n f) -> p n f", n=2)
            hT = c(2 * FF).rearrange("p (n f) -> p n f", n=2)
            st = c(2 * 6).rearrange("p (n f) -> p n f", n=2)
            m2 = c(2 * 2).rearrange("p (n f) -> p n f", n=2)
            v2 = c(2)
            r2 = c(2)
            s = sems(tag, "stats rstd xn tp xT vec pool up gel st2 r2 hn htp hT y x")

            def tensor(pe):
                def up(n):
                    if n >= 2:
                        pe.wait_ge(s.gel, n - 1)
                    nc.tensor.matmul(ps[:, 1 + n % 2, :], xnT[:, n * P:(n + 1) * P], w2fc[:, :],
                                     start=True, stop=True).then_inc(s.up, 1)

                def turn(n):
                    pe.wait_ge(s.hn, n + 1)
                    if n >= 2:
                        pe.wait_ge(s.hT, n - 1)
                    for f in range(FT):
                        last = nc.tensor.transpose(ps[:, 3 + n % 2, f * P:(f + 1) * P],
                                                   hn[:, n % 2, f * P:(f + 1) * P], ident[:, :])
                    last.then_inc(s.htp, 1)

                def down(n):
                    pe.wait_ge(s.hT, n + 1)
                    if n >= 2 * TPC:
                        pe.wait_ge(s.x, n // TPC - 1)
                    for f in range(FT):
                        last = nc.tensor.matmul(ps[:, 5 + n // TPC % 2, n % TPC * P:(n % TPC + 1) * P],
                                                hT[:, n % 2, f * P:(f + 1) * P], w2pj[:, f, :],
                                                start=f == 0, stop=f == FT - 1)
                    last.then_inc(s.y, 1)

                norm_tensor(pe, s, 0)
                norm_tensor(pe, s, 1)
                for n in range(TILES + 3):
                    if n % TPC == 0 and n // TPC + 2 < CHUNKS:
                        norm_tensor(pe, s, n // TPC + 2)
                    if n < TILES:
                        pe.wait_ge(s.xT, n // TPC + 1)
                        up(n)
                    if 2 <= n < TILES + 2:
                        turn(n - 2)
                    if n >= 3:
                        down(n - 3)

            def scalar(act):
                def copy_turned(ch):
                    act.wait_ge(s.tp, ch + 1)
                    nc.scalar.activation(xnT[:, ch * CHUNK:(ch + 1) * CHUNK], ps[:, TP, :], ACT.Copy)\
                        .then_inc(s.xT, 1)

                copy_turned(0)
                copy_turned(1)
                for n in range(TILES + 2):
                    if n % TPC == 0 and n // TPC + 2 < CHUNKS:
                        copy_turned(n // TPC + 2)
                    if n < TILES:
                        act.wait_ge(s.up, n + 1)
                        if n >= 2:
                            act.wait_ge(s.hn, n - 1)
                        nc.scalar.activation(hh[:, n % 2, :], ps[:, 1 + n % 2, :], ACT.Gelu)\
                            .then_inc(s.gel, 1)
                    if n >= 2:
                        k = n - 2
                        act.wait_ge(s.htp, k + 1)
                        if k >= 2:
                            act.wait_ge(s.y, k - 1)
                        for f in range(FT):
                            last = nc.scalar.activation(hT[:, k % 2, f * P:(f + 1) * P],
                                                        ps[:, 3 + k % 2, f * P:(f + 1) * P],
                                                        ACT.Identity, bias=col("l2_b", f),
                                                        scale=col("l2_w", f))
                        last.then_inc(s.hT, 1)

            def gpsimd(pool):
                t = Tally(s.pool)
                for ch in range(CHUNKS):
                    norm_gpsimd(pool, s, t, ch)
                for n in range(TILES):
                    k = n % 2
                    pool.wait_ge(s.st2, n + 1)
                    t.settle(pool, nc.gpsimd.tensor_scalar(v2[:, k:k + 1], m2[:, k, 1:2], EPS, None,
                                                           ALU.add))
                    nc.gpsimd.tensor_tensor(r2[:, k:k + 1], v2[:, k:k + 1], neghalf[:, 0:1], ALU.pow)\
                        .then_inc(s.r2, 1)
                if after:
                    rstd_gpsimd(pool, s, t, CHUNKS)

            def vector(dve):
                t = Tally(s.vec)
                norm_chunk(dve, s, t, x_rows, 0)
                norm_chunk(dve, s, t, x_rows, 1)
                for n in range(TILES + 1):
                    if n % TPC == 0 and n // TPC + 2 < CHUNKS:
                        norm_chunk(dve, s, t, x_rows, n // TPC + 2)
                    if n < TILES:
                        k = n % 2
                        dve.wait_ge(s.gel, n + 1)
                        t.settle(dve, nc.vector.bn_stats(st[:, k, :], hh[:, k, :]))
                        nc.vector.bn_aggr(m2[:, k, :], st[:, k, :]).then_inc(s.st2, 1)
                    if n:
                        k = (n - 1) % 2
                        dve.wait_ge(s.r2, n)
                        if n >= 3:
                            dve.wait_ge(s.htp, n - 2)
                        nc.vector.tensor_scalar(hn[:, k, :], hh[:, k, :], m2[:, k, 0:1], r2[:, k:k + 1],
                                                ALU.subtract, ALU.mult).then_inc(s.hn, 1)
                    if n >= TPC + 3 and (n - 3) % TPC == 0:
                        add(dve, (n - 3) // TPC - 1)
                dve.wait_ge(s.x, 1)
                ahead_stats(dve, s, t, CHUNKS, after)
                ahead_apply(dve, s, CHUNKS, after)
                add(dve, CHUNKS - 1)

            def add(dve, ch):
                dve.wait_ge(s.y, TPC * (ch + 1))
                r = slice(ch * CHUNK, (ch + 1) * CHUNK)
                nc.vector.scalar_tensor_tensor(x[:, r], ps[:, 5 + ch % 2, :], 0.5, x[:, r],
                                               ALU.mult, ALU.add).then_inc(s.x, 1)

            return dict(tensor=tensor, scalar=scalar, gpsimd=gpsimd, vector=vector, sems=s)

        def mlp_tensor(pe, s, w_in, w_out, b_row, hT):
            def up(ch):
                for f in range(FT):
                    if ch:
                        pe.wait_ge(s.gel, 4 * (ch - 1) + f + 1)
                    nc.tensor.matmul(ps[:, 1 + f, :], w_in[:, f * P:(f + 1) * P],
                                     xnT[:, ch * CHUNK:(ch + 1) * CHUNK], start=True, stop=True)\
                        .then_inc(s.up, 1)

            def down(ch):
                pe.wait_ge(s.gel, 4 * ch + 4)
                if ch >= 2:
                    pe.wait_ge(s.x, ch - 1)
                for n in range(TPC):
                    at = ps[:, 5 + ch % 2, n * P:(n + 1) * P]
                    for f in range(FT):
                        nc.tensor.matmul(at, hT[:, ch % 2, f, n * P:(n + 1) * P], w_out[:, f, :],
                                         start=f == 0, stop=False)
                    last = nc.tensor.matmul(at, ones[0:1, :], row(b_row), start=False, stop=True)
                last.then_inc(s.y, 1)

            norm_tensor(pe, s, 0)
            for ch in range(CHUNKS + 1):
                if ch + 1 < CHUNKS:
                    norm_tensor(pe, s, ch + 1)
                if ch < CHUNKS:
                    pe.wait_ge(s.xT, ch + 1)
                    up(ch)
                if ch:
                    down(ch - 1)

        def mlp_gelu(act, s, hT, bias_name, ch):
            for f in range(FT):
                act.wait_ge(s.up, 4 * ch + f + 1)
                if ch >= 2:
                    act.wait_ge(s.y, ch - 1)
                nc.scalar.activation(hT[:, ch % 2, f, :], ps[:, 1 + f, :], ACT.Gelu,
                                     bias=col(bias_name, f)).then_inc(s.gel, 1)

        def binary_mlp(tag, after):
            c = Carve()
            hT = c(2 * FT * CHUNK).rearrange("p (n f t) -> p n f t", n=2, f=FT)
            s = sems(tag, "stats rstd xn tp xT vec pool up gel y x")

            def tensor(pe):
                mlp_tensor(pe, s, w3a, w3b, ROW_L3B2, hT)

            def scalar(act):
                for ch in range(CHUNKS + 1):
                    if ch < CHUNKS:
                        act.wait_ge(s.tp, ch + 1)
                        nc.scalar.activation(xnT[:, ch * CHUNK:(ch + 1) * CHUNK], ps[:, TP, :],
                                             ACT.Copy).then_inc(s.xT, 1)
                    if ch:
                        mlp_gelu(act, s, hT, "l3w_b1", ch - 1)

            def gpsimd(pool):
                t = Tally(s.pool)
                for ch in range(CHUNKS):
                    norm_gpsimd(pool, s, t, ch)
                if after:
                    rstd_gpsimd(pool, s, t, CHUNKS)

            def vector(dve):
                t = Tally(s.vec)
                norm_chunk(dve, s, t, x_rows, 0)
                norm_chunk(dve, s, t, x_rows, 1)
                for ch in range(CHUNKS):
                    if ch + 2 < CHUNKS:
                        norm_chunk(dve, s, t, x_rows, ch + 2)
                    dve.wait_ge(s.y, ch + 1)
                    r = slice(ch * CHUNK, (ch + 1) * CHUNK)
                    nc.vector.scalar_tensor_tensor(x[:, r], ps[:, 5 + ch % 2, :], 0.5,
                                                   x[:, r], ALU.mult, ALU.add).then_inc(s.x, 1)
                    if ch == 2:
                        dve.wait_ge(s.x, 1)
                        ahead_stats(dve, s, t, CHUNKS, after)
                        ahead_apply(dve, s, CHUNKS, after)

            return dict(tensor=tensor, scalar=scalar, gpsimd=gpsimd, vector=vector, sems=s)

        def lion(tag, after):
            c = Carve()
            wq, wk, wo, wd = (c(D) for _ in range(4))
            wv = c(8 * D).rearrange("p (e m) -> p e m", e=8)
            f1 = c(FF)
            f2 = c(FF).rearrange("p (f d) -> p f d", f=FT)
            sel = c(8 * P).rearrange("p (e m) -> p e m", e=8)
            same = c(P)
            phq = c(TOKENS)
            phk = c(TOKENS)
            lam = c(TOKENS)
            low = c(2 * CHUNK).rearrange("p (n t) -> p n t", n=2)
            kv = c(2 * SEQ).rearrange("p (n t) -> p n t", n=2)
            fw = c(3 * SEQ).rearrange("p (n t) -> p n t", n=3)
            bw = c(2 * SEQ).rearrange("p (n t) -> p n t", n=2)
            oT = c(TOKENS)
            rowo = c(2 * D)
            hT = c(2 * FT * CHUNK).rearrange("p (n f t) -> p n f t", n=2, f=FT)
            s = sems(tag, "w stats rstd xn tp xT vec pool pj mn ex vps vr g gq acc dn oT y r up gel x")

            def sync(sp):
                for dst, name in ((wq, "wq3"), (wk, "wk3"), (wv, "wv3"), (wo, "wo3"), (wd, "wd3"),
                                  (f1, "f13"), (f2, "f23"), (sel, "sel"), (same, "same")):
                    sp.dma_start(dst, a[name]).then_inc(s.w, 16)
                sp.dma_start(rowo[0:1, :], a["rows3"]).then_inc(s.w, 16)
            NW = 160

            def tensor(pe):
                pe.wait_ge(s.w, NW)
                norm_tensor(pe, s, 0)
                for ch in range(CHUNKS):
                    pe.wait_ge(s.xT, ch + 1)
                    t = slice(ch * CHUNK, (ch + 1) * CHUNK)
                    for k, w in enumerate((wq, wk, wd)):
                        if ch:
                            pe.wait_ge(s.ex, 3 * (ch - 1) + k + 1)
                        nc.tensor.matmul(ps[:, 1 + k, :], w, xnT[:, t], start=True, stop=True)\
                            .then_inc(s.pj, 1)
                    if ch + 1 < CHUNKS:
                        norm_tensor(pe, s, ch + 1)

                def value(n):
                    b, e = divmod(n, 8)
                    if n >= 2:
                        pe.wait_ge(s.vr, n - 1)
                    for h in range(2):
                        last = nc.tensor.matmul(ps[:, 2 * (n % 2) + h, :],
                                                wv[:, e, :],
                                                xnT[:, b * SEQ + h * CHUNK:b * SEQ + (h + 1) * CHUNK],
                                                start=True, stop=True)
                    last.then_inc(s.vps, 1)

                def gather(n):
                    b, item = divmod(n, 9)
                    e = item - 1 if item else 8
                    pe.wait_ge(s.gq, n + 1)
                    if b and e == 8:
                        pe.wait_ge(s.dn, 1)
                    if b and e == 0:
                        pe.wait_ge(s.oT, 1)
                    for h in range(2):
                        w = sel[:, e, :] if e < 8 else same
                        last = nc.tensor.matmul(ps[:, (4 if e < 8 else 6) + h, :], w,
                                                fw[:, n % 3, h * CHUNK:(h + 1) * CHUNK],
                                                start=e in (0, 8), stop=e in (7, 8),
                                                skip_group_check=True)
                    last.then_inc(s.acc, 1)

                pe.wait_ge(s.ex, 3 * CHUNKS)
                value(0)
                value(1)
                nv = 2
                for n in range(18):
                    if n % 9 and nv < 16:
                        value(nv)
                        nv += 1
                    gather(n)
                for ch in range(CHUNKS):
                    if ch % 2 == 0:
                        pe.wait_ge(s.oT, ch // 2 + 1)
                    if ch >= 2:
                        pe.wait_ge(s.r, ch - 1)
                    for n in range(TPC):
                        t = slice(ch * CHUNK + n * P, ch * CHUNK + (n + 1) * P)
                        at = ps[:, 2 + ch % 2, n * P:(n + 1) * P]
                        nc.tensor.matmul(at, oT[:, t], wo, start=True, stop=False)
                        last = nc.tensor.matmul(at, ones[0:1, :], rowo[0:1, 0:D], start=False, stop=True)
                    last.then_inc(s.y, 1)
                norm_tensor(pe, s, CHUNKS)
                for ch in range(CHUNKS + 1):
                    if ch + 1 < CHUNKS:
                        norm_tensor(pe, s, CHUNKS + ch + 1)
                    if ch < CHUNKS:
                        pe.wait_ge(s.xT, CHUNKS + ch + 1)
                        for f in range(FT):
                            if ch:
                                pe.wait_ge(s.gel, 4 * (ch - 1) + f + 1)
                            nc.tensor.matmul(ps[:, 1 + f, :], f1[:, f * P:(f + 1) * P],
                                             xnT[:, ch * CHUNK:(ch + 1) * CHUNK], start=True, stop=True)\
                                .then_inc(s.up, 1)
                    if ch:
                        k = ch - 1
                        pe.wait_ge(s.gel, 4 * k + 4)
                        if k >= 2:
                            pe.wait_ge(s.x, k - 1)
                        for n in range(TPC):
                            at = ps[:, 5 + k % 2, n * P:(n + 1) * P]
                            for f in range(FT):
                                nc.tensor.matmul(at, hT[:, k % 2, f, n * P:(n + 1) * P], f2[:, f, :],
                                                 start=f == 0, stop=False)
                            last = nc.tensor.matmul(at, ones[0:1, :], rowo[0:1, D:2 * D], start=False,
                                                    stop=True)
                        last.then_inc(s.y, 1)

            def scalar(act):
                def copy_turned(k, gain, offset):
                    act.wait_ge(s.tp, k + 1)
                    t = slice(k % CHUNKS * CHUNK, (k % CHUNKS + 1) * CHUNK)
                    nc.scalar.activation(xnT[:, t], ps[:, TP, :], ACT.Identity, bias=col(offset),
                                         scale=col(gain)).then_inc(s.xT, 1)

                copy_turned(0, "l3_g1", "l3_o1")
                for ch in range(CHUNKS):
                    t = slice(ch * CHUNK, (ch + 1) * CHUNK)
                    for k, dst in enumerate((phq, phk, lam)):
                        if k < 2:
                            act.wait_ge(s.mn, 2 * ch + k + 1)
                            nc.scalar.activation(dst[:, t], ps[:, 1 + k, :], ACT.Exp,
                                                 bias=col(("l3_qb", "l3_kb")[k])).then_inc(s.ex, 1)
                        else:
                            act.wait_ge(s.pj, 3 * ch + 3)
                            nc.scalar.activation(dst[:, t], ps[:, 3, :], ACT.Sigmoid,
                                                 bias=col("l3_db")).then_inc(s.ex, 1)
                    if ch + 1 < CHUNKS:
                        copy_turned(ch + 1, "l3_g1", "l3_o1")
                copy_turned(CHUNKS, "l3_g2", "l3_o2")
                for ch in range(CHUNKS):
                    if ch + 1 < CHUNKS:
                        copy_turned(CHUNKS + ch + 1, "l3_g2", "l3_o2")
                    for f in range(FT):
                        act.wait_ge(s.up, 4 * ch + f + 1)
                        if ch >= 2:
                            act.wait_ge(s.y, CHUNKS + ch - 1)
                        nc.scalar.activation(hT[:, ch % 2, f, :], ps[:, 1 + f, :], ACT.Gelu,
                                             bias=col("l3_f1b", f)).then_inc(s.gel, 1)

            def gpsimd(pool):
                t = Tally(s.pool)
                for ch in range(2 * CHUNKS):
                    norm_gpsimd(pool, s, t, ch)
                for n in range(18):
                    pool.wait_ge(s.g, n + 1)
                    nc.gpsimd.tensor_tensor(fw[:, n % 3, :], fw[:, n % 3, :],
                                            phq[:, n // 9 * SEQ:(n // 9 + 1) * SEQ], ALU.mult)\
                        .then_inc(s.gq, 1)
                for ch in range(CHUNKS):
                    norm_gpsimd(pool, s, t, 2 * CHUNKS + ch)
                if after:
                    rstd_gpsimd(pool, s, t, 3 * CHUNKS)

            def vector(dve):
                t = Tally(s.vec)
                norm_outer(dve, s, t, 0)
                norm_inner(dve, s, 0)
                for ch in range(CHUNKS):
                    tt = slice(ch * CHUNK, (ch + 1) * CHUNK)
                    if ch + 1 < CHUNKS:
                        norm_outer(dve, s, t, ch + 1)
                    for k, b in enumerate(("l3_qb", "l3_kb")):
                        dve.wait_ge(s.pj, 3 * ch + k + 1)
                        nc.vector.tensor_scalar(low[:, k, :], ps[:, 1 + k, :], col(b), 0.0, ALU.add,
                                                ALU.max).then_inc(s.mn, 1)
                    for k, dst in enumerate((phq, phk)):
                        dve.wait_ge(s.ex, 3 * ch + k + 1)
                        last = nc.vector.scalar_tensor_tensor(dst[:, tt], dst[:, tt], 1.0,
                                                              low[:, k, :], ALU.min, ALU.add)
                    if ch + 1 < CHUNKS:
                        norm_inner(dve, s, ch + 1)
                    dve.wait_ge(s.ex, 3 * ch + 3)
                    t.settle(dve, nc.vector.tensor_scalar(lam[:, tt], lam[:, tt], 1e-8, None,
                                                          ALU.max))
                nc.vector.memset(bw[:, 0, SEQ - 1:SEQ], 0.0)
                t.settle(dve, nc.vector.memset(bw[:, 1, SEQ - 1:SEQ], 0.0))
                def scans(n):
                    b, item = divmod(n, 9)
                    k = n % 2
                    bb = slice(b * SEQ, (b + 1) * SEQ)
                    if item:
                        v = 8 * b + item - 1
                        dve.wait_ge(s.vps, v + 1)
                        nc.vector.scalar_tensor_tensor(
                            kv[:, k, :],
                            ps[:, 2 * (v % 2):2 * (v % 2) + 2, :].rearrange("p b t -> p (b t)"),
                            col("l3_vb", item - 1), phk[:, bb], ALU.add, ALU.mult).then_inc(s.vr, 1)
                        dve.wait_ge(s.vr, v + 1)
                    else:
                        t.settle(dve, nc.vector.tensor_copy(kv[:, k, :], phk[:, bb]))
                    if n >= 3:
                        dve.wait_ge(s.acc, n - 2)
                    nc.vector.tensor_tensor_scan(fw[:, n % 3, :], lam[:, bb], kv[:, k, :], 0.0,
                                                 ALU.mult, ALU.add)
                    t.settle(dve, nc.vector.tensor_tensor_scan(
                        bw[:, k, 0:SEQ - 1][:, ::-1], kv[:, k, 1:SEQ][:, ::-1],
                        lam[:, b * SEQ + 1:(b + 1) * SEQ][:, ::-1], 0.0, ALU.add, ALU.mult))
                    nc.vector.tensor_tensor(fw[:, n % 3, :], fw[:, n % 3, :], bw[:, k, :],
                                            ALU.add).then_inc(s.g, 1)

                def denominators(b):
                    bb = slice(b * SEQ, (b + 1) * SEQ)
                    dve.wait_ge(s.acc, 9 * b + 1)
                    nc.vector.tensor_scalar(oT[:, bb], ps[:, 6:8, :].rearrange("p b t -> p (b t)"),
                                            1e-6, None, ALU.max).then_inc(s.dn, 1)
                    dve.wait_ge(s.dn, b + 1)
                    t.settle(dve, nc.vector.reciprocal(oT[:, bb], oT[:, bb]))

                def quotients(b):
                    bb = slice(b * SEQ, (b + 1) * SEQ)
                    dve.wait_ge(s.acc, 9 * b + 9)
                    nc.vector.tensor_tensor(oT[:, bb], oT[:, bb],
                                            ps[:, 4:6, :].rearrange("p b t -> p (b t)"),
                                            ALU.mult).then_inc(s.oT, 1)

                for n in range(18):
                    scans(n)
                    if n == 9:
                        quotients(0)
                    if n % 9 == 2:
                        denominators(n // 9)
                quotients(1)
                for ch in range(CHUNKS):
                    r = slice(ch * CHUNK, (ch + 1) * CHUNK)
                    dve.wait_ge(s.y, ch + 1)
                    nc.vector.tensor_tensor(res[:, r], res[:, r], ps[:, 2 + ch % 2, :], ALU.add)\
                        .then_inc(s.r, 1)
                dve.wait_ge(s.r, CHUNKS)
                for ch in range(CHUNKS):
                    r = slice(ch * CHUNK, (ch + 1) * CHUNK)
                    last = nc.vector.tensor_tensor(x[:, r], x[:, r], res[:, r], ALU.add)
                t.settle(dve, last)
                norm_chunk(dve, s, t, res_rows, 0, 2 * CHUNKS, CHUNKS)
                norm_chunk(dve, s, t, res_rows, 1, 2 * CHUNKS, CHUNKS)
                for ch in range(CHUNKS):
                    if ch + 2 < CHUNKS:
                        norm_chunk(dve, s, t, res_rows, ch + 2, 2 * CHUNKS, CHUNKS)
                    dve.wait_ge(s.y, CHUNKS + ch + 1)
                    r = slice(ch * CHUNK, (ch + 1) * CHUNK)
                    nc.vector.tensor_tensor(x[:, r], x[:, r], ps[:, 5 + ch % 2, :], ALU.add)\
                        .then_inc(s.x, 1)
                    if ch == 2:
                        dve.wait_ge(s.x, 1)
                        ahead_stats(dve, s, t, 3 * CHUNKS, after)
                        ahead_apply(dve, s, 3 * CHUNKS, after, 2 * CHUNKS)

            return dict(sync=sync, tensor=tensor, scalar=scalar, gpsimd=gpsimd, vector=vector, sems=s)

        cw = Carve()
        raw_fc, raw_pj, raw_a, raw_b = (cw(FF) for _ in range(4))
        tmp_v, tmp_s = cw(FF), cw(FF)
        gam = cw(8)

        def boot_sync(sp):
            for dst, name in ((x, "x"), (ident, "ident"), (masks, "masks"), (lower, "lower"),
                              (cols[:, 0:n_cols - 4], "cols"), (rows[0:1, :], "rows"), (raw_fc, "fc2"),
                              (raw_pj, "pj2"), (raw_a, "w13"), (raw_b, "w23")):
                sp.dma_start(dst, a[name]).then_inc(boot.const, 16)
        NBOOT = 160

        def boot_gpsimd(pool):
            pool.wait_ge(boot.bw, 1)
            rstd_gpsimd(pool, boot, Tally(boot.pool), 0)

        def boot_tensor(pe):
            pe.wait_ge(boot.gabs, 1)
            nc.tensor.matmul(ps[:, 0, 0:2], ones[:, :], gam[:, 0:2], start=True, stop=True)\
                .then_inc(boot.gsum, 1)
            pe.wait_ge(boot.gabs, 2)
            nc.tensor.matmul(ps[:, 1, :], ones[:, :], tmp_v, start=True, stop=True)\
                .then_inc(boot.gsum, 1)
            pe.wait_ge(boot.gabs, 3)
            for f in range(FT):
                last = nc.tensor.matmul(ps[:, 2, 0:D], ones[:, :], tmp_v[:, f * D:(f + 1) * D],
                                        start=f == 0, stop=f == FT - 1)
            last.then_inc(boot.gsum, 1)

        def boot_scalar(act):
            act.wait_ge(boot.const, NBOOT)
            nc.scalar.activation(w3a[:, :], raw_a, ACT.Sign).then_inc(boot.bsign, 1)
            nc.scalar.activation(w3b.rearrange("p f d -> p (f d)"), raw_b, ACT.Sign)\
                .then_inc(boot.bsign, 1)

        def boot_vector(dve):
            t = Tally(boot.vec)
            dve.wait_ge(boot.const, NBOOT)
            nc.vector.memset(neghalf[:, :], -0.5).then_inc(boot.bw, 1)
            ahead_stats(dve, boot, t, 0, "single")
            nc.vector.memset(ones[:, :], 1.0)
            nc.vector.tensor_copy(identb[:, :], ident[:, :])
            nc.vector.tensor_copy(maskb.rearrange("p n t -> p (n t)"),
                                  masks[:, 0:2, :].rearrange("p n t -> p (n t)"))
            for k, src in enumerate((raw_fc, raw_pj)):
                t.settle(dve, nc.vector.scalar_tensor_tensor(tmp_s, src, -1.0, src, ALU.mult, ALU.max))
                last = nc.vector.tensor_reduce(gam[:, k:k + 1], tmp_s, AXX, ALU.add)
                if k == 0:
                    t.settle(dve, last)
            last.then_inc(boot.gabs, 1)
            dve.wait_ge(boot.gsum, 1)
            t.settle(dve, nc.vector.tensor_scalar(gam[:, 2:4], ps[:, 0, 0:2], 1.0 / (D * FF), 1e-6,
                                                  ALU.mult, ALU.add))
            t.settle(dve, nc.vector.tensor_scalar(gam[:, 2:4], gam[:, 2:4], 0.5, None, ALU.mult))
            t.settle(dve, nc.vector.tensor_scalar(gam[:, 4:6], gam[:, 2:4], -1.0, None, ALU.mult))
            for k, (src, dst) in enumerate(((raw_fc, w2fc[:, :]),
                                            (raw_pj, w2pj.rearrange("p f d -> p (f d)")))):
                t.settle(dve, nc.vector.tensor_scalar(tmp_s, src, gam[:, 4 + k:5 + k], None,
                                                      ALU.is_lt))
                t.settle(dve, nc.vector.scalar_tensor_tensor(dst, src, gam[:, 2 + k:3 + k], tmp_s,
                                                             ALU.is_gt, ALU.subtract))
            nc.vector.scalar_tensor_tensor(tmp_v, raw_a, -1.0, raw_a, ALU.mult, ALU.max)\
                .then_inc(boot.gabs, 1)
            dve.wait_ge(boot.gsum, 2)
            dve.wait_ge(boot.bsign, 2)

            def binarise(dst, alpha, src, k):
                t.settle(dve, nc.vector.scalar_tensor_tensor(dst, alpha, k, dst, ALU.mult, ALU.mult))
                t.settle(dve, nc.vector.tensor_tensor(dst, dst, src, ALU.subtract))
                t.settle(dve, nc.vector.tensor_tensor(dst, dst, src, ALU.add))

            binarise(w3a[:, :], ps[:, 1, :], raw_a, 1.0 / D)
            nc.vector.scalar_tensor_tensor(tmp_v, raw_b, -1.0, raw_b, ALU.mult, ALU.max)\
                .then_inc(boot.gabs, 1)
            dve.wait_ge(boot.gsum, 3)
            for f in range(FT):
                binarise(w3b[:, f, :], ps[:, 2, 0:D], raw_b[:, f * D:(f + 1) * D], 1.0 / FF)
            ahead_apply(dve, boot, 0, "single", 0)

        ROOT8 = 1.0 / 8.0 ** 0.5
        layers = [
            (moe, ("m0",)),
            (retention, ("a0",)),
            (moe, ("m1",)),
            (attention, ("f1", 4, True, None, 0.5, True)),
            (attention, ("a1", 8, False, "r1", ROOT8, False)),
            (attention, ("f2", 4, True, None, 0.5, True)),
            (ternary_mlp, ("t1",)),
            (attention, ("a2", 8, False, "r2", ROOT8, False)),
            (ternary_mlp, ("t2",)),
            (binary_mlp, ("b1",)),
            (lion, ("l3",)),
            (binary_mlp, ("b2",)),
        ]

        last_sems = sems("final", "out")

        def finish_sync(sp):
            sp.dma_start(out.rearrange("(n p) d -> p n d", p=P),
                         x.rearrange("p (n d) -> p n d", d=D)).then_inc(last_sems.out, 16)
            sp.wait_ge(last_sems.out, 16)

        def run(part, ahead=None):
            loaded = [nc.alloc_semaphore(name=f"{ahead}_loaded")] if ahead in WEIGHTS else []

            def sync(sp):
                if loaded:
                    total = load_projections(sp, loaded[0], ahead)
                if "sync" in part:
                    part["sync"](sp)
                if loaded:
                    sp.wait_ge(loaded[0], total)

            with nc.Block() as block:
                if "sync" in part or loaded:
                    block.sync(sync)
                if "tensor" in part:
                    block.tensor(part["tensor"])
                if "scalar" in part:
                    block.scalar(part["scalar"])
                if "gpsimd" in part:
                    block.gpsimd(part["gpsimd"])
                if "vector" in part:
                    block.vector(part["vector"])
            nc.clear_and_free_semaphores(list(part["sems"]) + loaded)
            nc.all_engine_barrier()

        run(dict(sync=boot_sync, tensor=boot_tensor, scalar=boot_scalar, vector=boot_vector,
                 gpsimd=boot_gpsimd, sems=boot))
        for n, (make, args) in enumerate(layers):
            after = None
            if n + 1 < len(layers):
                double = layers[n + 1][0] is lion or layers[n + 1][1][-1] is True
                after = "outer" if double else "single"
            run(make(args[0], after, *args[1:]), layers[n + 1][1][0] if after else None)
        run(dict(sync=finish_sync, sems=last_sems))


def _layout(i):
    import numpy as np
    f = np.float32
    c = np.ascontiguousarray
    T = lambda w: c(np.asarray(w).T)
    o = {}
    o["x"] = c(np.asarray(i["L0_attn_x"]).reshape(TILES, P, D).transpose(1, 0, 2)).reshape(P, TILES * D)
    o["ident"] = np.eye(P, dtype=f)
    r, q = np.arange(P)[:, None], np.arange(P)[None, :]
    big = f(-1e30)
    o["masks"] = c(np.stack([np.where(q > r, big, f(0)), np.where(q < r, big, f(0)),
                             np.where(q >= r, f(1), f(0))], 1).astype(f))
    e = np.arange(EXPERTS)
    o["lower"] = np.tile((e[None, :] < e[:, None]).astype(f).reshape(1, -1), (P, 1))

    gu = np.asarray(i["L0_ffn_experts_gate_up"])
    dn = np.asarray(i["L0_ffn_experts_down"])
    sg, su, sd = (np.asarray(i["L0_ffn_shared_" + n + "_w"]) for n in ("gate", "up", "down"))
    G = [gu[k, :INTER] for k in range(EXPERTS)] + [sg[:INTER], sg[INTER:]]
    U = [gu[k, INTER:] for k in range(EXPERTS)] + [su[:INTER], su[INTER:]]
    Dn = [dn[k] for k in range(EXPERTS)] + [sd[:, :INTER], sd[:, INTER:]]
    up = np.zeros((UPS_, P, D), f)
    down = np.zeros((P, PAIRS * 3, D), f)
    for p in range(PAIRS):
        for h in range(2):
            w = 2 * p + h
            up[6 * p + 2 * h] = G[w][:P]
            up[6 * p + 2 * h + 1] = U[w][:P]
            up[6 * p + 4, 64 * h:64 * h + TAIL] = G[w][P:]
            up[6 * p + 5, 64 * h:64 * h + TAIL] = U[w][P:]
            down[:, 3 * p + h] = Dn[w][:, :P].T
            down[64 * h:64 * h + TAIL, 3 * p + 2] = Dn[w][:, P:].T
    o["up0"] = c(up.transpose(2, 0, 1)).reshape(D, UPS_ * P)
    o["down0"] = c(down).reshape(P, PAIRS * 3 * D)
    o["gate0"] = c(np.concatenate([np.asarray(i["L0_ffn_gate_w"]),
                                   np.asarray(i["L0_ffn_shared_expert_gate_w"])], 0).T)

    hd = 8
    feat = np.arange(D)
    inv = (f(1.0) / f(10000.0) ** (np.arange(0, hd, 2, dtype=f) / f(hd))).astype(f)
    ang = (np.arange(SEQ, dtype=f)[:, None] * inv[None, :]).astype(f)
    cos, sin = np.cos(ang).T.astype(f), np.sin(ang).T.astype(f)
    def by_dim(hd):
        return feat // (4 * hd) * 4 * hd + feat % 4 * hd + feat % (4 * hd) // 4

    by8, by4 = by_dim(8), by_dim(4)
    half_perm = feat // hd * hd + (feat % hd + hd // 2) % hd
    pair_perm = feat ^ 1
    sgn_half = np.where(feat % hd < hd // 2, f(-1), f(1))[:, None]
    sgn_pair = np.where(feat % 2 == 0, f(-1), f(1))[:, None]
    o["r0_tab"] = c(np.stack([cos[feat % (hd // 2)], sin[feat % (hd // 2)] * sgn_half], 1).astype(f))
    pair_tab = c(np.stack([cos[feat % hd // 2], sin[feat % hd // 2] * sgn_pair], 1)[by8].astype(f))
    o["r1_tab"] = o["r2_tab"] = pair_tab
    wqkv, bqkv = np.asarray(i["L0_attn_W_qkv"]), np.asarray(i["L0_attn_b_qkv"])
    o["wq0"], o["wk0"], o["wv0"] = (T(wqkv[k * D:(k + 1) * D]) for k in range(3))
    o["r0_wqs"], o["r0_wks"] = c(o["wq0"][:, half_perm]), c(o["wk0"][:, half_perm])
    o["one_of"] = (feat[:, None] // hd == np.arange(17)[None, :]).astype(f)
    place = np.zeros((P, 4, P), f)
    for g in range(4):
        for j in range(4):
            for k in range(hd):
                place[32 * j + k, g, hd * (4 * g + j) + k] = 1
    o["place"] = place
    for n in "qkvo":
        o[f"w{n}1"] = c(np.asarray(i["L1_attn_w" + n]))
        o[f"w{n}f"] = c(np.asarray(i["L1_ffn_w" + n]))
        o[f"w{n}2"] = T(i["L2_attn_W" + n])
        o[f"w{n}3"] = c(np.asarray(i[f"L3_attn_{n}_w"]))
    for k in "12":
        o[f"r{k}_wqs"], o[f"r{k}_wks"] = c(o["wq" + k][:, pair_perm[by8]]), c(o["wk" + k][:, pair_perm[by8]])
    for k, by in (("1", by8), ("2", by8), ("f", by4)):
        o["wq" + k], o["wk" + k] = c(o["wq" + k][:, by]), c(o["wk" + k][:, by])

    o["w1_1"] = c(np.asarray(i["L1_ffn_w1"]).transpose(1, 0, 2)).reshape(D, EXPERTS * FF)
    o["w2_1"] = c(np.asarray(i["L1_ffn_w2"]).reshape(EXPERTS, FT, P, D).transpose(2, 0, 1, 3))\
        .reshape(P, EXPERTS * FT * D)
    o["fc2"] = T(i["L2_ffn_W_fc"])
    o["pj2"] = c(np.asarray(i["L2_ffn_W_proj"]).T.reshape(FT, P, D).transpose(1, 0, 2)).reshape(P, FF)
    o["w13"] = T(i["L3_ffn_w1"])
    o["w23"] = c(np.asarray(i["L3_ffn_w2"]).T.reshape(FT, P, D).transpose(1, 0, 2)).reshape(P, FF)
    o["wd3"] = c(np.asarray(i["L3_attn_dec_w"])[:, feat // hd])
    o["wv3"] = c(np.stack([o["wv3"][:, feat // hd * hd + k] for k in range(hd)], 1))
    o["f13"] = c(np.asarray(i["L3_attn_f1_w"]))
    o["f23"] = c(np.asarray(i["L3_attn_f2_w"]).reshape(FT, P, D).transpose(1, 0, 2))
    o["rows3"] = np.concatenate([np.asarray(i["L3_attn_o_b"]), np.asarray(i["L3_attn_f2_b"])])[None]
    h_of, e_of = feat // hd, feat % hd
    same = (h_of[:, None] == h_of[None, :]).astype(f)
    o["same"] = same
    o["sel"] = c(np.stack([same * (e_of == k)[None, :].astype(f) for k in range(8)], 1))

    b = {"b_q": bqkv[:D], "b_qs": bqkv[:D][half_perm], "b_k": bqkv[D:2 * D],
         "b_ks": bqkv[D:2 * D][half_perm], "ln_g": i["L1_ffn_ln_g"], "ln_b": i["L1_ffn_ln_b"]}
    parts = [np.asarray(b[n]).reshape(P, 1) for n in ("b_q", "b_qs", "b_k", "b_ks", "ln_g", "ln_b")]
    parts.append(np.asarray(i["L1_ffn_b1"]).reshape(EXPERTS * FT, P).T)
    for n in ("L3_ffn_b1", "L2_ffn_ln_w", "L2_ffn_ln_b", "L3_attn_f1_b"):
        parts.append(np.asarray(i[n]).reshape(FT, P).T)
    parts += [np.asarray(i[f"L3_attn_{n}_b"]).reshape(P, 1) for n in "qk"]
    parts.append(np.repeat(np.asarray(i["L3_attn_dec_b"]), 8).reshape(P, 1))
    parts.append(np.repeat(np.asarray(i["L3_attn_v_b"]).reshape(16, 8), 8, 0))
    parts += [np.asarray(i["L3_attn_ln" + n]).reshape(P, 1) for n in ("1_w", "1_b", "2_w", "2_b")]
    o["cols"] = c(np.concatenate(parts, 1).astype(f))
    o["rows"] = c(np.concatenate([np.asarray(i["L1_ffn_b2"]).reshape(-1), np.asarray(i["L3_ffn_b2"]),
                                  bqkv[2 * D:]])[None])
    return o


UPS_ = 6 * PAIRS


def kernel(**inputs):
    import numpy as _np
    import concourse.bacc as _bacc
    from concourse.bass_utils import run_bass_kernel_spmd as _run

    nc = _bacc.Bacc("TRN2", target_bir_lowering=False, num_devices=1)
    arrays, aps = {}, {}
    for name, v in _layout(inputs).items():
        v = _np.ascontiguousarray(v)
        arrays["in_" + name] = v
        aps[name] = nc.dram_tensor("in_" + name, v.shape, mybir.dt.from_np(v.dtype),
                                   kind="ExternalInput").ap()
    out = nc.dram_tensor("out_x", (TOKENS, D), F32, kind="ExternalOutput").ap()
    macaron(nc, aps, out)
    r = _run(nc, [arrays], core_ids=[0])
    return r.results[0]["out_x"].reshape(BATCH, SEQ, D)
```
